# Optimizing a Trainium2 kernel written in Bass

```python
import numpy as np
import jax
import jax.numpy as jnp

def _softmax(x, axis=-1):
    return jax.nn.softmax(x, axis=axis)

def _gelu(x):
    return jax.nn.gelu(x, approximate=True)

def _silu(x):
    return jax.nn.silu(x)

def _sigmoid(x):
    return jax.nn.sigmoid(x)

def _layernorm(x, axis=-1, eps=1e-05):
    m = jnp.mean(x, axis=axis, keepdims=True)
    v = jnp.var(x, axis=axis, keepdims=True)
    return (x - m) / jnp.sqrt(v + eps)

def _scatter_add(tgt, idx, src, axis=0):
    return tgt.at[idx].add(src)

def _segment_sum(src, seg, n):
    return jax.ops.segment_sum(src, seg, n)
kernel_name = 'mk_pixart_resid_d1_seqx_r4_2f8f26'

def setup_inputs(seed: int=0):
    np.random.seed(seed)
    _w = jnp.asarray

    def _rec_inputs():
        import jax
        import jax.numpy as jnp
        _rk = jax.random.key(seed)
        x = 7.22e-05 + 1 * jax.random.normal(jax.random.fold_in(_rk, 1), (2, 1024, 256), jnp.float32)
        _lenS = 1024 - jax.random.randint(jax.random.fold_in(_rk, 7), (2,), 0, max(1, 1024 // 4) + 1, jnp.int32)
        _lenS2 = 154 - jax.random.randint(jax.random.fold_in(_rk, 8), (2,), 0, max(1, 154 // 4) + 1, jnp.int32)
        _ctx_1024P = jax.random.normal(jax.random.fold_in(_rk, 11), (2, 16, 256), jnp.float32)
        _ctx_1024c = jax.random.dirichlet(jax.random.fold_in(_rk, 511), 0.3 * jnp.ones((16,), jnp.float32), (2, 154))
        _ctx_1024t = jnp.einsum('bsk,bkd->bsd', _ctx_1024c, _ctx_1024P)
        _ctx_1024t = _ctx_1024t * jax.lax.rsqrt(jnp.mean(jnp.square(_ctx_1024t)) + 1e-12) * 0.953939
        ctx_1024 = 4.13588e-05 + 0.999923 * (_ctx_1024t + 0.3 * jax.random.normal(jax.random.fold_in(_rk, 611), (2, 154, 256), jnp.float32))
        condB_tau = jax.random.uniform(jax.random.fold_in(_rk, 12), (2,), jnp.float32, 0.0, 1.45372)
        fside_BxS2_0 = 0.0088954 + 1.00633 * jax.random.normal(jax.random.fold_in(_rk, 13), (2, 154), jnp.float32)
        return (x, ctx_1024, condB_tau, fside_BxS2_0)
    x, ctx_1024, condB_tau, fside_BxS2_0 = _rec_inputs()

    def _L0_xcond_setup():
        import jax, jax.numpy as jnp
        import numpy as np
        D_MODEL = 256
        N_HEADS = 16
        key = jax.random.key(seed)
        ks = jax.random.split(key, 16)
        B, L, S, D = (4, 512, 512, D_MODEL)
        inp = {'q': jax.random.normal(ks[0], (B, L, D), jnp.float32), 'k': jax.random.normal(ks[1], (B, S, D), jnp.float32), 'v': jax.random.normal(ks[2], (B, S, D), jnp.float32), 'tau': jax.random.uniform(ks[3], (B, 1), jnp.float32, 0.5, 1.5), 'delta': jax.random.normal(ks[4], (B, S), jnp.float32)}
        s = 1.0 / np.sqrt(D)
        inp['Wq'] = jax.random.normal(ks[5], (D, D), jnp.float32) * s
        inp['bq'] = jnp.zeros((D,), jnp.float32)
        inp['Wk'] = jax.random.normal(ks[6], (D, D), jnp.float32) * s
        inp['bk'] = jnp.zeros((D,), jnp.float32)
        inp['Wv'] = jax.random.normal(ks[7], (D, D), jnp.float32) * s
        inp['bv'] = jnp.zeros((D,), jnp.float32)
        inp['Wo'] = jax.random.normal(ks[8], (D, D), jnp.float32) * s
        inp['bo'] = jnp.zeros((D,), jnp.float32)
        return inp
    _L0_xcond_all = _L0_xcond_setup()
    _L0_xcond_in = {k: v for k, v in _L0_xcond_all.items() if k in ('Wq', 'bq', 'Wk', 'bk', 'Wv', 'bv', 'Wo', 'bo')}
    del _L0_xcond_all

    def _L0_ffn_setup():
        import jax, jax.numpy as jnp
        import numpy as np
        DIM = 256
        HIDDEN = 1024
        E = 8
        B, S = (2, 1024)
        key = jax.random.key(seed)
        ks = jax.random.split(key, 8)
        sd = 1.0 / np.sqrt(DIM)
        sh = 1.0 / np.sqrt(HIDDEN)
        return {'x': jax.random.normal(ks[0], (B, S, DIM), dtype=jnp.float32), 'router_w': jax.random.uniform(ks[1], (DIM, E), jnp.float32, -sd, sd), 'router_b': jax.random.uniform(ks[2], (E,), jnp.float32, -sd, sd), 'w1': jax.random.uniform(ks[3], (E, DIM, 2 * HIDDEN), jnp.float32, -sd, sd), 'b1': jax.random.uniform(ks[4], (E, 2 * HIDDEN), jnp.float32, -sd, sd), 'w2': jax.random.uniform(ks[5], (E, HIDDEN, DIM), jnp.float32, -sh, sh), 'b2': jax.random.uniform(ks[6], (E, DIM), jnp.float32, -sh, sh)}
    _L0_ffn_all = _L0_ffn_setup()
    _L0_ffn_in = {k: v for k, v in _L0_ffn_all.items() if k in ('router_w', 'router_b', 'w1', 'b1', 'w2', 'b2')}
    del _L0_ffn_all
    return {'x': x, 'ctx_1024': ctx_1024, 'condB_tau': condB_tau, 'fside_BxS2_0': fside_BxS2_0, 'L0_xcond_Wq': _L0_xcond_in['Wq'], 'L0_xcond_bq': _L0_xcond_in['bq'], 'L0_xcond_Wk': _L0_xcond_in['Wk'], 'L0_xcond_bk': _L0_xcond_in['bk'], 'L0_xcond_Wv': _L0_xcond_in['Wv'], 'L0_xcond_bv': _L0_xcond_in['bv'], 'L0_xcond_Wo': _L0_xcond_in['Wo'], 'L0_xcond_bo': _L0_xcond_in['bo'], 'L0_ffn_router_w': _L0_ffn_in['router_w'], 'L0_ffn_router_b': _L0_ffn_in['router_b'], 'L0_ffn_w1': _L0_ffn_in['w1'], 'L0_ffn_b1': _L0_ffn_in['b1'], 'L0_ffn_w2': _L0_ffn_in['w2'], 'L0_ffn_b2': _L0_ffn_in['b2']}

def reference(x, ctx_1024, condB_tau, fside_BxS2_0, L0_xcond_Wq, L0_xcond_bq, L0_xcond_Wk, L0_xcond_bk, L0_xcond_Wv, L0_xcond_bv, L0_xcond_Wo, L0_xcond_bo, L0_ffn_router_w, L0_ffn_router_b, L0_ffn_w1, L0_ffn_b1, L0_ffn_w2, L0_ffn_b2):
    import jax
    import jax.numpy as jnp

    def _L0_xcond_ref(q, k, v, tau, delta, Wq, bq, Wk, bk, Wv, bv, Wo, bo):
        import jax, jax.numpy as jnp
        import numpy as np
        D_MODEL = 256
        N_HEADS = 16
        B, L, D = q.shape
        S = k.shape[1]
        H = N_HEADS
        E = D // H
        qh = (q @ Wq.T + bq).reshape(B, L, H, E)
        kh = (k @ Wk.T + bk).reshape(B, S, H, E)
        vh = (v @ Wv.T + bv).reshape(B, S, H, E)
        scale = 1.0 / np.sqrt(E).astype(np.float32)
        scores = jnp.einsum('blhe,bshe->bhls', qh, kh)
        scores = scores * tau[:, None, None, :] + delta[:, None, None, :]
        a = jax.nn.softmax(scale * scores, axis=-1)
        out = jnp.einsum('bhls,bshd->blhd', a, vh).reshape(B, L, D)
        return out @ Wo.T + bo

    def _L0_ffn_ref(x, router_w, router_b, w1, b1, w2, b2):
        import jax, jax.numpy as jnp
        import numpy as np
        DIM = 256
        HIDDEN = 1024
        E = 8
        B, S = (2, 1024)
        logits = jnp.einsum('bsd,de->bse', x, router_w) + router_b
        probs = jax.nn.softmax(logits, axis=-1)
        top1 = jnp.argmax(probs, axis=-1)
        out = jnp.zeros_like(x)
        for i in range(E):
            h = jnp.einsum('bsd,df->bsf', x, w1[i]) + b1[i]
            a, g = jnp.split(h, 2, axis=-1)
            y = jnp.einsum('bsh,hd->bsd', a * jax.nn.sigmoid(g), w2[i]) + b2[i]
            out = out + jnp.where((top1 == i)[..., None], y, 0.0)
        return out
    x = x + _L0_xcond_ref(_layernorm(x, axis=-1), ctx_1024, ctx_1024, condB_tau[:, None], fside_BxS2_0, L0_xcond_Wq, L0_xcond_bq, L0_xcond_Wk, L0_xcond_bk, L0_xcond_Wv, L0_xcond_bv, L0_xcond_Wo, L0_xcond_bo)
    x = x + _L0_ffn_ref(_layernorm(x, axis=-1), L0_ffn_router_w, L0_ffn_router_b, L0_ffn_w1, L0_ffn_b1, L0_ffn_w2, L0_ffn_b2)
    return x

_drawn_inputs = setup_inputs


def setup_inputs(seed=0):
    import zlib

    import numpy as np

    out = dict(_drawn_inputs(seed))
    spreads = {'L0_xcond_bq': (0.0, 0.392),
     'L0_xcond_bk': (0.0, 0.8),
     'L0_xcond_bv': (0.0, 0.1),
     'L0_xcond_bo': (0.0, 0.1)}
    factors = {'L0_ffn_b1': 5.936, 'L0_ffn_b2': 3.541}
    for name, (base, spread) in spreads.items():
        noise = np.random.default_rng([zlib.crc32(name.encode()), seed]).standard_normal(out[name].shape)
        drawn = base * np.exp(spread * noise) if base else spread * noise
        out[name] = jnp.asarray(drawn.astype(out[name].dtype))
    for name, factor in factors.items():
        out[name] = (out[name] * factor).astype(out[name].dtype)
    return out
```

```python
from contextlib import ExitStack

import numpy as np

import concourse.bass as bass
from concourse import mybir

ALU = mybir.AluOpType
ACT = mybir.ActivationFunctionType
AX_X = mybir.AxisListType.X
F32 = mybir.dt.float32
BF16 = mybir.dt.bfloat16
I32 = mybir.dt.int32
U32 = mybir.dt.uint32

P = 128
BATCH, SEQ, DIM = 2, 1024, 256
HEADS, HDIM = 16, 16
CTX = 154
CTX_PAD = 160
HEAD_ROWS = 128
REST = CTX - HEAD_ROWS
EXPERTS, HIDDEN = 8, 1024
EPS = 1e-5
SCALE = HDIM ** -0.5

TOKENS = BATCH * SEQ
TILES = TOKENS // P
CHUNK = 512
CHUNKS = TOKENS // CHUNK
TPC = CHUNK // P
KD = DIM // P
GROUPS = HEADS // 4
SLOT_TILES = TOKENS // P + EXPERTS - 1
QUARTERS = 4
HQ = HIDDEN // QUARTERS
KH = HQ // P
BANK = 512

Q_PARTS = (0, 0, 1, 1, 0, 2)
K_PARTS = (0, 1, 0, 1, 2, 0)
SPLIT = len(Q_PARTS) * HDIM
STACK = SPLIT + 3
HEADS_PER_BANK = BANK // CTX
SCORE_BANKS = -(-HEADS // HEADS_PER_BANK)
UNITS_PER_GROUP = 5
UNITS = GROUPS * UNITS_PER_GROUP
EXPERT_W = KD * 2 * HQ + KH * DIM
EARLY_EXPERTS = 2
OUT_AT = 3
GATHERS = 3


def constants():
    p = np.arange(P)
    parts = {
        "ident": np.eye(P),
        "upper": (p[:, None] < p[None, :]) * 1.0,
        "slot_in_tile": np.tile(p, (P, 1)),
        "first_expert": np.tile(EXPERTS - np.arange(EXPERTS), (P, 1)),
        "tile_starts": np.tile(np.arange(TILES) * P, (P, 1)),
        "slot_tile": np.tile(np.arange(SLOT_TILES), (P, 1)),
        "tile_of_token": np.tile(np.arange(TILES), (P, 1)),
        "row": p[:, None],
        "one8": np.ones((P, EXPERTS)),
        "spare_row": TOKENS + p[:, None],
        "carry": np.tile((np.arange(EXPERTS * TILES) % TILES > 0) * 1.0, (P, 1)),
        "minus_head": -1.0 * ((p[:, None] % HEADS == np.arange(HEADS)[None, :]) & (p[:, None] < 3 * HEADS)),
        "rest_rows": ((p[:, None] // 32 == np.arange(4)[None, :]) & (p[:, None] % 32 < REST)) * 1.0,
    }
    at, spans = 0, {}
    for name, a in parts.items():
        spans[name] = (at, at + a.shape[1])
        at += a.shape[1]
    return np.concatenate([np.asarray(a, np.float32) for a in parts.values()], axis=1), spans


CONSTANTS, SPANS = constants()


def build(nc, x, ctx_t, tau, delta, wq, bq, wk, bk, wv, bv, wo, bo, rw, rb, weights, b1, b2, const, ones, out,
          q_parts, k_parts, d_parts, rows):
    ctx = ExitStack()
    early = ExitStack()
    with ctx:
        def sb(name, shape, dt=F32, stack=ctx):
            return stack.enter_context(nc.sbuf_tensor(name, shape, dt))

        def bank(name):
            return ctx.enter_context(nc.psum_tensor(name, [P, BANK], F32))

        def sem(name):
            return ctx.enter_context(nc.semaphore(name))

        consts = sb("consts", [P, CONSTANTS.shape[1]])
        slot_row = sb("slot_row", [P, SLOT_TILES], U32)
        tile_expert = sb("tile_expert", [1, SLOT_TILES], I32)

        def const_of(name):
            return consts[:, SPANS[name][0]:SPANS[name][1]]

        ident = const_of("ident")
        ident_b = sb("ident_b", [P, P], BF16)[:, :]

        sb("first_experts", [P, EARLY_EXPERTS * EXPERT_W], stack=early)
        x_sb = sb("x_sb", [P, TILES, DIM], stack=early)
        q_stack = sb("q_stack", [P, 3, HEADS, CHUNK], BF16, early)
        xn = sb("xn", [P, 2, TPC, DIM], stack=early)
        xn_t = sb("xn_t", [P, KD, CHUNK], stack=early)
        q_split = sb("q_split", [P, KD, 3, CHUNK], BF16, early)
        q_rest = sb("q_rest", [P, KD, CHUNK], stack=early)
        k_stack = sb("k_stack", [P, BATCH, HEADS, CTX_PAD], BF16, early)
        v_main = sb("v_main", [P, BATCH, HEADS, 32], stack=early)
        v_rest = sb("v_rest", [P, BATCH, GROUPS, 4, 32], stack=early)
        v_tmp = sb("v_tmp", [P, BATCH, DIM], stack=early)
        minus_max_sel = sb("minus_max_sel", [P, HEADS, HEAD_ROWS], BF16, early)
        minus_max_rest = sb("minus_max_rest", [P, HEADS, 32], BF16, early)
        probs = sb("probs", [P, 4, CHUNK], stack=early)
        attn_t = sb("attn_t", [P, 2, GROUPS, CHUNK], stack=early)
        inverse = sb("inverse", [P, 2, HEADS], stack=early)
        attn = sb("attn", [P, 2, DIM], stack=early)
        attn_nt = sb("attn_nt", [P, 2, KD, P], stack=early)
        bo_sb = sb("bo_sb", [P, DIM], stack=early)
        wq_sb = sb("wq_sb", [P, KD, DIM], stack=early)
        wk_sb = sb("wk_sb", [P, KD, DIM], stack=early)
        wv_sb = sb("wv_sb", [P, KD, DIM], stack=early)
        wo_sb = sb("wo_sb", [P, KD, DIM], stack=early)
        rw_sb = sb("rw_sb", [P, KD, EXPERTS], stack=early)
        rb_sb = sb("rb_sb", [P, EXPERTS], stack=early)
        bq_sb = sb("bq_sb", [P, KD], stack=early)
        bk_sb = sb("bk_sb", [P, KD], stack=early)
        bv_sb = sb("bv_sb", [P, DIM], stack=early)
        tau_sb = sb("tau_sb", [P, BATCH], stack=early)
        ctx_sb = sb("ctx_sb", [P, KD, BATCH, CTX_PAD], stack=early)
        k_full = sb("k_full", [P, KD, BATCH, CTX_PAD], stack=early)
        k_rest = sb("k_rest", [P, KD, BATCH * CTX_PAD], stack=early)
        k_split = sb("k_split", [P, KD, 3, BATCH * CTX_PAD], BF16, early)
        delta_sb = sb("delta_sb", [BATCH, CTX], stack=early)
        delta_rest = sb("delta_rest", [BATCH, CTX], stack=early)
        delta_split = sb("delta_split", [BATCH, 3, CTX], BF16, early)
        stats1 = sb("stats1", [P, TILES, 6], stack=early)
        mv1 = sb("mv1", [P, TILES, 2], stack=early)
        var1 = sb("var1", [P, TILES], stack=early)
        rstd1 = sb("rstd1", [P, TILES], stack=early)
        stats2 = sb("stats2", [P, TILES, 6], stack=early)
        mv2 = sb("mv2", [P, TILES, 2], stack=early)
        var2 = sb("var2", [P, TILES], stack=early)
        rstd2 = sb("rstd2", [P, TILES], stack=early)
        minus_half = sb("minus_half", [P, TPC], stack=early)
        row_max = sb("row_max", [P, 2, TPC, HEADS], stack=early)
        max_rest = sb("max_rest", [P, TPC, HEADS], stack=early)
        max_split = sb("max_split", [P, TPC, 3, HEADS], BF16, early)
        max_t = sb("max_t", [P, 2, CHUNK], BF16, early)
        row_buf = sb("row_buf", [P, 2, 2 * DIM], stack=early)
        x2n_t = sb("x2n_t", [P, 2, KD, P], stack=early)
        logits = sb("logits", [P, TILES, EXPERTS], stack=early)
        upper_b = sb("upper_b", [P, P], BF16, early)
        ones_b = sb("ones_b", [P, P], BF16, early)
        best = sb("best", [P, TILES], stack=early)
        key = sb("key", [P, TILES, EXPERTS], stack=early)
        onehot = sb("onehot", [P, TILES, EXPERTS], stack=early)
        onehot_b = sb("onehot_b", [P, TILES, EXPERTS], BF16, early)
        counts = sb("counts", [P, EXPERTS, TILES], stack=early)
        upto = sb("upto", [P, EXPERTS, TILES], stack=early)
        over = sb("over", [P, EXPERTS, TILES], stack=early)
        n_tiles = sb("n_tiles", [P, EXPERTS], stack=early)
        last_tile = sb("last_tile", [P, EXPERTS], stack=early)
        start_slot = sb("start_slot", [P, EXPERTS], stack=early)
        place = sb("place", [P, TILES, EXPERTS], stack=early)
        slot = sb("slot", [P, TILES], stack=early)
        slot_tile_of = sb("slot_tile_of", [P, TILES], stack=early)
        slot_lane = sb("slot_lane", [P, TILES], stack=early)
        passed = sb("passed", [P, TILES, SLOT_TILES], stack=early)
        lane_hot = sb("lane_hot", [P, TILES, P], BF16, early)
        tile_hot = sb("tile_hot", [P, TILES, 3, SLOT_TILES], BF16, early)
        slot_info = sb("slot_info", [P, 3, SLOT_TILES], stack=early)
        row_f = sb("row_f", [P, 2, SLOT_TILES], stack=early)
        ended = sb("ended", [P, SLOT_TILES, EXPERTS], stack=early)
        expert_f = sb("expert_f", [P, SLOT_TILES], stack=early)
        early.close()

        w_sb = sb("w_sb", [P, 2 * EXPERTS, EXPERT_W])
        b1_sb = sb("b1_sb", [P, 2 * EXPERTS, 2 * HQ])
        b2_sb = sb("b2_sb", [P, EXPERTS, DIM])
        y_acc = sb("y_acc", [P, SLOT_TILES, DIM])
        slot_xt = sb("slot_xt", [P, SLOT_TILES, KD, P])
        slot_in = sb("slot_in", [P, GATHERS, 2 * DIM])
        hidden = sb("hidden", [P, 2, 2 * HQ])
        gate = sb("gate", [P, 2, HQ])
        act_u = sb("act_u", [P, 2, HQ])
        act_ut = sb("act_ut", [P, 2, KH, P])

        banks = [bank(f"bank{n}") for n in range(8)]
        score_ps, st_ps, o_ps, work_ps = banks[0:2], banks[2:4], banks[4:6], banks[6:8]
        h_ps, ut_ps, y_ps, xin_ps = banks[0:2], banks[2:4], banks[4:6], banks[6:8]

        s_consts = sem("s_consts")
        s_x = [sem(f"s_x{c}") for c in range(CHUNKS)]
        s_q_weights = sem("s_q_weights")
        s_kv_inputs = sem("s_kv_inputs")
        s_out_weights = sem("s_out_weights")
        s_delta = sem("s_delta")
        s_quarter = [sem(f"s_quarter{q}") for q in range(QUARTERS)]
        quarter_ready = sem("quarter_ready")
        k_stored = sem("k_stored")
        d_stored = sem("d_stored")
        ones_loaded = sem("ones_loaded")
        k_loaded = sem("k_loaded")
        q_stored = sem("q_stored")
        q_loaded = [sem(f"q_loaded{c}") for c in range(CHUNKS)]
        rows_stored = [sem("rows_stored0"), sem("rows_stored1")]
        zeros_stored = sem("zeros_stored")
        gathered = [sem(f"gathered{n}") for n in range(GATHERS)]
        s_out = sem("s_out")
        pool_ready = sem("pool_ready")
        sel_ready = sem("sel_ready")
        dve_step = sem("dve_step")
        pool_step = sem("pool_step")
        k_ready = sem("k_ready")
        k_split_done = sem("k_split_done")
        d_split_done = sem("d_split_done")
        v_ready = sem("v_ready")
        v_done = sem("v_done")
        ln1_stats = sem("ln1_stats")
        ln1_done = sem("ln1_done")
        xt_ready = sem("xt_ready")
        xt_copied = sem("xt_copied")
        q_ready = sem("q_ready")
        rstd1_done = sem("rstd1_done")
        rstd2_done = sem("rstd2_done")
        x_biased = sem("x_biased")
        o_copied = sem("o_copied")
        on_ready = sem("on_ready")
        o_turned = sem("o_turned")
        on_turned = sem("on_turned")
        on_copied = sem("on_copied")
        q_high = sem("q_high")
        q_rest_done = sem("q_rest_done")
        q_low = sem("q_low")
        score_ready = sem("score_ready")
        max_done = sem("max_done")
        max_parts = sem("max_parts")
        mt_ready = sem("mt_ready")
        mt_copied = sem("mt_copied")
        st_ready = sem("st_ready")
        probs_ready = sem("probs_ready")
        pv_done = sem("pv_done")
        proj_ready = sem("proj_ready")
        x2_done = sem("x2_done")
        ln2_stats = sem("ln2_stats")
        ln2_done = sem("ln2_done")
        x2t_ready = sem("x2t_ready")
        x2t_copied = sem("x2t_copied")
        logits_ready = sem("logits_ready")
        logits_done = sem("logits_done")
        onehot_done = sem("onehot_done")
        count_ready = sem("count_ready")
        hots_done = sem("hots_done")
        info_ready = sem("info_ready")
        routed = sem("routed")
        xin_ready = sem("xin_ready")
        xin_copied = sem("xin_copied")
        y_started = sem("y_started")
        h_ready = sem("h_ready")
        biased = sem("biased")
        gate_ready = sem("gate_ready")
        u_ready = sem("u_ready")
        ut_ready = sem("ut_ready")
        ut_copied = sem("ut_copied")
        y_ready = sem("y_ready")
        y_added = sem("y_added")

        block = ctx.enter_context(nc.Block())
        STEPS = SCORE_BANKS * TPC

        @block.sync
        def _(sp):
            sp.dma_start(x_sb[:, 0:TPC, :], x[0:CHUNK, :].rearrange("(t p) d -> p t d", p=P)).then_inc(s_x[0], 16)
            sp.dma_start(consts[:, :], const).then_inc(s_consts, 16)
            for dst, src in ((ctx_sb[:, :, :, :].rearrange("p k b s -> p (k b) s"), ctx_t),
                             (wk_sb[:, :, :], wk.rearrange("(k p) n -> p k n", p=P)),
                             (bk_sb[:, :], bk),
                             (tau_sb[:, :], tau.rearrange("(o b) -> o b", o=1).to_broadcast([P, BATCH])),
                             (wv_sb[:, :, :], wv.rearrange("(k p) n -> p k n", p=P)),
                             (bv_sb[:, :], bv.rearrange("(o n) -> o n", o=1).to_broadcast([P, DIM]))):
                sp.dma_start(dst, src).then_inc(s_kv_inputs, 16)
            sp.dma_start(delta_sb[:, :], delta).then_inc(s_delta, 16)
            sp.dma_start(wq_sb[:, :, :], wq.rearrange("(k p) n -> p k n", p=P)).then_inc(s_q_weights, 16)
            sp.dma_start(bq_sb[:, :], bq).then_inc(s_q_weights, 16)
            for c in range(1, CHUNKS):
                sp.dma_start(x_sb[:, TPC * c:TPC * (c + 1), :],
                             x[CHUNK * c:CHUNK * (c + 1), :].rearrange("(t p) d -> p t d", p=P)).then_inc(s_x[c], 16)
            sp.dma_start(wo_sb[:, :, :], wo.rearrange("(k p) n -> p k n", p=P)).then_inc(s_out_weights, 16)
            sp.dma_start(bo_sb[:, :], bo.rearrange("(o n) -> o n", o=1).to_broadcast([P, DIM])).then_inc(s_out_weights, 16)
            sp.dma_start(rw_sb[:, :, :], rw.rearrange("(k p) n -> p k n", p=P)).then_inc(s_out_weights, 16)
            sp.dma_start(rb_sb[:, :], rb.rearrange("(o n) -> o n", o=1).to_broadcast([P, EXPERTS])).then_inc(s_out_weights, 16)
            for n in range(3):
                sp.dma_start(q_stack[SPLIT:STACK, n, :, :].rearrange("p h s -> p (h s)"), ones).then_inc(ones_loaded, 16)
            sp.wait_ge(pool_ready, 1)
            sp.dma_start(rows[TOKENS:TOKENS + P, :], row_buf[:, 0, :]).then_inc(zeros_stored, 16)
            sp.wait_ge(d_split_done, 1)
            sp.dma_start(d_parts.rearrange("b w s -> b (w s)"),
                         delta_split[:, :, :].rearrange("b w s -> b (w s)")).then_inc(d_stored, 16)
            sp.wait_ge(k_split_done, 1)
            sp.dma_start(k_parts.rearrange("(m p) w s -> p m (w s)", p=P),
                         k_split[:, :, :, :].rearrange("p m w s -> p m (w s)")).then_inc(k_stored, 16)
            sp.wait_ge(d_stored, 16)
            sp.wait_ge(pool_ready, 3)
            for b in range(BATCH):
                src = d_parts[b].rearrange("w (o s) -> w o s", o=1).to_broadcast([3, HEADS, CTX])
                sp.dma_start(k_stack[SPLIT:STACK, b, :, 0:CTX], src).then_inc(k_loaded, 16)
            sp.wait_ge(k_stored, 16)
            for b in range(BATCH):
                for n, part in enumerate(K_PARTS):
                    src = k_parts[:, part, CTX_PAD * b:CTX_PAD * b + CTX].rearrange("(h d) s -> d h s", d=HDIM)
                    sp.dma_start(k_stack[HDIM * n:HDIM * (n + 1), b, :, 0:CTX], src).then_inc(k_loaded, 16)

            def regroup_q(c):
                sp.wait_ge(q_low, c + 1)
                sp.dma_start(q_parts[c].rearrange("(m p) w s -> p m (w s)", p=P),
                             q_split[:, :, :, :].rearrange("p m w s -> p m (w s)")).then_inc(q_stored, 16)
                sp.wait_ge(q_stored, 16 * (c + 1))
                if c >= 3:
                    sp.wait_ge(st_ready, UNITS * (c - 2))
                for n, part in enumerate(Q_PARTS):
                    src = q_parts[c][:, part, :].rearrange("(h d) s -> d h s", d=HDIM)
                    sp.dma_start(q_stack[HDIM * n:HDIM * (n + 1), c % 3, :, :], src).then_inc(q_loaded[c], 16)

            def store_rows(t):
                sp.wait_ge(ln2_done, t + 1)
                sp.dma_start(rows[P * t:P * (t + 1), :], row_buf[:, t % 2, :]).then_inc(rows_stored[t % 2], 16)

            def load_experts(q, first, last):
                for e in range(first, last):
                    sp.dma_start(w_sb[:, (q % 2) * EXPERTS + e, :], weights[q, :, e, :]).then_inc(s_quarter[q], 16)

            regroup_q(0)
            for c in range(-1, CHUNKS + 1):
                if c + 2 < CHUNKS:
                    regroup_q(c + 2)
                if c == -1:
                    load_experts(0, 0, EARLY_EXPERTS)
                if c >= 1:
                    for t in range(TPC):
                        store_rows(TPC * (c - 1) + t)
            sp.wait_ge(logits_done, TILES)
            for n in range(2):
                sp.wait_ge(rows_stored[n], 16 * TILES // 2)
            load_experts(0, EARLY_EXPERTS, EXPERTS)

            def load_b1(q):
                src = b1[q].rearrange("(o n) -> o n", o=1).to_broadcast([P, EXPERTS * 2 * HQ])
                at = (q % 2) * EXPERTS
                sp.dma_start(b1_sb[:, at:at + EXPERTS, :].rearrange("p e n -> p (e n)"), src).then_inc(s_quarter[q], 16)

            load_b1(0)
            sp.dma_start(b2_sb[:, :, :].rearrange("p e n -> p (e n)"),
                         b2.rearrange("(o n) -> o n", o=1).to_broadcast([P, EXPERTS * DIM])).then_inc(s_quarter[0], 16)
            load_b1(1)
            load_experts(1, 0, EXPERTS)
            for q in range(QUARTERS):
                if q >= 2:
                    sp.wait_ge(y_ready, SLOT_TILES * (q - 1))
                    load_b1(q)
                    load_experts(q, 0, EXPERTS)
                sp.wait_ge(s_quarter[q], 16 * (EXPERTS + 1 + (q == 0)))
                sp.sem_inc(quarter_ready, 1)

        @block.gpsimd
        def _(pool):
            pool.memset(row_buf[:, 0, :], 0.0).then_inc(pool_ready, 1)
            pool.memset(minus_half[:, :], -0.5).then_inc(pool_ready, 1)
            pool.memset(k_stack[:, :, :, CTX:CTX_PAD], 0.0).then_inc(pool_ready, 1)
            pool.memset(v_main[:, :, :, :], 0.0).then_inc(pool_ready, 1)
            pool.memset(v_rest[:, :, :, :, :], 0.0).then_inc(pool_ready, 1)
            pool.memset(max_t[:, :, :], 0.0).then_inc(pool_ready, 1)

            def power(var, rstd, mv, t0, n, signal):
                pool.tensor_scalar(var[:, t0:t0 + n], mv[:, t0:t0 + n, 1], EPS, None, ALU.add).then_inc(pool_step, 1)
                count[0] += 1
                pool.wait_ge(pool_step, count[0])
                pool.tensor_tensor(rstd[:, t0:t0 + n], var[:, t0:t0 + n], minus_half[:, 0:n],
                                   ALU.pow).then_inc(signal, 1)

            count = [0]

            def power1(c):
                pool.wait_ge(ln1_stats, c + 1)
                if c == 0:
                    pool.wait_ge(pool_ready, 2)
                power(var1, rstd1, mv1, TPC * c, TPC, rstd1_done)

            def add_bo(c):
                pool.wait_ge(ln1_done, c + 1)
                if c == 0:
                    pool.wait_ge(s_out_weights, 64)
                at = x_sb[:, TPC * c:TPC * (c + 1), :]
                pool.tensor_tensor(at, at, bo_sb[:, :].rearrange("p (o n) -> p o n", o=1).to_broadcast([P, TPC, DIM]),
                                   ALU.add).then_inc(x_biased, 1)

            def power2(t):
                pool.wait_ge(ln2_stats, t + 1)
                power(var2, rstd2, mv2, t, 1, rstd2_done)

            power1(0)
            power1(1)
            for c in range(-1, CHUNKS + 1):
                for i in range(STEPS):
                    if c >= 1 and i >= OUT_AT + 2 and (i - OUT_AT - 2) % 5 == 0 and (i - OUT_AT - 2) // 5 < TPC:
                        power2(TPC * (c - 1) + (i - OUT_AT - 2) // 5)
                    if c + 3 < CHUNKS and i == 8:
                        power1(c + 3)
                    if 0 <= c + 1 < CHUNKS and i == 12:
                        add_bo(c + 1)

            pool.wait_ge(routed, 2)
            pool.wait_ge(zeros_stored, 16)
            for n in range(2):
                pool.wait_ge(rows_stored[n], 16 * TILES // 2)

            def gather(j):
                if j >= GATHERS:
                    pool.wait_ge(xin_ready, j - GATHERS + 1)
                    pool.wait_ge(y_started, j - GATHERS + 1)
                pool.indirect_dma_start(slot_in[:, j % GATHERS, :], None, rows,
                                        bass.IndirectOffsetOnAxis(slot_row[:, j:j + 1], 0)).then_inc(gathered[j % GATHERS], 16)

            for j in range(GATHERS):
                gather(j)
            pool.wait_ge(quarter_ready, 1)
            for j in range(SLOT_TILES):
                expert = pool.value_load(tile_expert[0:1, j:j + 1], min_val=0, max_val=EXPERTS - 1)
                pool.wait_ge(gathered[j % GATHERS], 16 * (j // GATHERS + 1))
                pool.tensor_tensor(y_acc[:, j, :], slot_in[:, j % GATHERS, DIM:2 * DIM],
                                   b2_sb[:, bass.ds(expert, 1), :].rearrange("p o n -> p (o n)"),
                                   ALU.add).then_inc(y_started, 1)
                if j + GATHERS < SLOT_TILES:
                    gather(j + GATHERS)
            for j in range(SLOT_TILES):
                pool.wait_ge(y_added, SLOT_TILES * (QUARTERS - 1) + j + 1)
                if j >= 1:
                    pool.wait_ge(s_out, 16 * j)
                pool.indirect_dma_start(out, bass.IndirectOffsetOnAxis(slot_row[:, j:j + 1], 0), y_acc[:, j, :],
                                        None).then_inc(s_out, 16)
            pool.wait_ge(s_out, 16 * SLOT_TILES)

        @block.tensor
        def _(pe):
            pe.wait_ge(s_consts, 16)
            pe.wait_ge(s_kv_inputs, 96)
            for m in range(KD):
                for k in range(KD):
                    ins = pe.matmul(score_ps[m][:, 0:BATCH * CTX_PAD], wk_sb[:, k, P * m:P * (m + 1)],
                                    ctx_sb[:, k, :, :].rearrange("p b s -> p (b s)"), start=(k == 0), stop=(k == KD - 1))
                ins.then_inc(k_ready, 1)
            for b in range(BATCH):
                for k in range(KD):
                    ins = pe.matmul(st_ps[b][:, 0:DIM], ctx_sb[:, k, b, 0:HEAD_ROWS], wv_sb[:, k, :],
                                    start=(k == 0), stop=(k == KD - 1))
                ins.then_inc(v_ready, 1)
                for j in range(4):
                    for k in range(KD):
                        ins = pe.matmul(o_ps[b][32 * j:32 * j + 32, 0:DIM], ctx_sb[:, k, b, HEAD_ROWS:CTX_PAD],
                                        wv_sb[:, k, :], start=(k == 0), stop=(k == KD - 1))
                ins.then_inc(v_ready, 1)

            def turn_x(c):
                pe.wait_ge(ln1_done, c + 1)
                if c >= 1:
                    pe.wait_ge(q_rest_done, KD * c)
                if c >= 2:
                    pe.wait_ge(mt_copied, c - 1)
                for k in range(KD):
                    for t in range(TPC):
                        ins = pe.transpose(work_ps[k][:, P * t:P * (t + 1)], xn[:, c % 2, t, P * k:P * (k + 1)], ident)
                    ins.then_inc(xt_ready, 1)

            def project_q(c):
                pe.wait_ge(xt_copied, KD * (c + 1))
                if c == 0:
                    pe.wait_ge(s_q_weights, 32)
                for m in range(KD):
                    for k in range(KD):
                        ins = pe.matmul(work_ps[m][:, :], wq_sb[:, k, P * m:P * (m + 1)], xn_t[:, k, :],
                                        start=(k == 0), stop=(k == KD - 1))
                    ins.then_inc(q_ready, 1)

            def scores(c, i):
                n = STEPS * c + i
                if n == 0:
                    pe.wait_ge(pool_ready, 6)
                    pe.wait_ge(ones_loaded, 48)
                    pe.wait_ge(k_loaded, 16 * BATCH * (len(K_PARTS) + 1))
                    pe.wait_ge(k_split_done, 1)
                if i == 0:
                    pe.wait_ge(q_loaded[c], 16 * len(Q_PARTS))
                if n >= 2:
                    pe.wait_ge(max_done, n - 1)
                t, first = i // SCORE_BANKS, HEADS_PER_BANK * (i % SCORE_BANKS)
                for h in range(first, min(first + HEADS_PER_BANK, HEADS)):
                    at = CTX * (h - first)
                    ins = pe.matmul(score_ps[n % 2][:, at:at + CTX], q_stack[0:STACK, c % 3, h, P * t:P * (t + 1)],
                                    k_stack[0:STACK, c // 2, h, 0:CTX], start=True, stop=True)
                ins.then_inc(score_ready, 1)

            def turn_max(c):
                pe.wait_ge(max_parts, c + 1)
                if c >= 2:
                    pe.wait_ge(x2t_copied, TPC * (c - 1))
                pe.wait_ge(q_rest_done, KD * min(c + 2, CHUNKS))
                turned = work_ps[1][0:3 * HEADS, 0:CHUNK // 2].bitcast(BF16)
                for t in range(TPC):
                    ins = pe.transpose(turned[:, P * t:P * (t + 1)],
                                       max_split[:, t, :, :].rearrange("p w h -> p (w h)"), ident_b)
                ins.then_inc(mt_ready, 1)

            def scores_t(c, u):
                n = UNITS * c + u
                if n == 0:
                    pe.wait_ge(sel_ready, 2)
                    pe.wait_ge(v_done, 3 * BATCH + 2)
                if u == 0:
                    pe.wait_ge(mt_copied, c + 1)
                if n >= 2:
                    pe.wait_ge(probs_ready, n - 1)
                g, j = u // UNITS_PER_GROUP, u % UNITS_PER_GROUP - 1
                if j < 0:
                    for j in range(4):
                        h = 4 * g + j
                        o = st_ps[n % 2][32 * j:32 * j + 32, :]
                        pe.matmul(o, k_stack[0:STACK, c // 2, h, HEAD_ROWS:CTX_PAD], q_stack[0:STACK, c % 3, h, :],
                                  start=True, stop=False)
                        ins = pe.matmul(o, minus_max_rest[:, h, :], max_t[:, c % 2, :], start=False, stop=True)
                else:
                    h = 4 * g + j
                    pe.matmul(st_ps[n % 2][:, :], k_stack[0:STACK, c // 2, h, 0:HEAD_ROWS],
                              q_stack[0:STACK, c % 3, h, :], start=True, stop=False)
                    ins = pe.matmul(st_ps[n % 2][:, :], minus_max_sel[:, h, :], max_t[:, c % 2, :], start=False, stop=True)
                ins.then_inc(st_ready, 1)

            def values(c, u):
                n = UNITS * c + u
                group = GROUPS * c + u // UNITS_PER_GROUP
                g, j = u // UNITS_PER_GROUP, u % UNITS_PER_GROUP - 1
                pe.wait_ge(probs_ready, n + 1)
                o = o_ps[group % 2]
                if j < 0:
                    if group >= 2:
                        pe.wait_ge(o_copied, group - 1)
                    ins = pe.matmul(o[:, :], v_rest[:, c // 2, g, :, :].rearrange("p j n -> p (j n)"),
                                    probs[:, n % 4, :], start=True, stop=False, skip_group_check=True)
                else:
                    ins = pe.matmul(o[32 * j:32 * j + 32, :], v_main[:, c // 2, 4 * g + j, :], probs[:, n % 4, :],
                                    start=False, stop=True, skip_group_check=True)
                ins.then_inc(pv_done, 1)

            def turn_o(t):
                c = t // TPC
                pe.wait_ge(o_copied, GROUPS * (c + 1))
                if t >= 1:
                    pe.wait_ge(logits_done, t)
                pe.wait_ge(q_rest_done, KD * min(c + 4, CHUNKS))
                for g in range(GROUPS):
                    ins = pe.transpose(work_ps[0][:, P * g:P * (g + 1)],
                                       attn_t[:, c % 2, g, P * (t % TPC):P * (t % TPC + 1)], ident)
                ins.then_inc(o_turned, 1)

            def turn_on(t):
                pe.wait_ge(on_ready, t + 1)
                if t >= 1:
                    pe.wait_ge(x2t_copied, t)
                pe.wait_ge(mt_copied, min(t // TPC + 2, CHUNKS))
                for k in range(KD):
                    ins = pe.transpose(work_ps[1][:, P * k:P * (k + 1)], attn[:, t % 2, P * k:P * (k + 1)], ident)
                ins.then_inc(on_turned, 1)

            def project_out(t):
                pe.wait_ge(on_copied, t + 1)
                if t == 0:
                    pe.wait_ge(s_out_weights, 64)
                for k in range(KD):
                    ins = pe.matmul(work_ps[0][:, 0:DIM], attn_nt[:, t % 2, k, :], wo_sb[:, k, :],
                                    start=(k == 0), stop=(k == KD - 1))
                ins.then_inc(proj_ready, 1)

            def turn_x2(t):
                pe.wait_ge(ln2_done, t + 1)
                for k in range(KD):
                    ins = pe.transpose(work_ps[1][:, P * k:P * (k + 1)], row_buf[:, t % 2, P * k:P * (k + 1)], ident)
                ins.then_inc(x2t_ready, 1)

            def route(t):
                pe.wait_ge(x2t_copied, t + 1)
                pe.wait_ge(x2_done, t + 1)
                for k in range(KD):
                    ins = pe.matmul(work_ps[0][:, 0:EXPERTS], x2n_t[:, t % 2, k, :], rw_sb[:, k, :],
                                    start=(k == 0), stop=(k == KD - 1))
                ins.then_inc(logits_ready, 1)

            turn_x(0)
            project_q(0)
            for c in range(-1, CHUNKS + 1):
                for i in range(STEPS):
                    if i == 0 and 0 <= c < CHUNKS:
                        turn_max(c)
                    if i == 0 and c + 2 < CHUNKS:
                        turn_x(c + 2)
                    if i == 1 and c + 2 < CHUNKS:
                        project_q(c + 2)
                    if c + 1 < CHUNKS:
                        scores(c + 1, i)
                    if 0 <= c < CHUNKS:
                        if 1 <= i <= UNITS:
                            scores_t(c, i - 1)
                        if 3 <= i <= UNITS + 2:
                            values(c, i - 3)
                    if c >= 1:
                        for at, step in enumerate((turn_o, turn_on, project_out, turn_x2, route), OUT_AT):
                            if i >= at and (i - at) % 5 == 0 and (i - at) // 5 < TPC:
                                step(TPC * (c - 1) + (i - at) // 5)

            pe.wait_ge(onehot_done, 1)
            hot = onehot_b[:, :, :].rearrange("p t e -> p (t e)")
            pe.matmul(score_ps[0][:, 0:TILES * EXPERTS], upper_b[:, :], hot, start=True, stop=True).then_inc(count_ready, 1)
            pe.matmul(score_ps[1][:, 0:TILES * EXPERTS], ones_b[:, :], hot, start=True, stop=True).then_inc(count_ready, 1)
            pe.wait_ge(hots_done, 1)
            for t in range(TILES):
                ins = pe.matmul(st_ps[0][:, 0:3 * SLOT_TILES], lane_hot[:, t, :],
                                tile_hot[:, t, :, :].rearrange("p w j -> p (w j)"), start=(t == 0), stop=(t == TILES - 1))
            ins.then_inc(info_ready, 1)

            experts = [None] * SLOT_TILES

            def load_expert(j):
                experts[j] = pe.value_load(tile_expert[0:1, j:j + 1], min_val=0, max_val=EXPERTS - 1)

            def turn_in(j):
                pe.wait_ge(gathered[j % GATHERS], 16 * (j // GATHERS + 1))
                if j >= 2:
                    pe.wait_ge(xin_copied, j - 1)
                for k in range(KD):
                    ins = pe.transpose(xin_ps[j % 2][:, P * k:P * (k + 1)], slot_in[:, j % GATHERS, P * k:P * (k + 1)], ident)
                ins.then_inc(xin_ready, 1)

            def wait_bank(used, n, j, known):
                if known is None or known + j > 1 or (j == 0 and known > 0):
                    pe.wait_ge(used, n if j == 0 else n - 1)

            def up(n, j, buffer, known=None):
                wait_bank(biased, n, j, known)
                for k in range(KD):
                    at = k * 2 * HQ
                    ins = pe.matmul(h_ps[j % 2][:, :], slot_xt[:, j, k, :],
                                    w_sb[:, bass.ds(buffer + experts[j], 1), at:at + 2 * HQ].rearrange("p o n -> p (o n)"),
                                    start=(k == 0), stop=(k == KD - 1))
                ins.then_inc(h_ready, 1)

            def turn_u(n, j, known=None):
                wait_bank(ut_copied, n, j, known)
                pe.wait_ge(u_ready, n + 1)
                for k in range(KH):
                    ins = pe.transpose(ut_ps[j % 2][:, P * k:P * (k + 1)], act_u[:, j % 2, P * k:P * (k + 1)], ident)
                ins.then_inc(ut_ready, 1)

            def down(n, j, buffer, known=None):
                wait_bank(y_added, n, j, known)
                pe.wait_ge(ut_copied, n + 1)
                for k in range(KH):
                    at = KD * 2 * HQ + k * DIM
                    ins = pe.matmul(y_ps[j % 2][:, 0:DIM], act_ut[:, j % 2, k, :],
                                    w_sb[:, bass.ds(buffer + experts[j], 1), at:at + DIM].rearrange("p o n -> p (o n)"),
                                    start=(k == 0), stop=(k == KH - 1))
                ins.then_inc(y_ready, 1)

            pe.wait_ge(routed, 2)
            load_expert(0)
            turn_in(0)
            turn_in(1)
            for j in range(SLOT_TILES):
                if j == 0:
                    pe.wait_ge(quarter_ready, 1)
                pe.wait_ge(xin_copied, j + 1)
                up(j, j, 0, j)
                if j + 1 < SLOT_TILES:
                    load_expert(j + 1)
                if j + 2 < SLOT_TILES:
                    turn_in(j + 2)
                if j >= 1:
                    turn_u(j - 1, j - 1, j - 1)
                if j >= 2:
                    down(j - 2, j - 2, 0, j - 2)
            with pe.Fori(1, QUARTERS, 1) as q:
                buffer = pe.snap((q % 2) * EXPERTS)
                other = pe.snap(((q + 1) % 2) * EXPERTS)
                pe.wait_ge(quarter_ready, q + 1)
                for j in range(SLOT_TILES):
                    n = SLOT_TILES * q + j
                    up(n, j, buffer)
                    turn_u(n - 1, (j - 1) % SLOT_TILES)
                    down(n - 2, (j - 2) % SLOT_TILES, buffer if j >= 2 else other)
            n = SLOT_TILES * QUARTERS
            turn_u(n - 1, SLOT_TILES - 1, n)
            for back in (2, 1):
                down(n - back, SLOT_TILES - back, ((QUARTERS - 1) % 2) * EXPERTS, n)

        @block.scalar
        def _(act):
            def copy_xt(c):
                for k in range(KD):
                    act.wait_ge(xt_ready, KD * c + k + 1)
                    if c >= 1 and k == 0:
                        act.wait_ge(q_ready, KD * c)
                    act.activation(xn_t[:, k, :], work_ps[k][:, :], ACT.Copy).then_inc(xt_copied, 1)

            def q_highs(c):
                if c == 0:
                    act.wait_ge(s_q_weights, 32)
                for m in range(KD):
                    act.wait_ge(q_ready, KD * c + m + 1)
                    if c >= 1 and m == 0:
                        act.wait_ge(q_stored, 16 * c)
                    act.activation(q_split[:, m, 0, :], work_ps[m][:, :], ACT.Identity,
                                   bias=bq_sb[:, m:m + 1]).then_inc(q_high, 1)

            def copy_max(c):
                act.wait_ge(mt_ready, c + 1)
                if c == 0:
                    act.wait_ge(pool_ready, 6)
                if c >= 2:
                    act.wait_ge(st_ready, UNITS * (c - 1))
                act.activation(max_t[0:3 * HEADS, c % 2, :], work_ps[1][0:3 * HEADS, 0:CHUNK // 2].bitcast(BF16),
                               ACT.Copy).then_inc(mt_copied, 1)

            def exps(c, u):
                n = UNITS * c + u
                act.wait_ge(st_ready, n + 1)
                if n >= 4:
                    act.wait_ge(pv_done, n - 3)
                act.activation(probs[:, n % 4, :], st_ps[n % 2][:, :], ACT.Exp, scale=SCALE).then_inc(probs_ready, 1)

            def copy_o(c, g):
                group = GROUPS * c + g
                act.wait_ge(pv_done, UNITS_PER_GROUP * (group + 1))
                if c >= 2:
                    act.wait_ge(o_turned, TPC * (c - 1))
                act.activation(attn_t[:, c % 2, g, :], o_ps[group % 2][:, :], ACT.Copy).then_inc(o_copied, 1)

            def copy_on(t):
                act.wait_ge(on_turned, t + 1)
                if t >= 2:
                    act.wait_ge(proj_ready, t - 1)
                act.activation(attn_nt[:, t % 2, :, :].rearrange("p k n -> p (k n)"), work_ps[1][:, 0:DIM],
                               ACT.Copy).then_inc(on_copied, 1)

            def copy_x2(t):
                act.wait_ge(x2t_ready, t + 1)
                if t >= 2:
                    act.wait_ge(logits_ready, t - 1)
                act.activation(x2n_t[:, t % 2, :, :].rearrange("p k n -> p (k n)"), work_ps[1][:, 0:DIM],
                               ACT.Copy).then_inc(x2t_copied, 1)

            copy_xt(0)
            q_highs(0)
            for c in range(-1, CHUNKS + 1):
                for i in range(STEPS):
                    if i == 0 and 0 <= c < CHUNKS:
                        copy_max(c)
                    if i == 0 and c + 2 < CHUNKS:
                        copy_xt(c + 2)
                    if i == 1 and c + 2 < CHUNKS:
                        q_highs(c + 2)
                    if 0 <= c < CHUNKS and 1 <= i <= UNITS:
                        exps(c, i - 1)
                    if 0 <= c < CHUNKS and i >= 7 and (i - 7) % 5 == 0 and (i - 7) // 5 < GROUPS:
                        copy_o(c, (i - 7) // 5)
                    if c >= 1:
                        for at, copy in ((OUT_AT + 1, copy_on), (OUT_AT + 3, copy_x2)):
                            if i >= at and (i - at) % 5 == 0 and (i - at) // 5 < TPC:
                                copy(TPC * (c - 1) + (i - at) // 5)

            def copy_in(j):
                act.wait_ge(xin_ready, j + 1)
                act.activation(slot_xt[:, j, :, :].rearrange("p k n -> p (k n)"), xin_ps[j % 2][:, 0:DIM],
                               ACT.Copy).then_inc(xin_copied, 1)

            def wait_slot(used, n, j, known):
                if known is None or known + j > 1 or (j == 0 and known > 0):
                    act.wait_ge(used, n if j == 0 else n - 1)

            def gates(n, j, known=None):
                wait_slot(u_ready, n, j, known)
                act.wait_ge(biased, n + 1)
                act.activation(gate[:, j % 2, :], hidden[:, j % 2, HQ:2 * HQ], ACT.Sigmoid).then_inc(gate_ready, 1)

            def copy_u(n, j, known=None):
                wait_slot(y_ready, n, j, known)
                act.wait_ge(ut_ready, n + 1)
                act.activation(act_ut[:, j % 2, :, :].rearrange("p k n -> p (k n)"), ut_ps[j % 2][:, 0:HQ],
                               ACT.Copy).then_inc(ut_copied, 1)

            act.wait_ge(routed, 2)
            copy_in(0)
            copy_in(1)
            for j in range(SLOT_TILES):
                if j + 2 < SLOT_TILES:
                    copy_in(j + 2)
                gates(j, j, j)
                if j >= 1:
                    copy_u(j - 1, j - 1, j - 1)
            with act.Fori(1, QUARTERS, 1) as q:
                for j in range(SLOT_TILES):
                    n = SLOT_TILES * q + j
                    gates(n, j)
                    copy_u(n - 1, (j - 1) % SLOT_TILES)
            n = SLOT_TILES * QUARTERS
            copy_u(n - 1, SLOT_TILES - 1, n)

        @block.vector
        def _(dve):
            count = [0]

            def step(ins):
                ins.then_inc(dve_step, 1)
                count[0] += 1

            def settle():
                dve.wait_ge(dve_step, count[0])

            def split3(full, rest, high, mid, low, signal):
                settle()
                step(dve.tensor_copy(high, full))
                settle()
                step(dve.tensor_tensor(rest, full, high, ALU.subtract))
                settle()
                step(dve.tensor_copy(mid, rest))
                settle()
                dve.tensor_tensor(low, rest, mid, ALU.subtract).then_inc(signal, 1)

            def stats1_of(c):
                dve.wait_ge(s_x[c], 16)
                for t in range(TPC * c, TPC * (c + 1)):
                    step(dve.bn_stats(stats1[:, t, :], x_sb[:, t, :]))
                settle()
                for t in range(TPC * c, TPC * (c + 1)):
                    ins = dve.bn_aggr(mv1[:, t, :], stats1[:, t, :])
                ins.then_inc(ln1_stats, 1)

            def norm1(c):
                dve.wait_ge(rstd1_done, c + 1)
                if c >= 2:
                    dve.wait_ge(xt_ready, KD * (c - 1))
                for t in range(TPC):
                    n = TPC * c + t
                    ins = dve.tensor_scalar(xn[:, c % 2, t, :], x_sb[:, n, :], mv1[:, n, 0:1], rstd1[:, n:n + 1],
                                            ALU.subtract, ALU.mult)
                ins.then_inc(ln1_done, 1)

            def rest_of_q(c):
                for m in range(KD):
                    dve.wait_ge(q_high, KD * c + m + 1)
                    dve.scalar_tensor_tensor(q_rest[:, m, :], work_ps[m][:, :], bq_sb[:, m:m + 1], q_split[:, m, 0, :],
                                             ALU.add, ALU.subtract).then_inc(q_rest_done, 1)
                dve.wait_ge(q_rest_done, KD * (c + 1))
                step(dve.tensor_copy(q_split[:, :, 1, :], q_rest[:, :, :]))
                settle()
                dve.tensor_tensor(q_split[:, :, 2, :], q_rest[:, :, :], q_split[:, :, 1, :],
                                  ALU.subtract).then_inc(q_low, 1)

            stats1_of(0)
            stats1_of(1)
            norm1(0)
            norm1(1)
            dve.wait_ge(s_delta, 16)
            split3(delta_sb[:, :], delta_rest[:, :], delta_split[:, 0, :], delta_split[:, 1, :], delta_split[:, 2, :],
                   d_split_done)
            dve.wait_ge(s_kv_inputs, 96)
            for m in range(KD):
                dve.wait_ge(k_ready, m + 1)
                for b in range(BATCH):
                    step(dve.tensor_scalar(k_full[:, m, b, :], score_ps[m][:, CTX_PAD * b:CTX_PAD * (b + 1)],
                                           bk_sb[:, m:m + 1], tau_sb[:, b:b + 1], ALU.add, ALU.mult))
            split3(k_full[:, :, :, :].rearrange("p m b s -> p m (b s)"), k_rest[:, :, :], k_split[:, :, 0, :],
                   k_split[:, :, 1, :], k_split[:, :, 2, :], k_split_done)
            rest_of_q(0)
            dve.wait_ge(pool_ready, 5)
            dve.wait_ge(s_consts, 16)
            mask = const_of("rest_rows")
            for b in range(BATCH):
                dve.wait_ge(v_ready, 2 * b + 1)
                dve.tensor_tensor(v_main[:, b, :, 0:HDIM], st_ps[b][:, 0:DIM].rearrange("p (h d) -> p h d", d=HDIM),
                                  bv_sb[:, :].rearrange("p (h d) -> p h d", d=HDIM), ALU.add).then_inc(v_done, 1)
                dve.wait_ge(v_ready, 2 * b + 2)
                step(dve.tensor_tensor(v_tmp[:, b, :], o_ps[b][:, 0:DIM], bv_sb[:, :], ALU.add))
                settle()
                wide = mask.rearrange("p (o j q) -> p o j q", o=1, q=1).to_broadcast([P, GROUPS, 4, HDIM])
                dve.tensor_tensor(v_rest[:, b, :, :, 0:HDIM],
                                  v_tmp[:, b, :].rearrange("p (g j d) -> p g j d", g=GROUPS, j=4), wide,
                                  ALU.mult).then_inc(v_done, 1)
                dve.tensor_copy(v_rest[:, b, :, :, HDIM],
                                mask.rearrange("p (o j) -> p o j", o=1).to_broadcast([P, GROUPS, 4])).then_inc(v_done, 1)
            dve.memset(v_main[:, :, :, HDIM:HDIM + 1], 1.0).then_inc(v_done, 1)
            dve.tensor_copy(ident_b, ident).then_inc(v_done, 1)
            sel = const_of("minus_head").rearrange("p (h o) -> p h o", o=1)
            dve.tensor_copy(minus_max_sel[:, :, :], sel.to_broadcast([P, HEADS, HEAD_ROWS])).then_inc(sel_ready, 1)
            step(dve.memset(minus_max_rest[:, :, :], 0.0))
            settle()
            dve.tensor_copy(minus_max_rest[:, :, 0:REST], sel.to_broadcast([P, HEADS, REST])).then_inc(sel_ready, 1)
            step(dve.tensor_copy(upper_b[:, :], const_of("upper")))
            step(dve.memset(ones_b[:, :], 1.0))

            def maxes(c, i):
                n = STEPS * c + i
                t, first = i // SCORE_BANKS, HEADS_PER_BANK * (i % SCORE_BANKS)
                k = min(HEADS_PER_BANK, HEADS - first)
                dve.wait_ge(score_ready, n + 1)
                dve.tensor_reduce(row_max[:, c % 2, t, first:first + k],
                                  score_ps[n % 2][:, 0:k * CTX].rearrange("p (h s) -> p h s", s=CTX), AX_X,
                                  ALU.max).then_inc(max_done, 1)

            def split_max(c):
                dve.wait_ge(max_done, STEPS * (c + 1))
                if c >= 1:
                    dve.wait_ge(mt_ready, c)
                split3(row_max[:, c % 2, :, :], max_rest[:, :, :], max_split[:, :, 0, :], max_split[:, :, 1, :],
                       max_split[:, :, 2, :], max_parts)

            def normalise(t):
                dve.wait_ge(o_turned, t + 1)
                o = work_ps[0][:, :].rearrange("p (h n) -> p h n", n=32)
                step(dve.reciprocal(inverse[:, t % 2, :], o[:, :, HDIM]))
                settle()
                if t >= 2:
                    dve.wait_ge(on_turned, t - 1)
                dve.tensor_tensor(attn[:, t % 2, :].rearrange("p (h d) -> p h d", d=HDIM), o[:, :, 0:HDIM],
                                  inverse[:, t % 2, :].rearrange("p (h o) -> p h o", o=1).to_broadcast([P, HEADS, HDIM]),
                                  ALU.mult).then_inc(on_ready, 1)

            def residual(t):
                dve.wait_ge(proj_ready, t + 1)
                if t == 0:
                    dve.wait_ge(zeros_stored, 16)
                dve.wait_ge(x_biased, t // TPC + 1)
                if t >= 2:
                    dve.wait_ge(rows_stored[t % 2], 16 * (t // 2))
                    dve.wait_ge(x2t_ready, t - 1)
                dve.tensor_tensor(row_buf[:, t % 2, DIM:2 * DIM], work_ps[0][:, 0:DIM], x_sb[:, t, :],
                                  ALU.add).then_inc(x2_done, 1)
                dve.wait_ge(x2_done, t + 1)
                step(dve.bn_stats(stats2[:, t, :], row_buf[:, t % 2, DIM:2 * DIM]))
                settle()
                dve.bn_aggr(mv2[:, t, :], stats2[:, t, :]).then_inc(ln2_stats, 1)

            def norm2(t):
                dve.wait_ge(rstd2_done, t + 1)
                dve.tensor_scalar(row_buf[:, t % 2, 0:DIM], row_buf[:, t % 2, DIM:2 * DIM], mv2[:, t, 0:1],
                                  rstd2[:, t:t + 1], ALU.subtract, ALU.mult).then_inc(ln2_done, 1)

            def logits_of(t):
                dve.wait_ge(logits_ready, t + 1)
                if t == 0:
                    dve.wait_ge(s_out_weights, 64)
                dve.tensor_tensor(logits[:, t, :], work_ps[0][:, 0:EXPERTS], rb_sb[:, :], ALU.add).then_inc(logits_done, 1)

            for c in range(-1, CHUNKS + 1):
                for i in range(STEPS):
                    if i == 2 and c + 2 < CHUNKS:
                        rest_of_q(c + 2)
                    if c + 1 < CHUNKS:
                        maxes(c + 1, i)
                        if i == STEPS - 1:
                            split_max(c + 1)
                    if c >= 1:
                        for at, do in ((OUT_AT, normalise), (OUT_AT + 2, residual), (OUT_AT + 3, norm2),
                                       (OUT_AT + 4, logits_of)):
                            if i >= at and (i - at) % 5 == 0 and (i - at) // 5 < TPC:
                                do(TPC * (c - 1) + (i - at) // 5)
                    if i == 8 and c + 3 < CHUNKS:
                        stats1_of(c + 3)
                    if i == 10 and c + 3 < CHUNKS:
                        norm1(c + 3)

            def wide_e(ap):
                return ap.rearrange("p (t o) -> p t o", o=1).to_broadcast([P, TILES, EXPERTS])

            def row_e(ap):
                return ap.rearrange("p (o e) -> p o e", o=1).to_broadcast([P, TILES, EXPERTS])

            dve.wait_ge(logits_done, TILES)
            step(dve.tensor_reduce(best[:, :], logits[:, :, :], AX_X, ALU.max))
            settle()
            step(dve.tensor_tensor(key[:, :, :], logits[:, :, :], wide_e(best[:, :]), ALU.is_equal))
            settle()
            step(dve.tensor_tensor(key[:, :, :], key[:, :, :], row_e(const_of("first_expert")), ALU.mult))
            settle()
            step(dve.tensor_reduce(best[:, :], key[:, :, :], AX_X, ALU.max))
            settle()
            step(dve.tensor_tensor(onehot[:, :, :], row_e(const_of("first_expert")), wide_e(best[:, :]), ALU.is_equal))
            settle()
            dve.tensor_copy(onehot_b[:, :, :], onehot[:, :, :]).then_inc(onehot_done, 1)
            dve.wait_ge(count_ready, 2)
            step(dve.tensor_copy(counts[:, :, :], score_ps[1][:, 0:TILES * EXPERTS].rearrange("p (t e) -> p e t", e=EXPERTS)))
            settle()
            flat = lambda ap: ap.rearrange("p a b -> p (a b)")
            step(dve.tensor_tensor_scan(flat(upto[:, :, :]), const_of("carry"), flat(counts[:, :, :]), 0.0, ALU.mult, ALU.add))
            settle()
            step(dve.tensor_tensor(over[:, :, :], upto[:, :, TILES - 1:TILES].to_broadcast([P, EXPERTS, TILES]),
                                   const_of("tile_starts").rearrange("p (o t) -> p o t", o=1).to_broadcast([P, EXPERTS, TILES]),
                                   ALU.is_gt))
            settle()
            step(dve.tensor_reduce(n_tiles[:, :], over[:, :, :], AX_X, ALU.add))
            step(dve.tensor_tensor(upto[:, :, :], upto[:, :, :], counts[:, :, :], ALU.subtract))
            settle()
            step(dve.tensor_tensor_scan(last_tile[:, :], const_of("one8"), n_tiles[:, :], 0.0, ALU.mult, ALU.add))
            settle()
            step(dve.tensor_tensor(start_slot[:, :], last_tile[:, :], n_tiles[:, :], ALU.subtract))
            settle()
            step(dve.tensor_scalar(start_slot[:, :], start_slot[:, :], float(P), None, ALU.mult))
            step(dve.tensor_tensor(place[:, :, :], score_ps[0][:, 0:TILES * EXPERTS].rearrange("p (t e) -> p t e", e=EXPERTS),
                                   upto[:, :, :].rearrange("p e t -> p t e"), ALU.add))
            settle()
            step(dve.tensor_tensor(place[:, :, :], place[:, :, :], row_e(start_slot[:, :]), ALU.add))
            settle()
            step(dve.tensor_tensor(place[:, :, :], place[:, :, :], onehot[:, :, :], ALU.mult))
            settle()
            step(dve.tensor_reduce(slot[:, :], place[:, :, :], AX_X, ALU.add))
            settle()

            def wide_j(ap):
                return ap.rearrange("p (t o) -> p t o", o=1).to_broadcast([P, TILES, SLOT_TILES])

            def row_j(ap):
                return ap.rearrange("p (o j) -> p o j", o=1).to_broadcast([P, TILES, SLOT_TILES])

            step(dve.tensor_scalar(slot_lane[:, :], slot[:, :], 1.0 / P, None, ALU.mult))
            step(dve.tensor_scalar(row_f[:, 0, :], const_of("slot_tile"), 1.0, None, ALU.add))
            settle()
            step(dve.tensor_tensor(passed[:, :, :], wide_j(slot_lane[:, :]), row_j(row_f[:, 0, :]), ALU.is_ge))
            settle()
            step(dve.tensor_reduce(slot_tile_of[:, :], passed[:, :, :], AX_X, ALU.add))
            settle()
            step(dve.scalar_tensor_tensor(slot_lane[:, :], slot_tile_of[:, :], -float(P), slot[:, :], ALU.mult, ALU.add))
            step(dve.tensor_tensor(passed[:, :, :], wide_j(slot_tile_of[:, :]), row_j(const_of("slot_tile")), ALU.is_equal))
            settle()
            step(dve.tensor_tensor(lane_hot[:, :, :],
                                   slot_lane[:, :].rearrange("p (t o) -> p t o", o=1).to_broadcast([P, TILES, P]),
                                   const_of("slot_in_tile").rearrange("p (o n) -> p o n", o=1).to_broadcast([P, TILES, P]),
                                   ALU.is_equal))
            step(dve.tensor_tensor(tile_hot[:, :, 0, :], passed[:, :, :], wide_j(const_of("tile_of_token")), ALU.mult))
            step(dve.tensor_scalar(tile_hot[:, :, 1, :], passed[:, :, :], const_of("row"), None, ALU.mult))
            step(dve.tensor_copy(tile_hot[:, :, 2, :], passed[:, :, :]))
            settle()
            dve.sem_inc(hots_done, 1)
            step(dve.tensor_tensor(ended[:, :, :],
                                   const_of("slot_tile").rearrange("p (j o) -> p j o", o=1).to_broadcast([P, SLOT_TILES, EXPERTS]),
                                   last_tile[:, :].rearrange("p (o e) -> p o e", o=1).to_broadcast([P, SLOT_TILES, EXPERTS]),
                                   ALU.is_ge))
            settle()
            step(dve.tensor_reduce(expert_f[:, :], ended[:, :, :], AX_X, ALU.add))
            settle()
            dve.tensor_scalar(tile_expert[:, :], expert_f[0:1, :], float(EXPERTS - 1), None, ALU.min).then_inc(routed, 1)
            dve.wait_ge(info_ready, 1)
            step(dve.tensor_copy(flat(slot_info[:, :, :]), st_ps[0][:, 0:3 * SLOT_TILES]))
            settle()
            step(dve.scalar_tensor_tensor(row_f[:, 0, :], slot_info[:, 0, :], float(P), slot_info[:, 1, :], ALU.mult, ALU.add))
            step(dve.tensor_scalar(row_f[:, 1, :], slot_info[:, 2, :], -1.0, 1.0, ALU.mult, ALU.add))
            settle()
            step(dve.tensor_scalar(row_f[:, 1, :], row_f[:, 1, :], const_of("spare_row"), None, ALU.mult))
            settle()
            dve.tensor_tensor(slot_row[:, :], row_f[:, 0, :], row_f[:, 1, :], ALU.add).then_inc(routed, 1)

            experts = [None] * SLOT_TILES

            def bias(n, j, buffer, known=None):
                if known is None or known + j > 1 or (j == 0 and known > 0):
                    dve.wait_ge(u_ready, n if j == 0 else n - 1)
                dve.wait_ge(h_ready, n + 1)
                dve.tensor_tensor(hidden[:, j % 2, :], h_ps[j % 2][:, :],
                                  b1_sb[:, bass.ds(buffer + experts[j], 1), :].rearrange("p o n -> p (o n)"),
                                  ALU.add).then_inc(biased, 1)

            def gated(n, j, known=None):
                if known is None or known + j > 1 or (j == 0 and known > 0):
                    dve.wait_ge(ut_ready, n if j == 0 else n - 1)
                dve.wait_ge(gate_ready, n + 1)
                dve.tensor_tensor(act_u[:, j % 2, :], hidden[:, j % 2, 0:HQ], gate[:, j % 2, :],
                                  ALU.mult).then_inc(u_ready, 1)

            def add_y(n, j, known=None):
                dve.wait_ge(y_ready, n + 1)
                if known is not None and known < SLOT_TILES:
                    dve.wait_ge(y_started, j + 1)
                dve.tensor_tensor(y_acc[:, j, :], y_ps[j % 2][:, 0:DIM], y_acc[:, j, :], ALU.add).then_inc(y_added, 1)

            dve.wait_ge(quarter_ready, 1)
            dve.wait_ge(routed, 2)
            experts[0] = dve.value_load(tile_expert[0:1, 0:1], min_val=0, max_val=EXPERTS - 1)
            for j in range(SLOT_TILES):
                bias(j, j, 0, j)
                if j + 1 < SLOT_TILES:
                    experts[j + 1] = dve.value_load(tile_expert[0:1, j + 1:j + 2], min_val=0, max_val=EXPERTS - 1)
                gated(j, j, j)
                if j >= 2:
                    add_y(j - 2, j - 2, j - 2)
            dve.wait_ge(y_started, SLOT_TILES)
            with dve.Fori(1, QUARTERS, 1) as q:
                buffer = dve.snap((q % 2) * EXPERTS)
                dve.wait_ge(quarter_ready, q + 1)
                for j in range(SLOT_TILES):
                    n = SLOT_TILES * q + j
                    bias(n, j, buffer)
                    gated(n, j)
                    if j >= 2:
                        add_y(n - 2, j - 2)
                    else:
                        add_y(n - 2, SLOT_TILES + j - 2)
            n = SLOT_TILES * QUARTERS
            for back in (2, 1):
                add_y(n - back, SLOT_TILES - back, n)


def kernel(**inputs):
    import concourse.bacc as _bacc
    from concourse.bass_utils import run_bass_kernel_spmd as _run

    a = {name: np.ascontiguousarray(value) for name, value in inputs.items()}
    ctx_t = np.zeros((BATCH, DIM, CTX_PAD), np.float32)
    ctx_t[:, :, :CTX] = a["ctx_1024"].transpose(0, 2, 1)
    w1 = a["L0_ffn_w1"].reshape(EXPERTS, KD, P, 2, QUARTERS, HQ).transpose(4, 2, 0, 1, 3, 5)
    w2 = a["L0_ffn_w2"].reshape(EXPERTS, QUARTERS, KH, P, DIM).transpose(1, 3, 0, 2, 4)
    arrays = {
        "x": a["x"].reshape(TOKENS, DIM),
        "ctx_t": ctx_t.reshape(BATCH, KD, P, CTX_PAD).transpose(2, 1, 0, 3).reshape(P, KD * BATCH, CTX_PAD),
        "tau": a["condB_tau"],
        "delta": a["fside_BxS2_0"],
        "wq": a["L0_xcond_Wq"].T, "bq": a["L0_xcond_bq"].reshape(KD, P).T,
        "wk": a["L0_xcond_Wk"].T, "bk": a["L0_xcond_bk"].reshape(KD, P).T,
        "wv": a["L0_xcond_Wv"].T, "bv": a["L0_xcond_bv"],
        "wo": a["L0_xcond_Wo"].T, "bo": a["L0_xcond_bo"],
        "rw": a["L0_ffn_router_w"], "rb": a["L0_ffn_router_b"],
        "weights": np.concatenate([w1.reshape(QUARTERS, P, EXPERTS, -1), w2.reshape(QUARTERS, P, EXPERTS, -1)], axis=3),
        "b1": a["L0_ffn_b1"].reshape(EXPERTS, 2, QUARTERS, HQ).transpose(2, 0, 1, 3).reshape(QUARTERS, -1),
        "b2": a["L0_ffn_b2"].reshape(-1),
        "const": CONSTANTS,
        "ones": np.ones((STACK - SPLIT, HEADS * CHUNK), mybir.dt.np(BF16)),
    }
    nc = _bacc.Bacc("TRN2", target_bir_lowering=False, num_devices=1)
    feeds, args = {}, []
    for name, value in arrays.items():
        value = np.ascontiguousarray(value)
        feeds[f"in_{name}_dram"] = value
        args.append(nc.dram_tensor(f"in_{name}_dram", value.shape, mybir.dt.from_np(value.dtype), kind="ExternalInput").ap())
    args.append(nc.dram_tensor("out_dram", (TOKENS + P, DIM), F32, kind="ExternalOutput").ap())
    args.append(nc.dram_tensor("q_parts", (CHUNKS, DIM, 3, CHUNK), BF16).ap())
    args.append(nc.dram_tensor("k_parts", (DIM, 3, BATCH * CTX_PAD), BF16).ap())
    args.append(nc.dram_tensor("d_parts", (BATCH, 3, CTX), BF16).ap())
    args.append(nc.dram_tensor("rows", (TOKENS + P, 2 * DIM), F32).ap())
    build(nc, *args)
    r = _run(nc, [feeds], core_ids=[0])
    return r.results[0]["out_dram"][:TOKENS].reshape(BATCH, SEQ, DIM)
```

```python
from contextlib import ExitStack

import numpy as np

import concourse.bass as bass
from concourse import mybir

ALU = mybir.AluOpType
ACT = mybir.ActivationFunctionType
AX_X = mybir.AxisListType.X
F32 = mybir.dt.float32
BF16 = mybir.dt.bfloat16
I32 = mybir.dt.int32
U32 = mybir.dt.uint32

P = 128
BATCH, SEQ, DIM = 2, 1024, 256
HEADS, HDIM = 16, 16
CTX = 154
CTX_PAD = 160
HEAD_ROWS = 128
REST = CTX - HEAD_ROWS
EXPERTS, HIDDEN = 8, 1024
EPS = 1e-5
SCALE = HDIM ** -0.5

TOKENS = BATCH * SEQ
TILES = TOKENS // P
CHUNK = 512
CHUNKS = TOKENS // CHUNK
TPC = CHUNK // P
KD = DIM // P
GROUPS = HEADS // 4
SLOT_TILES = TOKENS // P + EXPERTS - 1
QUARTERS = 4
HQ = HIDDEN // QUARTERS
KH = HQ // P
HIDDEN_BLOCKS = 2 * KH
BANK = 512

Q_PARTS = (0, 0, 1, 1, 0, 2)
K_PARTS = (0, 1, 0, 1, 2, 0)
SPLIT = len(Q_PARTS) * HDIM
STACK = SPLIT + 3
HEADS_PER_BANK = BANK // CTX
SCORE_BANKS = -(-HEADS // HEADS_PER_BANK)
UNITS_PER_GROUP = 5
UNITS = GROUPS * UNITS_PER_GROUP
EXPERT_W = KD * 2 * HQ + KH * DIM
EARLY_EXPERTS = 2
MAX_AT = 1
UNIT_AT = 3
OUT_PERIOD = 5
TURN_O, NORMALISE, TURN_ON, COPY_ON, PROJECT, RESIDUAL, NORM2, TURN_X2, COPY_X2, ROUTE, LOGITS = 0, 1, 2, 3, 3, 4, 5, 6, 7, 7, 8
Q_AT = {1: (-1, 0), 2: (0, 3), 3: (0, 14)}
PROBS = 6
GATHERS = 4
RING = 3


def constants():
    p = np.arange(P)
    parts = {
        "ident": np.eye(P),
        "upper": (p[:, None] < p[None, :]) * 1.0,
        "slot_in_tile": np.tile(p, (P, 1)),
        "first_expert": np.tile(EXPERTS - np.arange(EXPERTS), (P, 1)),
        "tile_starts": np.tile(np.arange(TILES) * P, (P, 1)),
        "slot_tile": np.tile(np.arange(SLOT_TILES), (P, 1)),
        "tile_of_token": np.tile(np.arange(TILES), (P, 1)),
        "row": p[:, None],
        "one8": np.ones((P, EXPERTS)),
        "spare_row": TOKENS + np.stack([np.tile(p[:, None], (1, SLOT_TILES)),
                                        P * np.arange(SLOT_TILES)[None, :] + p[:, None]], axis=1).reshape(P, -1),
        "carry": np.tile((np.arange(EXPERTS * TILES) % TILES > 0) * 1.0, (P, 1)),
        "minus_head": -1.0 * ((p[:, None] % HEADS == np.arange(HEADS)[None, :]) & (p[:, None] < 3 * HEADS)),
        "rest_rows": ((p[:, None] // 32 == np.arange(4)[None, :]) & (p[:, None] % 32 < REST)) * 1.0,
    }
    at, spans = 0, {}
    for name, a in parts.items():
        spans[name] = (at, at + a.shape[1])
        at += a.shape[1]
    return np.concatenate([np.asarray(a, np.float32) for a in parts.values()], axis=1), spans


CONSTANTS, SPANS = constants()


def build(nc, x, ctx_t, tau, delta, wq, bq, wk, bk, wv, bv, wo, bo, rw, rb, weights, b1, b2, const, ones, out,
          q_parts, k_parts, d_parts, rows):
    ctx = ExitStack()
    early = ExitStack()
    with ctx:
        def sb(name, shape, dt=F32, stack=ctx):
            return stack.enter_context(nc.sbuf_tensor(name, shape, dt))

        def bank(name):
            return ctx.enter_context(nc.psum_tensor(name, [P, BANK], F32))

        def sem(name):
            return ctx.enter_context(nc.semaphore(name))

        consts = sb("consts", [P, CONSTANTS.shape[1]])
        slot_row = sb("slot_row", [P, 2, SLOT_TILES], U32)
        tile_expert = sb("tile_expert", [1, SLOT_TILES], I32)

        def const_of(name):
            return consts[:, SPANS[name][0]:SPANS[name][1]]

        ident = const_of("ident")
        ident_b = sb("ident_b", [P, P], BF16)[:, :]

        b1_sb = sb("b1_sb", [P, QUARTERS * EXPERTS, HIDDEN_BLOCKS])

        sb("first_experts", [P, EARLY_EXPERTS * EXPERT_W], stack=early)
        q_stack = sb("q_stack", [P, 3, HEADS, CHUNK], BF16, early)
        xn = sb("xn", [P, 2, TPC, DIM], stack=early)
        xn_t = sb("xn_t", [P, KD, CHUNK], stack=early)
        q_split = sb("q_split", [P, KD, 3, CHUNK], BF16, early)
        q_rest = sb("q_rest", [P, KD, CHUNK], stack=early)
        k_stack = sb("k_stack", [P, BATCH, HEADS, CTX_PAD], BF16, early)
        minus_max_sel = sb("minus_max_sel", [P, HEADS, HEAD_ROWS], BF16, early)
        minus_max_rest = sb("minus_max_rest", [P, HEADS, 32], BF16, early)
        wq_sb = sb("wq_sb", [P, KD, DIM], stack=early)
        wk_sb = sb("wk_sb", [P, KD, DIM], stack=early)
        wv_sb = sb("wv_sb", [P, KD, DIM], stack=early)
        row_max = sb("row_max", [P, 2, TPC, HEADS], stack=early)
        max_rest = sb("max_rest", [P, TPC, HEADS], stack=early)
        max_split = sb("max_split", [P, TPC, 3, HEADS], BF16, early)
        max_t = sb("max_t", [P, 2, CHUNK], BF16, early)
        v_main = sb("v_main", [P, BATCH, HEADS, 32], stack=early)
        v_rest = sb("v_rest", [P, BATCH, GROUPS, 4, 32], stack=early)
        probs = sb("probs", [P, PROBS, CHUNK], stack=early)
        x_sb = sb("x_sb", [P, TILES, DIM], stack=early)
        attn_t = sb("attn_t", [P, 2, GROUPS, CHUNK], stack=early)
        inverse = sb("inverse", [P, TPC, HEADS], stack=early)
        attn = sb("attn", [P, TPC, DIM], stack=early)
        attn_nt = sb("attn_nt", [P, TPC, KD, P], stack=early)
        row_buf = sb("row_buf", [P, TPC, 2 * DIM], stack=early)
        x2n_t = sb("x2n_t", [P, TPC, KD, P], stack=early)
        bo_sb = sb("bo_sb", [P, DIM], stack=early)
        wo_sb = sb("wo_sb", [P, KD, DIM], stack=early)
        rw_sb = sb("rw_sb", [P, KD, EXPERTS], stack=early)
        rb_sb = sb("rb_sb", [P, EXPERTS], stack=early)
        bq_sb = sb("bq_sb", [P, KD], stack=early)
        bk_sb = sb("bk_sb", [P, KD], stack=early)
        bv_sb = sb("bv_sb", [P, DIM], stack=early)
        tau_sb = sb("tau_sb", [P, BATCH], stack=early)
        stats1 = sb("stats1", [P, TILES, 6], stack=early)
        mv1 = sb("mv1", [P, TILES, 2], stack=early)
        var1 = sb("var1", [P, TILES], stack=early)
        rstd1 = sb("rstd1", [P, TILES], stack=early)
        stats2 = sb("stats2", [P, TILES, 6], stack=early)
        mv2 = sb("mv2", [P, TILES, 2], stack=early)
        var2 = sb("var2", [P, TILES], stack=early)
        rstd2 = sb("rstd2", [P, TILES], stack=early)
        minus_half = sb("minus_half", [P, TPC], stack=early)
        logits = sb("logits", [P, TILES, EXPERTS], stack=early)
        upper_b = sb("upper_b", [P, P], BF16, early)
        ones_b = sb("ones_b", [P, P], BF16, early)
        setup = early.enter_context(ExitStack())
        v_tmp = sb("v_tmp", [P, BATCH, DIM], stack=setup)
        ctx_sb = sb("ctx_sb", [P, KD, BATCH, CTX_PAD], stack=setup)
        k_full = sb("k_full", [P, KD, BATCH, CTX_PAD], stack=setup)
        k_rest = sb("k_rest", [P, KD, BATCH * CTX_PAD], stack=setup)
        k_split = sb("k_split", [P, KD, 3, BATCH * CTX_PAD], BF16, setup)
        delta_sb = sb("delta_sb", [BATCH, CTX], stack=setup)
        delta_rest = sb("delta_rest", [BATCH, CTX], stack=setup)
        delta_split = sb("delta_split", [BATCH, 3, CTX], BF16, setup)
        setup.close()
        best = sb("best", [P, TILES], stack=early)
        key = sb("key", [P, TILES, EXPERTS], stack=early)
        onehot = sb("onehot", [P, TILES, EXPERTS], stack=early)
        onehot_b = sb("onehot_b", [P, TILES, EXPERTS], BF16, early)
        counts = sb("counts", [P, EXPERTS, TILES], stack=early)
        upto = sb("upto", [P, EXPERTS, TILES], stack=early)
        over = sb("over", [P, EXPERTS, TILES], stack=early)
        n_tiles = sb("n_tiles", [P, EXPERTS], stack=early)
        last_tile = sb("last_tile", [P, EXPERTS], stack=early)
        start_slot = sb("start_slot", [P, EXPERTS], stack=early)
        place = sb("place", [P, TILES, EXPERTS], stack=early)
        slot = sb("slot", [P, TILES], stack=early)
        slot_tile_of = sb("slot_tile_of", [P, TILES], stack=early)
        slot_lane = sb("slot_lane", [P, TILES], stack=early)
        passed = sb("passed", [P, TILES, SLOT_TILES], stack=early)
        lane_hot = sb("lane_hot", [P, TILES, P], BF16, early)
        tile_hot = sb("tile_hot", [P, TILES, 3, SLOT_TILES], BF16, early)
        slot_info = sb("slot_info", [P, 3, SLOT_TILES], stack=early)
        row_f = sb("row_f", [P, 2, SLOT_TILES], stack=early)
        unused = sb("unused", [P, SLOT_TILES], stack=early)
        spare = sb("spare", [P, 2, SLOT_TILES], stack=early)
        ended = sb("ended", [P, SLOT_TILES, EXPERTS], stack=early)
        expert_f = sb("expert_f", [P, SLOT_TILES], stack=early)
        early.close()

        w_sb = sb("w_sb", [P, 2 * EXPERTS, EXPERT_W])
        b2_sb = sb("b2_sb", [P, EXPERTS, DIM])
        slot_in = sb("slot_in", [P, GATHERS, 2 * DIM])
        w1_now = sb("w1_now", [P, RING, KD, 2 * HQ])
        hidden = sb("hidden", [P, RING, HIDDEN_BLOCKS, P])
        gate = sb("gate", [P, RING, KH, P])
        act_ut = sb("act_ut", [P, RING, KH, P])
        y_acc = sb("y_acc", [P, SLOT_TILES, DIM])
        slot_xt = sb("slot_xt", [P, SLOT_TILES, KD, P])

        banks = [bank(f"bank{n}") for n in range(8)]
        score_ps, st_ps, o_ps, work_ps = banks[0:2], banks[2:4], banks[4:6], banks[6:8]
        h_ps, y_ps, xin_ps = banks[0:3], banks[3:6], banks[6:8]

        s_consts = sem("s_consts")
        s_x = [sem(f"s_x{c}") for c in range(CHUNKS)]
        s_q_weights = sem("s_q_weights")
        s_kv_inputs = sem("s_kv_inputs")
        s_out_weights = sem("s_out_weights")
        s_delta = sem("s_delta")
        s_biases = sem("s_biases")
        s_quarter = [sem(f"s_quarter{q}") for q in range(QUARTERS)]
        quarter_ready = sem("quarter_ready")
        k_stored = sem("k_stored")
        d_stored = sem("d_stored")
        ones_loaded = sem("ones_loaded")
        k_loaded = sem("k_loaded")
        q_stored = sem("q_stored")
        q_loaded = [sem(f"q_loaded{c}") for c in range(CHUNKS)]
        rows_stored = [sem(f"rows_stored{n}") for n in range(TPC)]
        zeros_stored = sem("zeros_stored")
        gathered = [sem(f"gathered{n}") for n in range(GATHERS)]
        s_out = sem("s_out")
        pool_ready = sem("pool_ready")
        sel_ready = sem("sel_ready")
        dve_step = sem("dve_step")
        pool_step = sem("pool_step")
        k_ready = sem("k_ready")
        k_split_done = sem("k_split_done")
        d_split_done = sem("d_split_done")
        v_ready = sem("v_ready")
        v_done = sem("v_done")
        ln1_stats = sem("ln1_stats")
        ln1_done = sem("ln1_done")
        xt_ready = sem("xt_ready")
        xt_copied = sem("xt_copied")
        q_ready = sem("q_ready")
        rstd1_done = sem("rstd1_done")
        rstd2_done = sem("rstd2_done")
        x_biased = sem("x_biased")
        o_copied = sem("o_copied")
        on_ready = sem("on_ready")
        o_turned = sem("o_turned")
        on_turned = sem("on_turned")
        on_copied = sem("on_copied")
        q_high = sem("q_high")
        q_rest_done = sem("q_rest_done")
        q_low = sem("q_low")
        score_ready = sem("score_ready")
        max_done = sem("max_done")
        max_parts = sem("max_parts")
        mt_ready = sem("mt_ready")
        mt_copied = sem("mt_copied")
        st_ready = sem("st_ready")
        probs_ready = sem("probs_ready")
        pv_done = sem("pv_done")
        proj_ready = sem("proj_ready")
        x2_done = sem("x2_done")
        ln2_stats = sem("ln2_stats")
        ln2_done = sem("ln2_done")
        x2t_ready = sem("x2t_ready")
        x2t_copied = sem("x2t_copied")
        logits_ready = sem("logits_ready")
        logits_done = sem("logits_done")
        onehot_done = sem("onehot_done")
        count_ready = sem("count_ready")
        hots_done = sem("hots_done")
        info_ready = sem("info_ready")
        routed = sem("routed")
        xin_ready = sem("xin_ready")
        xin_copied = sem("xin_copied")
        y_started = sem("y_started")
        h_ready = sem("h_ready")
        biased = sem("biased")
        gate_ready = sem("gate_ready")
        u_ready = sem("u_ready")
        w1_moved = sem("w1_moved")
        y_ready = sem("y_ready")
        y_added = sem("y_added")

        block = ctx.enter_context(nc.Block())

        def stack_slot(c):
            return (c + 2) % 3

        def out_ps(t):
            n = t % TPC if t >= TILES - TPC else 0
            return (work_ps, score_ps, st_ps, o_ps)[n]

        def slot_used(sem_of, engine, n, j):
            if j < RING:
                back = j + SLOT_TILES - max(i for i in range(SLOT_TILES) if i % RING == j)
            else:
                back = RING
            if not isinstance(n, int) or n >= back:
                engine.wait_ge(sem_of, n - back + 1)

        def due(c, i, step):
            return [TPC * (c - 1) + n for n in range(TPC) if c >= 1 and i == OUT_PERIOD * n + step]

        def q_due(c, i, step):
            return [chunk for chunk, at in Q_AT.items() if (c, i) == (at[0], at[1] + step)]

        STEPS = SCORE_BANKS * TPC

        @block.sync
        def _(sp):
            sp.dma_start(x_sb[:, 0:TPC, :], x[0:CHUNK, :].rearrange("(t p) d -> p t d", p=P)).then_inc(s_x[0], 16)
            sp.dma_start(consts[:, :], const).then_inc(s_consts, 16)
            for dst, src in ((ctx_sb[:, :, :, :].rearrange("p k b s -> p (k b) s"), ctx_t),
                             (wk_sb[:, :, :], wk.rearrange("(k p) n -> p k n", p=P)),
                             (bk_sb[:, :], bk),
                             (tau_sb[:, :], tau.rearrange("(o b) -> o b", o=1).to_broadcast([P, BATCH])),
                             (wv_sb[:, :, :], wv.rearrange("(k p) n -> p k n", p=P)),
                             (bv_sb[:, :], bv.rearrange("(o n) -> o n", o=1).to_broadcast([P, DIM]))):
                sp.dma_start(dst, src).then_inc(s_kv_inputs, 16)
            sp.dma_start(delta_sb[:, :], delta).then_inc(s_delta, 16)
            sp.dma_start(wq_sb[:, :, :], wq.rearrange("(k p) n -> p k n", p=P)).then_inc(s_q_weights, 16)
            sp.dma_start(bq_sb[:, :], bq).then_inc(s_q_weights, 16)
            for c in range(1, CHUNKS):
                sp.dma_start(x_sb[:, TPC * c:TPC * (c + 1), :],
                             x[CHUNK * c:CHUNK * (c + 1), :].rearrange("(t p) d -> p t d", p=P)).then_inc(s_x[c], 16)
            sp.dma_start(wo_sb[:, :, :], wo.rearrange("(k p) n -> p k n", p=P)).then_inc(s_out_weights, 16)
            sp.dma_start(bo_sb[:, :], bo.rearrange("(o n) -> o n", o=1).to_broadcast([P, DIM])).then_inc(s_out_weights, 16)
            sp.dma_start(rw_sb[:, :, :], rw.rearrange("(k p) n -> p k n", p=P)).then_inc(s_out_weights, 16)
            sp.dma_start(rb_sb[:, :], rb.rearrange("(o n) -> o n", o=1).to_broadcast([P, EXPERTS])).then_inc(s_out_weights, 16)
            sp.dma_start(b1_sb[:, :, :], b1.rearrange("p (e m) -> p e m", m=HIDDEN_BLOCKS)).then_inc(s_biases, 16)
            for n in range(3):
                sp.dma_start(q_stack[SPLIT:STACK, n, :, :].rearrange("p h s -> p (h s)"), ones).then_inc(ones_loaded, 16)
            sp.wait_ge(pool_ready, 1)
            sp.dma_start(rows[TOKENS:TOKENS + P, :], row_buf[:, 0, :]).then_inc(zeros_stored, 16)
            sp.wait_ge(d_split_done, 1)
            sp.dma_start(d_parts.rearrange("b w s -> b (w s)"),
                         delta_split[:, :, :].rearrange("b w s -> b (w s)")).then_inc(d_stored, 16)
            sp.wait_ge(k_split_done, 1)
            sp.dma_start(k_parts.rearrange("(m p) w s -> p m (w s)", p=P),
                         k_split[:, :, :, :].rearrange("p m w s -> p m (w s)")).then_inc(k_stored, 16)
            sp.wait_ge(d_stored, 16)
            sp.wait_ge(pool_ready, 3)
            for b in range(BATCH):
                src = d_parts[b].rearrange("w (o s) -> w o s", o=1).to_broadcast([3, HEADS, CTX])
                sp.dma_start(k_stack[SPLIT:STACK, b, :, 0:CTX], src).then_inc(k_loaded, 16)
            sp.wait_ge(k_stored, 16)
            for b in range(BATCH):
                for n, part in enumerate(K_PARTS):
                    src = k_parts[:, part, CTX_PAD * b:CTX_PAD * b + CTX].rearrange("(h d) s -> d h s", d=HDIM)
                    sp.dma_start(k_stack[HDIM * n:HDIM * (n + 1), b, :, 0:CTX], src).then_inc(k_loaded, 16)

            def regroup_q(c):
                sp.wait_ge(q_low, c + 1)
                sp.dma_start(q_parts[c].rearrange("(m p) w s -> p m (w s)", p=P),
                             q_split[:, :, :, :].rearrange("p m w s -> p m (w s)")).then_inc(q_stored, 16)
                sp.wait_ge(q_stored, 16 * (c + 1))
                if c >= 3:
                    sp.wait_ge(st_ready, UNITS * (c - 2))
                for n, part in enumerate(Q_PARTS):
                    src = q_parts[c][:, part, :].rearrange("(h d) s -> d h s", d=HDIM)
                    sp.dma_start(q_stack[HDIM * n:HDIM * (n + 1), stack_slot(c), :, :], src).then_inc(q_loaded[c], 16)

            def store_rows(t):
                sp.wait_ge(ln2_done, t + 1)
                sp.dma_start(rows[P * t:P * (t + 1), :], row_buf[:, t % TPC, :]).then_inc(rows_stored[t % TPC], 16)

            def load_experts(q, first, last):
                for e in range(first, last):
                    sp.dma_start(w_sb[:, (q % 2) * EXPERTS + e, :], weights[q, :, e, :]).then_inc(s_quarter[q], 16)

            regroup_q(0)
            for c in range(-1, CHUNKS):
                for chunk, at in Q_AT.items():
                    if at[0] == c:
                        regroup_q(chunk)
                if c == -1:
                    load_experts(0, 0, EARLY_EXPERTS)
                if c == CHUNKS - 1:
                    sp.wait_ge(st_ready, UNITS * c)
                    load_experts(0, EARLY_EXPERTS, EXPERTS - 1)
                if c >= 1:
                    for t in range(TPC):
                        store_rows(TPC * (c - 1) + t)
            sp.wait_ge(st_ready, UNITS * CHUNKS)
            load_experts(0, EXPERTS - 1, EXPERTS)
            for t in range(TILES - TPC, TILES):
                store_rows(t)
            sp.wait_ge(pv_done, UNITS * CHUNKS)
            sp.dma_start(b2_sb[:, :, :].rearrange("p e n -> p (e n)"),
                         b2.rearrange("(o n) -> o n", o=1).to_broadcast([P, EXPERTS * DIM])).then_inc(s_biases, 16)
            for q in range(QUARTERS):
                if q == 1:
                    for e in range(EXPERTS):
                        sp.wait_ge(xin_ready, 2 * e + 2)
                        load_experts(q, e, e + 1)
                if q >= 2:
                    sp.wait_ge(y_ready, SLOT_TILES * (q - 1))
                    load_experts(q, 0, EXPERTS)
                sp.wait_ge(s_quarter[q], 16 * EXPERTS)
                sp.sem_inc(quarter_ready, 1)
            sp.sem_inc(quarter_ready, 1)

        @block.gpsimd
        def _(pool):
            pool.memset(row_buf[:, 0, :], 0.0).then_inc(pool_ready, 1)
            pool.memset(minus_half[:, :], -0.5).then_inc(pool_ready, 1)
            pool.memset(k_stack[:, :, :, CTX:CTX_PAD], 0.0).then_inc(pool_ready, 1)
            pool.memset(v_main[:, :, :, :], 0.0).then_inc(pool_ready, 1)
            pool.memset(v_rest[:, :, :, :, :], 0.0).then_inc(pool_ready, 1)
            pool.memset(max_t[:, :, :], 0.0).then_inc(pool_ready, 1)

            def power(var, rstd, mv, t0, n, signal):
                pool.tensor_scalar(var[:, t0:t0 + n], mv[:, t0:t0 + n, 1], EPS, None, ALU.add).then_inc(pool_step, 1)
                count[0] += 1
                pool.wait_ge(pool_step, count[0])
                pool.tensor_tensor(rstd[:, t0:t0 + n], var[:, t0:t0 + n], minus_half[:, 0:n],
                                   ALU.pow).then_inc(signal, 1)

            count = [0]

            def power1(c):
                pool.wait_ge(ln1_stats, c + 1)
                if c == 0:
                    pool.wait_ge(pool_ready, 2)
                power(var1, rstd1, mv1, TPC * c, TPC, rstd1_done)

            def add_bo(c):
                pool.wait_ge(ln1_done, c + 1)
                if c == 0:
                    pool.wait_ge(s_out_weights, 64)
                at = x_sb[:, TPC * c:TPC * (c + 1), :]
                pool.tensor_tensor(at, at, bo_sb[:, :].rearrange("p (o n) -> p o n", o=1).to_broadcast([P, TPC, DIM]),
                                   ALU.add).then_inc(x_biased, 1)

            def power2(t):
                pool.wait_ge(ln2_stats, t + 1)
                power(var2, rstd2, mv2, t, 1, rstd2_done)

            power1(0)
            power1(1)
            for c in range(-1, CHUNKS):
                for i in range(STEPS):
                    for t in due(c, i, RESIDUAL):
                        power2(t)
                    if c + 3 < CHUNKS and i == 8:
                        power1(c + 3)
                    if c == -1 and i == 12:
                        add_bo(0)
                        add_bo(1)
                    if c == 0 and i == 12:
                        add_bo(2)
                        add_bo(3)
            for t in range(TILES - TPC, TILES):
                power2(t)

            pool.wait_ge(routed, 2)
            pool.wait_ge(zeros_stored, 16)
            for n in range(TPC):
                pool.wait_ge(rows_stored[n], 16 * CHUNKS)

            def gather(j):
                if j >= GATHERS:
                    pool.wait_ge(xin_ready, j - GATHERS + 1)
                    pool.wait_ge(y_started, j - GATHERS + 1)
                pool.indirect_dma_start(slot_in[:, j % GATHERS, :], None, rows,
                                        bass.IndirectOffsetOnAxis(slot_row[:, 0, j:j + 1], 0)).then_inc(gathered[j % GATHERS], 16)

            for j in range(GATHERS):
                gather(j)
            pool.wait_ge(s_biases, 32)
            for j in range(SLOT_TILES):
                expert = pool.value_load(tile_expert[0:1, j:j + 1], min_val=0, max_val=EXPERTS - 1)
                pool.wait_ge(gathered[j % GATHERS], 16 * (j // GATHERS + 1))
                pool.tensor_tensor(y_acc[:, j, :], slot_in[:, j % GATHERS, DIM:2 * DIM],
                                   b2_sb[:, bass.ds(expert, 1), :].rearrange("p o n -> p (o n)"),
                                   ALU.add).then_inc(y_started, 1)
                if j + GATHERS < SLOT_TILES:
                    gather(j + GATHERS)
            for j in range(SLOT_TILES):
                pool.wait_ge(y_added, SLOT_TILES * (QUARTERS - 1) + j + 1)
                pool.indirect_dma_start(out, bass.IndirectOffsetOnAxis(slot_row[:, 1, j:j + 1], 0), y_acc[:, j, :],
                                        None).then_inc(s_out, 16)
            pool.wait_ge(s_out, 16 * SLOT_TILES)

        @block.tensor
        def _(pe):
            pe.wait_ge(s_consts, 16)
            pe.wait_ge(s_kv_inputs, 96)
            for m in range(KD):
                for k in range(KD):
                    ins = pe.matmul(score_ps[m][:, 0:BATCH * CTX_PAD], wk_sb[:, k, P * m:P * (m + 1)],
                                    ctx_sb[:, k, :, :].rearrange("p b s -> p (b s)"), start=(k == 0), stop=(k == KD - 1))
                ins.then_inc(k_ready, 1)
            for b in range(BATCH):
                for k in range(KD):
                    ins = pe.matmul(st_ps[b][:, 0:DIM], ctx_sb[:, k, b, 0:HEAD_ROWS], wv_sb[:, k, :],
                                    start=(k == 0), stop=(k == KD - 1))
                ins.then_inc(v_ready, 1)
                for j in range(4):
                    for k in range(KD):
                        ins = pe.matmul(o_ps[b][32 * j:32 * j + 32, 0:DIM], ctx_sb[:, k, b, HEAD_ROWS:CTX_PAD],
                                        wv_sb[:, k, :], start=(k == 0), stop=(k == KD - 1))
                ins.then_inc(v_ready, 1)

            def turn_x(c):
                pe.wait_ge(ln1_done, c + 1)
                if c >= 1:
                    pe.wait_ge(q_rest_done, KD * c)
                if c >= 2:
                    pe.wait_ge(mt_copied, 1)
                for k in range(KD):
                    for t in range(TPC):
                        ins = pe.transpose(work_ps[k][:, P * t:P * (t + 1)], xn[:, c % 2, t, P * k:P * (k + 1)], ident)
                    ins.then_inc(xt_ready, 1)

            def project_q(c):
                pe.wait_ge(xt_copied, KD * (c + 1))
                if c == 0:
                    pe.wait_ge(s_q_weights, 32)
                for m in range(KD):
                    for k in range(KD):
                        ins = pe.matmul(work_ps[m][:, :], wq_sb[:, k, P * m:P * (m + 1)], xn_t[:, k, :],
                                        start=(k == 0), stop=(k == KD - 1))
                    ins.then_inc(q_ready, 1)

            def scores(c, i):
                n = STEPS * c + i
                if n == 0:
                    pe.wait_ge(pool_ready, 6)
                    pe.wait_ge(ones_loaded, 48)
                    pe.wait_ge(k_loaded, 16 * BATCH * (len(K_PARTS) + 1))
                    pe.wait_ge(k_split_done, 1)
                if i == 0:
                    pe.wait_ge(q_loaded[c], 16 * len(Q_PARTS))
                if n >= 2:
                    pe.wait_ge(max_done, n - 1)
                t, first = i // SCORE_BANKS, HEADS_PER_BANK * (i % SCORE_BANKS)
                for h in range(first, min(first + HEADS_PER_BANK, HEADS)):
                    at = CTX * (h - first)
                    ins = pe.matmul(score_ps[n % 2][:, at:at + CTX], q_stack[0:STACK, stack_slot(c), h, P * t:P * (t + 1)],
                                    k_stack[0:STACK, c // 2, h, 0:CTX], start=True, stop=True)
                ins.then_inc(score_ready, 1)

            def turn_max(c):
                pe.wait_ge(max_parts, c + 1)
                if c >= 2:
                    pe.wait_ge(x2t_copied, TPC * (c - 1))
                pe.wait_ge(q_rest_done, KD * (CHUNKS if c >= 1 else 2))
                turned = work_ps[1][0:3 * HEADS, 0:CHUNK // 2].bitcast(BF16)
                for t in range(TPC):
                    ins = pe.transpose(turned[:, P * t:P * (t + 1)],
                                       max_split[:, t, :, :].rearrange("p w h -> p (w h)"), ident_b)
                ins.then_inc(mt_ready, 1)

            def scores_t(c, u):
                n = UNITS * c + u
                if n == 0:
                    pe.wait_ge(sel_ready, 2)
                    pe.wait_ge(v_done, 3 * BATCH + 2)
                if u == 0:
                    pe.wait_ge(mt_copied, c + 1)
                if n >= 2:
                    pe.wait_ge(probs_ready, n - 1)
                g, j = u // UNITS_PER_GROUP, u % UNITS_PER_GROUP - 1
                if j < 0:
                    for j in range(4):
                        h = 4 * g + j
                        o = st_ps[n % 2][32 * j:32 * j + 32, :]
                        pe.matmul(o, k_stack[0:STACK, c // 2, h, HEAD_ROWS:CTX_PAD], q_stack[0:STACK, stack_slot(c), h, :],
                                  start=True, stop=False)
                        ins = pe.matmul(o, minus_max_rest[:, h, :], max_t[:, c % 2, :], start=False, stop=True)
                else:
                    h = 4 * g + j
                    pe.matmul(st_ps[n % 2][:, :], k_stack[0:STACK, c // 2, h, 0:HEAD_ROWS],
                              q_stack[0:STACK, stack_slot(c), h, :], start=True, stop=False)
                    ins = pe.matmul(st_ps[n % 2][:, :], minus_max_sel[:, h, :], max_t[:, c % 2, :], start=False, stop=True)
                ins.then_inc(st_ready, 1)

            def values_rest(c, g):
                group = GROUPS * c + g
                pe.wait_ge(probs_ready, UNITS_PER_GROUP * group + 1)
                if group >= 2:
                    pe.wait_ge(o_copied, group - 1)
                pe.matmul(o_ps[group % 2][:, :], v_rest[:, c // 2, g, :, :].rearrange("p j n -> p (j n)"),
                          probs[:, UNITS_PER_GROUP * group % PROBS, :], start=True, stop=False,
                          skip_group_check=True).then_inc(pv_done, 1)

            def values(c, g):
                group = GROUPS * c + g
                n = UNITS_PER_GROUP * group + 1
                pe.wait_ge(probs_ready, n + 4)
                for j in range(4):
                    pe.matmul(o_ps[group % 2][32 * j:32 * j + 32, :], v_main[:, c // 2, 4 * g + j, :],
                              probs[:, (n + j) % PROBS, :], start=False, stop=True,
                              skip_group_check=True).then_inc(pv_done, 1)

            def turn_o(t):
                c = t // TPC
                pe.wait_ge(o_copied, GROUPS * (c + 1))
                if t % TPC == 0 and t > 0:
                    pe.wait_ge(logits_done, t)
                elif t % TPC > 0 and c < CHUNKS - 1:
                    pe.wait_ge(x2_done, t)
                if c == CHUNKS - 1:
                    pe.wait_ge(max_done, STEPS * CHUNKS)
                    pe.wait_ge(probs_ready, UNITS * CHUNKS)
                pe.wait_ge(q_rest_done, KD * CHUNKS)
                for g in range(GROUPS):
                    ins = pe.transpose(out_ps(t)[0][:, P * g:P * (g + 1)],
                                       attn_t[:, c % 2, g, P * (t % TPC):P * (t % TPC + 1)], ident)
                ins.then_inc(o_turned, 1)

            def turn_on(t):
                pe.wait_ge(on_ready, t + 1)
                if 1 <= t <= TILES - TPC:
                    pe.wait_ge(x2t_copied, t)
                pe.wait_ge(mt_copied, min(t // TPC + 2, CHUNKS))
                for k in range(KD):
                    ins = pe.transpose(out_ps(t)[1][:, P * k:P * (k + 1)], attn[:, t % TPC, P * k:P * (k + 1)], ident)
                ins.then_inc(on_turned, 1)

            def project_out(t):
                pe.wait_ge(on_copied, t + 1)
                if t % TPC > 0 and t < TILES - TPC:
                    pe.wait_ge(logits_done, t)
                if t == 0:
                    pe.wait_ge(s_out_weights, 64)
                for k in range(KD):
                    ins = pe.matmul(out_ps(t)[0][:, 0:DIM], attn_nt[:, t % TPC, k, :], wo_sb[:, k, :],
                                    start=(k == 0), stop=(k == KD - 1))
                ins.then_inc(proj_ready, 1)

            def turn_x2(t):
                pe.wait_ge(ln2_done, t + 1)
                for k in range(KD):
                    ins = pe.transpose(out_ps(t)[1][:, P * k:P * (k + 1)], row_buf[:, t % TPC, P * k:P * (k + 1)], ident)
                ins.then_inc(x2t_ready, 1)

            def route(t):
                pe.wait_ge(x2t_copied, t + 1)
                if t % TPC < TPC - 1 and t < TILES - TPC:
                    pe.wait_ge(on_ready, t + 2)
                else:
                    pe.wait_ge(x2_done, t + 1)
                for k in range(KD):
                    ins = pe.matmul(out_ps(t)[0][:, 0:EXPERTS], x2n_t[:, t % TPC, k, :], rw_sb[:, k, :],
                                    start=(k == 0), stop=(k == KD - 1))
                ins.then_inc(logits_ready, 1)

            turn_x(0)
            project_q(0)
            for c in range(-1, CHUNKS):
                for i in range(STEPS):
                    for chunk in q_due(c, i, 0):
                        turn_x(chunk)
                    for chunk in q_due(c, i, 1):
                        project_q(chunk)
                    if c + 1 < CHUNKS:
                        scores(c + 1, i)
                    if c >= 0:
                        if 0 <= i - UNIT_AT < UNITS:
                            scores_t(c, i - UNIT_AT)
                        unit = i - UNIT_AT - 1
                        if 0 <= unit < UNITS and unit % UNITS_PER_GROUP == 0:
                            values_rest(c, unit // UNITS_PER_GROUP)
                        if 0 <= unit < UNITS and unit % UNITS_PER_GROUP == UNITS_PER_GROUP - 1:
                            values(c, unit // UNITS_PER_GROUP)
                        if i == MAX_AT:
                            turn_max(c)
                    for at, step in ((TURN_O, turn_o), (PROJECT, project_out), (TURN_X2, turn_x2), (ROUTE, route),
                                     (TURN_ON, turn_on)):
                        for t in due(c, i, at):
                            step(t)
            for step in (turn_o, turn_on, project_out, turn_x2, route):
                for t in range(TILES - TPC, TILES):
                    step(t)

            pe.wait_ge(onehot_done, 1)
            hot = onehot_b[:, :, :].rearrange("p t e -> p (t e)")
            pe.matmul(score_ps[0][:, 0:TILES * EXPERTS], upper_b[:, :], hot, start=True, stop=True).then_inc(count_ready, 1)
            pe.matmul(score_ps[1][:, 0:TILES * EXPERTS], ones_b[:, :], hot, start=True, stop=True).then_inc(count_ready, 1)
            pe.wait_ge(hots_done, 1)
            for t in range(TILES):
                ins = pe.matmul(st_ps[0][:, 0:3 * SLOT_TILES], lane_hot[:, t, :],
                                tile_hot[:, t, :, :].rearrange("p w j -> p (w j)"), start=(t == 0), stop=(t == TILES - 1))
            ins.then_inc(info_ready, 1)

            experts = [None] * SLOT_TILES

            def load_expert(j):
                experts[j] = pe.value_load(tile_expert[0:1, j:j + 1], min_val=0, max_val=EXPERTS - 1)

            def turn_in(j):
                pe.wait_ge(gathered[j % GATHERS], 16 * (j // GATHERS + 1))
                if j >= 2:
                    pe.wait_ge(xin_copied, j - 1)
                for k in range(KD):
                    ins = pe.transpose(xin_ps[j % 2][:, P * k:P * (k + 1)], slot_in[:, j % GATHERS, P * k:P * (k + 1)], ident)
                ins.then_inc(xin_ready, 1)

            def up(n, j):
                slot_used(biased, pe, n, j)
                pe.wait_ge(w1_moved, n + 1)
                for m in range(HIDDEN_BLOCKS):
                    for k in range(KD):
                        ins = pe.matmul(h_ps[j % RING][:, P * m:P * (m + 1)], w1_now[:, j % RING, k, P * m:P * (m + 1)],
                                        slot_xt[:, j, k, :], start=(k == 0), stop=(k == KD - 1))
                ins.then_inc(h_ready, 1)

            def down(n, j, buffer):
                slot_used(y_added, pe, n, j)
                pe.wait_ge(u_ready, n + 1)
                for k in range(KH):
                    at = KD * 2 * HQ + k * DIM
                    ins = pe.matmul(y_ps[j % RING][:, 0:DIM], act_ut[:, j % RING, k, :],
                                    w_sb[:, bass.ds(buffer + experts[j], 1), at:at + DIM].rearrange("p o n -> p (o n)"),
                                    start=(k == 0), stop=(k == KH - 1))
                ins.then_inc(y_ready, 1)

            pe.wait_ge(routed, 2)
            load_expert(0)
            turn_in(0)
            turn_in(1)
            for j in range(SLOT_TILES):
                pe.wait_ge(xin_copied, j + 1)
                up(j, j)
                if j + 1 < SLOT_TILES:
                    load_expert(j + 1)
                if j + 2 < SLOT_TILES:
                    turn_in(j + 2)
                if j >= 2:
                    down(j - 2, j - 2, 0)
            with pe.Fori(1, QUARTERS, 1) as q:
                buffer = pe.snap((q % 2) * EXPERTS)
                other = pe.snap(((q + 1) % 2) * EXPERTS)
                for j in range(SLOT_TILES):
                    n = SLOT_TILES * q + j
                    up(n, j)
                    down(n - 2, (j - 2) % SLOT_TILES, buffer if j >= 2 else other)
            n = SLOT_TILES * QUARTERS
            for back in (2, 1):
                down(n - back, SLOT_TILES - back, ((QUARTERS - 1) % 2) * EXPERTS)

        @block.scalar
        def _(act):
            def copy_xt(c):
                for k in range(KD):
                    act.wait_ge(xt_ready, KD * c + k + 1)
                    if c >= 1 and k == 0:
                        act.wait_ge(q_ready, KD * c)
                    act.activation(xn_t[:, k, :], work_ps[k][:, :], ACT.Copy).then_inc(xt_copied, 1)

            def q_highs(c):
                if c == 0:
                    act.wait_ge(s_q_weights, 32)
                for m in range(KD):
                    act.wait_ge(q_ready, KD * c + m + 1)
                    if c >= 1 and m == 0:
                        act.wait_ge(q_stored, 16 * c)
                    act.activation(q_split[:, m, 0, :], work_ps[m][:, :], ACT.Identity,
                                   bias=bq_sb[:, m:m + 1]).then_inc(q_high, 1)

            def copy_max(c):
                act.wait_ge(mt_ready, c + 1)
                if c == 0:
                    act.wait_ge(pool_ready, 6)
                if c >= 2:
                    act.wait_ge(st_ready, UNITS * (c - 1))
                act.activation(max_t[0:3 * HEADS, c % 2, :], work_ps[1][0:3 * HEADS, 0:CHUNK // 2].bitcast(BF16),
                               ACT.Copy).then_inc(mt_copied, 1)

            def exps(c, u):
                n = UNITS * c + u
                act.wait_ge(st_ready, n + 1)
                if n >= PROBS:
                    act.wait_ge(pv_done, n - PROBS + 1)
                act.activation(probs[:, n % PROBS, :], st_ps[n % 2][:, :], ACT.Exp, scale=SCALE).then_inc(probs_ready, 1)

            def copy_o(c, g):
                group = GROUPS * c + g
                act.wait_ge(pv_done, UNITS_PER_GROUP * (group + 1))
                if c >= 2:
                    act.wait_ge(o_turned, TPC * (c - 1))
                act.activation(attn_t[:, c % 2, g, :], o_ps[group % 2][:, :], ACT.Copy).then_inc(o_copied, 1)

            def copy_on(t):
                act.wait_ge(on_turned, t + 1)
                if t >= TPC:
                    act.wait_ge(proj_ready, t - TPC + 1)
                act.activation(attn_nt[:, t % TPC, :, :].rearrange("p k n -> p (k n)"), out_ps(t)[1][:, 0:DIM],
                               ACT.Copy).then_inc(on_copied, 1)

            def copy_x2(t):
                act.wait_ge(x2t_ready, t + 1)
                if t >= TPC:
                    act.wait_ge(logits_ready, t - TPC + 1)
                act.activation(x2n_t[:, t % TPC, :, :].rearrange("p k n -> p (k n)"), out_ps(t)[1][:, 0:DIM],
                               ACT.Copy).then_inc(x2t_copied, 1)

            copy_xt(0)
            q_highs(0)
            for c in range(-1, CHUNKS):
                for i in range(STEPS):
                    for t in due(c, i, COPY_ON):
                        copy_on(t)
                    for t in due(c, i, COPY_X2):
                        copy_x2(t)
                    if c >= 0 and i == MAX_AT + 1:
                        copy_max(c)
                    for chunk in q_due(c, i, 0):
                        copy_xt(chunk)
                    for chunk in q_due(c, i, 1):
                        q_highs(chunk)
                    unit = i - UNIT_AT
                    if c >= 0 and 0 <= unit < UNITS:
                        exps(c, unit)
                    if c >= 0 and 1 <= unit <= UNITS and unit % UNITS_PER_GROUP == 0:
                        copy_o(c, unit // UNITS_PER_GROUP - 1)
            for copy in (copy_on, copy_x2):
                for t in range(TILES - TPC, TILES):
                    copy(t)

            def copy_in(j):
                act.wait_ge(xin_ready, j + 1)
                act.activation(slot_xt[:, j, :, :].rearrange("p k n -> p (k n)"), xin_ps[j % 2][:, 0:DIM],
                               ACT.Copy).then_inc(xin_copied, 1)

            def move_w1(n, j, buffer):
                slot_used(h_ready, act, n, j)
                act.activation(w1_now[:, j % RING, :, :].rearrange("p k n -> p (k n)"),
                               w_sb[:, bass.ds(buffer + experts[j], 1), 0:KD * 2 * HQ].rearrange("p o n -> p (o n)"),
                               ACT.Copy).then_inc(w1_moved, 1)

            def gates(n, j):
                slot_used(u_ready, act, n, j)
                act.wait_ge(biased, n + 1)
                act.activation(gate[:, j % RING, :, :], hidden[:, j % RING, KH:2 * KH, :], ACT.Sigmoid).then_inc(gate_ready, 1)

            def load_expert(j):
                experts[j] = act.value_load(tile_expert[0:1, j:j + 1], min_val=0, max_val=EXPERTS - 1)

            experts = [None] * SLOT_TILES
            act.wait_ge(routed, 2)
            load_expert(0)
            act.wait_ge(quarter_ready, 1)
            move_w1(0, 0, 0)
            copy_in(0)
            copy_in(1)
            for j in range(SLOT_TILES):
                if j + 1 < SLOT_TILES:
                    load_expert(j + 1)
                    move_w1(j + 1, j + 1, 0)
                else:
                    act.wait_ge(quarter_ready, 2)
                    move_w1(j + 1, 0, EXPERTS)
                if j + 2 < SLOT_TILES:
                    copy_in(j + 2)
                gates(j, j)
            with act.Fori(1, QUARTERS, 1) as q:
                buffer = act.snap((q % 2) * EXPERTS)
                other = act.snap(((q + 1) % 2) * EXPERTS)
                for j in range(SLOT_TILES):
                    n = SLOT_TILES * q + j
                    if j + 1 < SLOT_TILES:
                        move_w1(n + 1, j + 1, buffer)
                    else:
                        act.wait_ge(quarter_ready, q + 2)
                        move_w1(n + 1, 0, other)
                    gates(n, j)

        @block.vector
        def _(dve):
            count = [0]

            def step(ins):
                ins.then_inc(dve_step, 1)
                count[0] += 1

            def settle():
                dve.wait_ge(dve_step, count[0])

            def split3(full, rest, high, mid, low, signal):
                settle()
                step(dve.tensor_copy(high, full))
                settle()
                step(dve.tensor_tensor(rest, full, high, ALU.subtract))
                settle()
                step(dve.tensor_copy(mid, rest))
                settle()
                dve.tensor_tensor(low, rest, mid, ALU.subtract).then_inc(signal, 1)

            def stats1_of(c):
                dve.wait_ge(s_x[c], 16)
                for t in range(TPC * c, TPC * (c + 1)):
                    step(dve.bn_stats(stats1[:, t, :], x_sb[:, t, :]))
                settle()
                for t in range(TPC * c, TPC * (c + 1)):
                    ins = dve.bn_aggr(mv1[:, t, :], stats1[:, t, :])
                ins.then_inc(ln1_stats, 1)

            def norm1(c):
                dve.wait_ge(rstd1_done, c + 1)
                if c >= 2:
                    dve.wait_ge(xt_ready, KD * (c - 1))
                for t in range(TPC):
                    n = TPC * c + t
                    ins = dve.tensor_scalar(xn[:, c % 2, t, :], x_sb[:, n, :], mv1[:, n, 0:1], rstd1[:, n:n + 1],
                                            ALU.subtract, ALU.mult)
                ins.then_inc(ln1_done, 1)

            def rest_of_q(c):
                for m in range(KD):
                    dve.wait_ge(q_high, KD * c + m + 1)
                    dve.scalar_tensor_tensor(q_rest[:, m, :], work_ps[m][:, :], bq_sb[:, m:m + 1], q_split[:, m, 0, :],
                                             ALU.add, ALU.subtract).then_inc(q_rest_done, 1)
                dve.wait_ge(q_rest_done, KD * (c + 1))
                step(dve.tensor_copy(q_split[:, :, 1, :], q_rest[:, :, :]))
                settle()
                dve.tensor_tensor(q_split[:, :, 2, :], q_rest[:, :, :], q_split[:, :, 1, :],
                                  ALU.subtract).then_inc(q_low, 1)

            stats1_of(0)
            stats1_of(1)
            norm1(0)
            norm1(1)
            dve.wait_ge(s_delta, 16)
            split3(delta_sb[:, :], delta_rest[:, :], delta_split[:, 0, :], delta_split[:, 1, :], delta_split[:, 2, :],
                   d_split_done)
            dve.wait_ge(s_kv_inputs, 96)
            for m in range(KD):
                dve.wait_ge(k_ready, m + 1)
                for b in range(BATCH):
                    step(dve.tensor_scalar(k_full[:, m, b, :], score_ps[m][:, CTX_PAD * b:CTX_PAD * (b + 1)],
                                           bk_sb[:, m:m + 1], tau_sb[:, b:b + 1], ALU.add, ALU.mult))
            split3(k_full[:, :, :, :].rearrange("p m b s -> p m (b s)"), k_rest[:, :, :], k_split[:, :, 0, :],
                   k_split[:, :, 1, :], k_split[:, :, 2, :], k_split_done)
            rest_of_q(0)
            dve.wait_ge(pool_ready, 5)
            dve.wait_ge(s_consts, 16)
            mask = const_of("rest_rows")
            for b in range(BATCH):
                dve.wait_ge(v_ready, 2 * b + 1)
                dve.tensor_tensor(v_main[:, b, :, 0:HDIM], st_ps[b][:, 0:DIM].rearrange("p (h d) -> p h d", d=HDIM),
                                  bv_sb[:, :].rearrange("p (h d) -> p h d", d=HDIM), ALU.add).then_inc(v_done, 1)
                dve.wait_ge(v_ready, 2 * b + 2)
                step(dve.tensor_tensor(v_tmp[:, b, :], o_ps[b][:, 0:DIM], bv_sb[:, :], ALU.add))
                settle()
                wide = mask.rearrange("p (o j q) -> p o j q", o=1, q=1).to_broadcast([P, GROUPS, 4, HDIM])
                dve.tensor_tensor(v_rest[:, b, :, :, 0:HDIM],
                                  v_tmp[:, b, :].rearrange("p (g j d) -> p g j d", g=GROUPS, j=4), wide,
                                  ALU.mult).then_inc(v_done, 1)
                dve.tensor_copy(v_rest[:, b, :, :, HDIM],
                                mask.rearrange("p (o j) -> p o j", o=1).to_broadcast([P, GROUPS, 4])).then_inc(v_done, 1)
            dve.memset(v_main[:, :, :, HDIM:HDIM + 1], 1.0).then_inc(v_done, 1)
            dve.tensor_copy(ident_b, ident).then_inc(v_done, 1)
            sel = const_of("minus_head").rearrange("p (h o) -> p h o", o=1)
            dve.tensor_copy(minus_max_sel[:, :, :], sel.to_broadcast([P, HEADS, HEAD_ROWS])).then_inc(sel_ready, 1)
            step(dve.memset(minus_max_rest[:, :, :], 0.0))
            settle()
            dve.tensor_copy(minus_max_rest[:, :, 0:REST], sel.to_broadcast([P, HEADS, REST])).then_inc(sel_ready, 1)
            step(dve.tensor_copy(upper_b[:, :], const_of("upper")))
            step(dve.memset(ones_b[:, :], 1.0))

            def maxes(c, i):
                n = STEPS * c + i
                t, first = i // SCORE_BANKS, HEADS_PER_BANK * (i % SCORE_BANKS)
                k = min(HEADS_PER_BANK, HEADS - first)
                dve.wait_ge(score_ready, n + 1)
                dve.tensor_reduce(row_max[:, c % 2, t, first:first + k],
                                  score_ps[n % 2][:, 0:k * CTX].rearrange("p (h s) -> p h s", s=CTX), AX_X,
                                  ALU.max).then_inc(max_done, 1)

            def split_max(c):
                dve.wait_ge(max_done, STEPS * (c + 1))
                if c >= 1:
                    dve.wait_ge(mt_ready, c)
                split3(row_max[:, c % 2, :, :], max_rest[:, :, :], max_split[:, :, 0, :], max_split[:, :, 1, :],
                       max_split[:, :, 2, :], max_parts)

            def normalise(t):
                dve.wait_ge(o_turned, t + 1)
                o = out_ps(t)[0][:, :].rearrange("p (h n) -> p h n", n=32)
                step(dve.reciprocal(inverse[:, t % TPC, :], o[:, :, HDIM]))
                settle()
                if t >= TPC:
                    dve.wait_ge(on_turned, t - TPC + 1)
                dve.tensor_tensor(attn[:, t % TPC, :].rearrange("p (h d) -> p h d", d=HDIM), o[:, :, 0:HDIM],
                                  inverse[:, t % TPC, :].rearrange("p (h o) -> p h o", o=1).to_broadcast([P, HEADS, HDIM]),
                                  ALU.mult).then_inc(on_ready, 1)

            def residual(t):
                dve.wait_ge(proj_ready, t + 1)
                if t == 0:
                    dve.wait_ge(zeros_stored, 16)
                dve.wait_ge(x_biased, t // TPC + 1)
                if t >= TPC:
                    dve.wait_ge(rows_stored[t % TPC], 16 * (t // TPC))
                    dve.wait_ge(x2t_ready, t - TPC + 1)
                dve.tensor_tensor(row_buf[:, t % TPC, DIM:2 * DIM], out_ps(t)[0][:, 0:DIM], x_sb[:, t, :],
                                  ALU.add).then_inc(x2_done, 1)
                dve.wait_ge(x2_done, t + 1)
                step(dve.bn_stats(stats2[:, t, :], row_buf[:, t % TPC, DIM:2 * DIM]))
                settle()
                dve.bn_aggr(mv2[:, t, :], stats2[:, t, :]).then_inc(ln2_stats, 1)

            def norm2(t):
                dve.wait_ge(rstd2_done, t + 1)
                dve.tensor_scalar(row_buf[:, t % TPC, 0:DIM], row_buf[:, t % TPC, DIM:2 * DIM], mv2[:, t, 0:1],
                                  rstd2[:, t:t + 1], ALU.subtract, ALU.mult).then_inc(ln2_done, 1)

            def logits_of(t):
                dve.wait_ge(logits_ready, t + 1)
                if t == 0:
                    dve.wait_ge(s_out_weights, 64)
                dve.tensor_tensor(logits[:, t, :], out_ps(t)[0][:, 0:EXPERTS], rb_sb[:, :], ALU.add).then_inc(logits_done, 1)

            for c in range(-1, CHUNKS):
                for i in range(STEPS):
                    for chunk in q_due(c, i, 2):
                        rest_of_q(chunk)
                    if c + 1 < CHUNKS:
                        maxes(c + 1, i)
                        if i == STEPS - 1:
                            split_max(c + 1)
                    for at, do in ((LOGITS, logits_of), (NORMALISE, normalise), (RESIDUAL, residual), (NORM2, norm2)):
                        for t in due(c, i, at):
                            do(t)
                    if i == 8 and c + 3 < CHUNKS:
                        stats1_of(c + 3)
                    if i == 10 and c + 3 < CHUNKS:
                        norm1(c + 3)
            for do in (normalise, residual, norm2, logits_of):
                for t in range(TILES - TPC, TILES):
                    do(t)

            def wide_e(ap):
                return ap.rearrange("p (t o) -> p t o", o=1).to_broadcast([P, TILES, EXPERTS])

            def row_e(ap):
                return ap.rearrange("p (o e) -> p o e", o=1).to_broadcast([P, TILES, EXPERTS])

            dve.wait_ge(logits_done, TILES)
            step(dve.tensor_reduce(best[:, :], logits[:, :, :], AX_X, ALU.max))
            settle()
            step(dve.tensor_tensor(key[:, :, :], logits[:, :, :], wide_e(best[:, :]), ALU.is_equal))
            settle()
            step(dve.tensor_tensor(key[:, :, :], key[:, :, :], row_e(const_of("first_expert")), ALU.mult))
            settle()
            step(dve.tensor_reduce(best[:, :], key[:, :, :], AX_X, ALU.max))
            settle()
            step(dve.tensor_tensor(onehot[:, :, :], row_e(const_of("first_expert")), wide_e(best[:, :]), ALU.is_equal))
            settle()
            dve.tensor_copy(onehot_b[:, :, :], onehot[:, :, :]).then_inc(onehot_done, 1)
            dve.wait_ge(count_ready, 2)
            step(dve.tensor_copy(counts[:, :, :], score_ps[1][:, 0:TILES * EXPERTS].rearrange("p (t e) -> p e t", e=EXPERTS)))
            settle()
            flat = lambda ap: ap.rearrange("p a b -> p (a b)")
            step(dve.tensor_tensor_scan(flat(upto[:, :, :]), const_of("carry"), flat(counts[:, :, :]), 0.0, ALU.mult, ALU.add))
            settle()
            step(dve.tensor_tensor(over[:, :, :], upto[:, :, TILES - 1:TILES].to_broadcast([P, EXPERTS, TILES]),
                                   const_of("tile_starts").rearrange("p (o t) -> p o t", o=1).to_broadcast([P, EXPERTS, TILES]),
                                   ALU.is_gt))
            settle()
            step(dve.tensor_reduce(n_tiles[:, :], over[:, :, :], AX_X, ALU.add))
            step(dve.tensor_tensor(upto[:, :, :], upto[:, :, :], counts[:, :, :], ALU.subtract))
            settle()
            step(dve.tensor_tensor_scan(last_tile[:, :], const_of("one8"), n_tiles[:, :], 0.0, ALU.mult, ALU.add))
            settle()
            step(dve.tensor_tensor(start_slot[:, :], last_tile[:, :], n_tiles[:, :], ALU.subtract))
            settle()
            step(dve.tensor_scalar(start_slot[:, :], start_slot[:, :], float(P), None, ALU.mult))
            step(dve.tensor_tensor(place[:, :, :], score_ps[0][:, 0:TILES * EXPERTS].rearrange("p (t e) -> p t e", e=EXPERTS),
                                   upto[:, :, :].rearrange("p e t -> p t e"), ALU.add))
            settle()
            step(dve.tensor_tensor(place[:, :, :], place[:, :, :], row_e(start_slot[:, :]), ALU.add))
            settle()
            step(dve.tensor_tensor(place[:, :, :], place[:, :, :], onehot[:, :, :], ALU.mult))
            settle()
            step(dve.tensor_reduce(slot[:, :], place[:, :, :], AX_X, ALU.add))
            settle()

            def wide_j(ap):
                return ap.rearrange("p (t o) -> p t o", o=1).to_broadcast([P, TILES, SLOT_TILES])

            def row_j(ap):
                return ap.rearrange("p (o j) -> p o j", o=1).to_broadcast([P, TILES, SLOT_TILES])

            step(dve.tensor_scalar(slot_lane[:, :], slot[:, :], 1.0 / P, None, ALU.mult))
            step(dve.tensor_scalar(row_f[:, 0, :], const_of("slot_tile"), 1.0, None, ALU.add))
            settle()
            step(dve.tensor_tensor(passed[:, :, :], wide_j(slot_lane[:, :]), row_j(row_f[:, 0, :]), ALU.is_ge))
            settle()
            step(dve.tensor_reduce(slot_tile_of[:, :], passed[:, :, :], AX_X, ALU.add))
            settle()
            step(dve.scalar_tensor_tensor(slot_lane[:, :], slot_tile_of[:, :], -float(P), slot[:, :], ALU.mult, ALU.add))
            step(dve.tensor_tensor(passed[:, :, :], wide_j(slot_tile_of[:, :]), row_j(const_of("slot_tile")), ALU.is_equal))
            settle()
            step(dve.tensor_tensor(lane_hot[:, :, :],
                                   slot_lane[:, :].rearrange("p (t o) -> p t o", o=1).to_broadcast([P, TILES, P]),
                                   const_of("slot_in_tile").rearrange("p (o n) -> p o n", o=1).to_broadcast([P, TILES, P]),
                                   ALU.is_equal))
            step(dve.tensor_tensor(tile_hot[:, :, 0, :], passed[:, :, :], wide_j(const_of("tile_of_token")), ALU.mult))
            step(dve.tensor_scalar(tile_hot[:, :, 1, :], passed[:, :, :], const_of("row"), None, ALU.mult))
            step(dve.tensor_copy(tile_hot[:, :, 2, :], passed[:, :, :]))
            settle()
            dve.sem_inc(hots_done, 1)
            step(dve.tensor_tensor(ended[:, :, :],
                                   const_of("slot_tile").rearrange("p (j o) -> p j o", o=1).to_broadcast([P, SLOT_TILES, EXPERTS]),
                                   last_tile[:, :].rearrange("p (o e) -> p o e", o=1).to_broadcast([P, SLOT_TILES, EXPERTS]),
                                   ALU.is_ge))
            settle()
            step(dve.tensor_reduce(expert_f[:, :], ended[:, :, :], AX_X, ALU.add))
            settle()
            dve.tensor_scalar(tile_expert[:, :], expert_f[0:1, :], float(EXPERTS - 1), None, ALU.min).then_inc(routed, 1)
            dve.wait_ge(info_ready, 1)
            step(dve.tensor_copy(flat(slot_info[:, :, :]), st_ps[0][:, 0:3 * SLOT_TILES]))
            settle()
            step(dve.scalar_tensor_tensor(row_f[:, 0, :], slot_info[:, 0, :], float(P), slot_info[:, 1, :], ALU.mult, ALU.add))
            step(dve.tensor_scalar(unused[:, :], slot_info[:, 2, :], -1.0, 1.0, ALU.mult, ALU.add))
            settle()

            def both(ap):
                return ap.rearrange("p (o j) -> p o j", o=1).to_broadcast([P, 2, SLOT_TILES])

            step(dve.tensor_tensor(spare[:, :, :], both(unused[:, :]),
                                   const_of("spare_row").rearrange("p (w j) -> p w j", w=2), ALU.mult))
            settle()
            dve.tensor_tensor(slot_row[:, :, :], spare[:, :, :], both(row_f[:, 0, :]), ALU.add).then_inc(routed, 1)

            experts = [None] * SLOT_TILES

            def bias(n, j, first):
                slot_used(u_ready, dve, n, j)
                dve.wait_ge(h_ready, n + 1)
                b1_now = b1_sb[:, bass.ds(first + experts[j], 1), :].rearrange("p o (m n) -> p (o m) n", n=1)
                dve.tensor_tensor(hidden[:, j % RING, :, :], h_ps[j % RING][:, :].rearrange("p (m n) -> p m n", n=P),
                                  b1_now.to_broadcast([P, HIDDEN_BLOCKS, P]), ALU.add).then_inc(biased, 1)

            def gated(n, j):
                slot_used(y_ready, dve, n, j)
                dve.wait_ge(gate_ready, n + 1)
                dve.tensor_tensor(act_ut[:, j % RING, :, :], hidden[:, j % RING, 0:KH, :], gate[:, j % RING, :, :],
                                  ALU.mult).then_inc(u_ready, 1)

            def add_y(n, j, known=None):
                dve.wait_ge(y_ready, n + 1)
                if known is not None and known < SLOT_TILES:
                    dve.wait_ge(y_started, j + 1)
                dve.tensor_tensor(y_acc[:, j, :], y_ps[j % RING][:, 0:DIM], y_acc[:, j, :], ALU.add).then_inc(y_added, 1)

            dve.wait_ge(s_biases, 32)
            dve.wait_ge(routed, 2)
            experts[0] = dve.value_load(tile_expert[0:1, 0:1], min_val=0, max_val=EXPERTS - 1)
            for j in range(SLOT_TILES):
                bias(j, j, 0)
                if j + 1 < SLOT_TILES:
                    experts[j + 1] = dve.value_load(tile_expert[0:1, j + 1:j + 2], min_val=0, max_val=EXPERTS - 1)
                gated(j, j)
                if j >= 2:
                    add_y(j - 2, j - 2, j - 2)
            dve.wait_ge(y_started, SLOT_TILES)
            with dve.Fori(1, QUARTERS, 1) as q:
                first = dve.snap(q * EXPERTS)
                for j in range(SLOT_TILES):
                    n = SLOT_TILES * q + j
                    bias(n, j, first)
                    gated(n, j)
                    if j >= 2:
                        add_y(n - 2, j - 2)
                    else:
                        add_y(n - 2, SLOT_TILES + j - 2)
            n = SLOT_TILES * QUARTERS
            for back in (2, 1):
                add_y(n - back, SLOT_TILES - back, n)


def kernel(**inputs):
    import concourse.bacc as _bacc
    from concourse.bass_utils import run_bass_kernel_spmd as _run

    a = {name: np.ascontiguousarray(value) for name, value in inputs.items()}
    ctx_t = np.zeros((BATCH, DIM, CTX_PAD), np.float32)
    ctx_t[:, :, :CTX] = a["ctx_1024"].transpose(0, 2, 1)
    w1 = a["L0_ffn_w1"].reshape(EXPERTS, KD, P, 2, QUARTERS, HQ).transpose(4, 2, 0, 1, 3, 5)
    w2 = a["L0_ffn_w2"].reshape(EXPERTS, QUARTERS, KH, P, DIM).transpose(1, 3, 0, 2, 4)
    arrays = {
        "x": a["x"].reshape(TOKENS, DIM),
        "ctx_t": ctx_t.reshape(BATCH, KD, P, CTX_PAD).transpose(2, 1, 0, 3).reshape(P, KD * BATCH, CTX_PAD),
        "tau": a["condB_tau"],
        "delta": a["fside_BxS2_0"],
        "wq": a["L0_xcond_Wq"].T, "bq": a["L0_xcond_bq"].reshape(KD, P).T,
        "wk": a["L0_xcond_Wk"].T, "bk": a["L0_xcond_bk"].reshape(KD, P).T,
        "wv": a["L0_xcond_Wv"].T, "bv": a["L0_xcond_bv"],
        "wo": a["L0_xcond_Wo"].T, "bo": a["L0_xcond_bo"],
        "rw": a["L0_ffn_router_w"], "rb": a["L0_ffn_router_b"],
        "weights": np.concatenate([w1.reshape(QUARTERS, P, EXPERTS, -1), w2.reshape(QUARTERS, P, EXPERTS, -1)], axis=3),
        "b1": a["L0_ffn_b1"].reshape(EXPERTS, 2, QUARTERS, KH, P).transpose(4, 2, 0, 1, 3).reshape(P, -1),
        "b2": a["L0_ffn_b2"].reshape(-1),
        "const": CONSTANTS,
        "ones": np.ones((STACK - SPLIT, HEADS * CHUNK), mybir.dt.np(BF16)),
    }
    nc = _bacc.Bacc("TRN2", target_bir_lowering=False, num_devices=1)
    feeds, args = {}, []
    for name, value in arrays.items():
        value = np.ascontiguousarray(value)
        feeds[f"in_{name}_dram"] = value
        args.append(nc.dram_tensor(f"in_{name}_dram", value.shape, mybir.dt.from_np(value.dtype), kind="ExternalInput").ap())
    args.append(nc.dram_tensor("out_dram", (TOKENS + P * SLOT_TILES, DIM), F32, kind="ExternalOutput").ap())
    args.append(nc.dram_tensor("q_parts", (CHUNKS, DIM, 3, CHUNK), BF16).ap())
    args.append(nc.dram_tensor("k_parts", (DIM, 3, BATCH * CTX_PAD), BF16).ap())
    args.append(nc.dram_tensor("d_parts", (BATCH, 3, CTX), BF16).ap())
    args.append(nc.dram_tensor("rows", (TOKENS + P, 2 * DIM), F32).ap())
    build(nc, *args)
    r = _run(nc, [feeds], core_ids=[0])
    return r.results[0]["out_dram"][:TOKENS].reshape(BATCH, SEQ, DIM)
```

```python
from contextlib import ExitStack

import numpy as np

import concourse.bass as bass
from concourse import mybir

ALU = mybir.AluOpType
ACT = mybir.ActivationFunctionType
AX_X = mybir.AxisListType.X
F32 = mybir.dt.float32
BF16 = mybir.dt.bfloat16
I32 = mybir.dt.int32
U32 = mybir.dt.uint32

P = 128
BATCH, SEQ, DIM = 2, 1024, 256
HEADS, HDIM = 16, 16
CTX = 154
CTX_PAD = 160
HEAD_ROWS = 128
REST = CTX - HEAD_ROWS
EXPERTS, HIDDEN = 8, 1024
EPS = 1e-5
SCALE = HDIM ** -0.5

TOKENS = BATCH * SEQ
TILES = TOKENS // P
CHUNK = 512
CHUNKS = TOKENS // CHUNK
TPC = CHUNK // P
KD = DIM // P
GROUPS = HEADS // 4
SLOT_TILES = TOKENS // P + EXPERTS - 1
QUARTERS = 4
HQ = HIDDEN // QUARTERS
KH = HQ // P
HIDDEN_BLOCKS = 2 * KH
BANK = 512

Q_PARTS = (0, 0, 1, 1, 0, 2)
K_PARTS = (0, 1, 0, 1, 2, 0)
SPLIT = len(Q_PARTS) * HDIM
STACK = SPLIT + 3
STACK_T = STACK + 3
HEADS_PER_BANK = BANK // CTX
SCORE_BANKS = -(-HEADS // HEADS_PER_BANK)
UNITS_PER_GROUP = 5
UNITS = GROUPS * UNITS_PER_GROUP
EXPERT_W = KD * 2 * HQ + KH * DIM
EARLY_EXPERTS = 2
MAX_AT = 0
UNIT_AT = 5
OUT_PERIOD = 4
TURN_O, NORMALISE, TURN_ON, COPY_ON, PROJECT, RESIDUAL, NORM2, TURN_X2, COPY_X2, ROUTE, LOGITS = 2, 3, 4, 5, 5, 6, 8, 10, 11, 12, 13
Q_AT = {2: (-1, 17), 3: (0, 18)}
PROBS = 6
WARM_UPS = 20
GATHERS = 4
RING = 3


def constants():
    p = np.arange(P)
    parts = {
        "ident": np.eye(P),
        "upper": (p[:, None] < p[None, :]) * 1.0,
        "slot_in_tile": np.tile(p, (P, 1)),
        "first_expert": np.tile(EXPERTS - np.arange(EXPERTS), (P, 1)),
        "tile_starts": np.tile(np.arange(TILES) * P, (P, 1)),
        "slot_tile": np.tile(np.arange(SLOT_TILES), (P, 1)),
        "tile_of_token": np.tile(np.arange(TILES), (P, 1)),
        "row": p[:, None],
        "one8": np.ones((P, EXPERTS)),
        "spare_row": TOKENS + np.stack([np.tile(p[:, None], (1, SLOT_TILES)),
                                        P * np.arange(SLOT_TILES)[None, :] + p[:, None]], axis=1).reshape(P, -1),
        "carry": np.tile((np.arange(EXPERTS * TILES) % TILES > 0) * 1.0, (P, 1)),
        "rest_rows": ((p[:, None] // 32 == np.arange(4)[None, :]) & (p[:, None] % 32 < REST)) * 1.0,
    }
    at, spans = 0, {}
    for name, a in parts.items():
        spans[name] = (at, at + a.shape[1])
        at += a.shape[1]
    return np.concatenate([np.asarray(a, np.float32) for a in parts.values()], axis=1), spans


CONSTANTS, SPANS = constants()


def build(nc, x, ctx_t, tau, delta, wq, bq, wk, bk, wv, bv, wo, bo, rw, rb, weights, b1, b2, const, ones, minus_ones, out,
          q_parts, k_parts, d_parts, rows):
    ctx = ExitStack()
    early = ExitStack()
    with ctx:
        def sb(name, shape, dt=F32, stack=ctx):
            return stack.enter_context(nc.sbuf_tensor(name, shape, dt))

        def bank(name):
            return ctx.enter_context(nc.psum_tensor(name, [P, BANK], F32))

        def sem(name):
            return ctx.enter_context(nc.semaphore(name))

        consts = sb("consts", [P, CONSTANTS.shape[1]])
        slot_row = sb("slot_row", [P, 2, SLOT_TILES], U32)
        tile_expert = sb("tile_expert", [1, SLOT_TILES], I32)

        def const_of(name):
            return consts[:, SPANS[name][0]:SPANS[name][1]]

        ident = const_of("ident")
        ident_b = sb("ident_b", [P, P], BF16)[:, :]

        b1_sb = sb("b1_sb", [P, QUARTERS * EXPERTS, HIDDEN_BLOCKS])

        sb("first_experts", [P, EARLY_EXPERTS * EXPERT_W], stack=early)
        q_stack = sb("q_stack", [P, 3, HEADS, CHUNK], BF16, early)
        xn = sb("xn", [P, 2, TPC, DIM], stack=early)
        xn_t = sb("xn_t", [P, KD, CHUNK], stack=early)
        q_split = sb("q_split", [P, KD, 3, CHUNK], BF16, early)
        q_rest = sb("q_rest", [P, KD, CHUNK], stack=early)
        k_stack = sb("k_stack", [P, BATCH, HEADS, CTX_PAD], BF16, early)
        wq_sb = sb("wq_sb", [P, KD, DIM], stack=early)
        wk_sb = sb("wk_sb", [P, KD, DIM], stack=early)
        wv_sb = sb("wv_sb", [P, KD, DIM], stack=early)
        row_max = sb("row_max", [P, 2, TPC, HEADS], stack=early)
        max_rest = sb("max_rest", [P, TPC, HEADS], stack=early)
        max_split = sb("max_split", [P, TPC, 3, HEADS], BF16, early)
        max_t = sb("max_t", [P, 2, CHUNK], BF16, early)
        v_main = sb("v_main", [P, BATCH, HEADS, 32], stack=early)
        v_rest = sb("v_rest", [P, BATCH, GROUPS, 4, 32], stack=early)
        probs = sb("probs", [P, PROBS, CHUNK], stack=early)
        x_sb = sb("x_sb", [P, TILES, DIM], stack=early)
        attn_t = sb("attn_t", [P, 2, GROUPS, CHUNK], stack=early)
        inverse = sb("inverse", [P, TPC, HEADS], stack=early)
        attn = sb("attn", [P, TPC, DIM], stack=early)
        attn_nt = sb("attn_nt", [P, TPC, KD, P], stack=early)
        row_buf = sb("row_buf", [P, TPC, 2 * DIM], stack=early)
        x2n_t = sb("x2n_t", [P, TPC, KD, P], stack=early)
        bo_sb = sb("bo_sb", [P, DIM], stack=early)
        wo_sb = sb("wo_sb", [P, KD, DIM], stack=early)
        rw_sb = sb("rw_sb", [P, KD, EXPERTS], stack=early)
        rb_sb = sb("rb_sb", [P, EXPERTS], stack=early)
        bq_sb = sb("bq_sb", [P, KD], stack=early)
        bk_sb = sb("bk_sb", [P, KD], stack=early)
        bv_sb = sb("bv_sb", [P, DIM], stack=early)
        tau_sb = sb("tau_sb", [P, BATCH], stack=early)
        stats1 = sb("stats1", [P, TILES, 6], stack=early)
        mv1 = sb("mv1", [P, TILES, 2], stack=early)
        var1 = sb("var1", [P, TILES], stack=early)
        rstd1 = sb("rstd1", [P, TILES], stack=early)
        stats2 = sb("stats2", [P, TILES, 6], stack=early)
        mv2 = sb("mv2", [P, TILES, 2], stack=early)
        var2 = sb("var2", [P, TILES], stack=early)
        rstd2 = sb("rstd2", [P, TILES], stack=early)
        warm = sb("warm", [P, CHUNK], BF16, early)
        minus_half = sb("minus_half", [P, TPC], stack=early)
        logits = sb("logits", [P, TILES, EXPERTS], stack=early)
        upper_b = sb("upper_b", [P, P], BF16, early)
        lanes_b = sb("lanes_b", [P, P], BF16, early)
        ones_b = sb("ones_b", [P, P], BF16, early)
        setup = early.enter_context(ExitStack())
        v_tmp = sb("v_tmp", [P, BATCH, 2, DIM], stack=setup)
        ctx_sb = sb("ctx_sb", [P, KD, BATCH, CTX_PAD], stack=setup)
        k_full = sb("k_full", [P, BATCH, KD, CTX_PAD], stack=setup)
        k_rest = sb("k_rest", [P, BATCH, KD, CTX_PAD], stack=setup)
        k_split = sb("k_split", [P, BATCH, KD, 3, CTX_PAD], BF16, setup)
        delta_sb = sb("delta_sb", [BATCH, CTX], stack=setup)
        delta_rest = sb("delta_rest", [BATCH, CTX], stack=setup)
        delta_split = sb("delta_split", [BATCH, 3, CTX], BF16, setup)
        setup.close()
        best = sb("best", [P, TILES], stack=early)
        key = sb("key", [P, TILES, EXPERTS], stack=early)
        onehot = sb("onehot", [P, TILES, EXPERTS], stack=early)
        onehot_b = sb("onehot_b", [P, TILES, EXPERTS], BF16, early)
        counts = sb("counts", [P, EXPERTS, TILES], stack=early)
        upto = sb("upto", [P, EXPERTS, TILES], stack=early)
        over = sb("over", [P, EXPERTS, TILES], stack=early)
        n_tiles = sb("n_tiles", [P, EXPERTS], stack=early)
        last_tile = sb("last_tile", [P, EXPERTS], stack=early)
        start_slot = sb("start_slot", [P, EXPERTS], stack=early)
        place = sb("place", [P, TILES, EXPERTS], stack=early)
        slot = sb("slot", [P, TILES], stack=early)
        slot_tile_of = sb("slot_tile_of", [P, TILES], stack=early)
        slot_lane = sb("slot_lane", [P, TILES], stack=early)
        passed = sb("passed", [P, TILES, SLOT_TILES], stack=early)
        lane_hot = sb("lane_hot", [P, TILES, P], BF16, early)
        tile_hot = sb("tile_hot", [P, TILES, 3, SLOT_TILES], BF16, early)
        slot_info = sb("slot_info", [P, 3, SLOT_TILES], stack=early)
        row_f = sb("row_f", [P, 2, SLOT_TILES], stack=early)
        unused = sb("unused", [P, SLOT_TILES], stack=early)
        spare = sb("spare", [P, 2, SLOT_TILES], stack=early)
        ended = sb("ended", [P, SLOT_TILES, EXPERTS], stack=early)
        expert_f = sb("expert_f", [P, SLOT_TILES], stack=early)
        early.close()

        w_sb = sb("w_sb", [P, 2 * EXPERTS, EXPERT_W])
        b2_sb = sb("b2_sb", [P, EXPERTS, DIM])
        slot_in = sb("slot_in", [P, GATHERS, 2 * DIM])
        w1_now = sb("w1_now", [P, RING, KD, 2 * HQ])
        hidden = sb("hidden", [P, RING, HIDDEN_BLOCKS, P])
        gate = sb("gate", [P, RING, KH, P])
        act_ut = sb("act_ut", [P, RING, KH, P])
        y_acc = sb("y_acc", [P, SLOT_TILES, DIM])
        slot_xt = sb("slot_xt", [P, SLOT_TILES, KD, P])

        banks = [bank(f"bank{n}") for n in range(8)]
        score_ps, st_ps, o_ps, work_ps = banks[0:2], banks[2:4], banks[4:6], banks[6:8]
        h_ps, y_ps, xin_ps = banks[0:3], banks[3:6], banks[6:8]

        s_consts = sem("s_consts")
        s_x = [sem(f"s_x{c}") for c in range(CHUNKS)]
        s_q_weights = sem("s_q_weights")
        s_k_inputs = sem("s_k_inputs")
        s_v_inputs = sem("s_v_inputs")
        s_out_weights = sem("s_out_weights")
        s_delta = sem("s_delta")
        s_biases = sem("s_biases")
        s_quarter = [sem(f"s_quarter{q}") for q in range(QUARTERS)]
        quarter_ready = sem("quarter_ready")
        k_stored = [sem(f"k_stored{b}") for b in range(BATCH)]
        d_stored = sem("d_stored")
        ones_loaded = sem("ones_loaded")
        k_loaded = [sem(f"k_loaded{b}") for b in range(BATCH)]
        q_stored = sem("q_stored")
        q_loaded = [sem(f"q_loaded{c}") for c in range(CHUNKS)]
        rows_stored = [sem(f"rows_stored{n}") for n in range(TPC)]
        zeros_stored = sem("zeros_stored")
        gathered = [sem(f"gathered{n}") for n in range(GATHERS)]
        s_out = sem("s_out")
        warm_ready = sem("warm_ready")
        pool_ready = sem("pool_ready")
        dve_step = sem("dve_step")
        pool_step = sem("pool_step")
        k_ready = sem("k_ready")
        k_split_done = sem("k_split_done")
        d_split_done = sem("d_split_done")
        v_ready = sem("v_ready")
        v_copied = sem("v_copied")
        v_biased = sem("v_biased")
        v_done = sem("v_done")
        ident_ready = sem("ident_ready")
        ln1_stats = sem("ln1_stats")
        ln1_done = sem("ln1_done")
        xt_ready = sem("xt_ready")
        xt_copied = sem("xt_copied")
        q_ready = sem("q_ready")
        rstd1_done = sem("rstd1_done")
        rstd2_done = sem("rstd2_done")
        x_biased = sem("x_biased")
        o_copied = sem("o_copied")
        on_ready = sem("on_ready")
        o_turned = sem("o_turned")
        on_turned = sem("on_turned")
        on_copied = sem("on_copied")
        q_high = sem("q_high")
        q_rest_done = sem("q_rest_done")
        q_low = sem("q_low")
        score_ready = sem("score_ready")
        max_done = sem("max_done")
        max_parts = sem("max_parts")
        mt_ready = sem("mt_ready")
        mt_copied = sem("mt_copied")
        max_loaded = sem("max_loaded")
        st_ready = sem("st_ready")
        probs_ready = sem("probs_ready")
        pv_done = sem("pv_done")
        proj_ready = sem("proj_ready")
        x2_done = sem("x2_done")
        ln2_stats = sem("ln2_stats")
        ln2_done = sem("ln2_done")
        x2t_ready = sem("x2t_ready")
        x2t_copied = sem("x2t_copied")
        logits_ready = sem("logits_ready")
        logits_done = sem("logits_done")
        onehot_done = sem("onehot_done")
        count_ready = sem("count_ready")
        hots_done = sem("hots_done")
        info_ready = sem("info_ready")
        routed = sem("routed")
        xin_ready = sem("xin_ready")
        xin_copied = sem("xin_copied")
        y_started = sem("y_started")
        h_ready = sem("h_ready")
        biased = sem("biased")
        gate_ready = sem("gate_ready")
        u_ready = sem("u_ready")
        w1_moved = sem("w1_moved")
        y_ready = sem("y_ready")
        y_added = sem("y_added")

        block = ctx.enter_context(nc.Block())

        def stack_slot(c):
            return (c + 2) % 3

        def out_ps(t):
            n = t % TPC if t >= TILES - TPC else 0
            return (work_ps, score_ps, st_ps, o_ps)[n]

        def slot_used(sem_of, engine, n, j):
            if j < RING:
                back = j + SLOT_TILES - max(i for i in range(SLOT_TILES) if i % RING == j)
            else:
                back = RING
            if not isinstance(n, int) or n >= back:
                engine.wait_ge(sem_of, n - back + 1)

        STEPS = SCORE_BANKS * TPC
        SCHEDULE = [(c, i) for c in range(-1, CHUNKS) for i in range(STEPS)] + [(CHUNKS, 0), (CHUNKS, 1)]

        def due(c, i, step):
            chunk, n = divmod(STEPS * (c - 1) + i - step, STEPS)
            return [TPC * chunk + n // OUT_PERIOD] if 0 <= chunk < CHUNKS - 1 and n in range(0, TPC * OUT_PERIOD, OUT_PERIOD) else []

        def score_bank(c, i):
            return (score_ps + st_ps)[i % 4] if c == 0 else score_ps[i % 2]

        def unit_due(c, i, lag):
            chunk, unit = divmod(STEPS * c + i - UNIT_AT - lag, STEPS)
            return [(chunk, unit)] if 0 <= chunk < CHUNKS and unit < UNITS else []

        def q_due(c, i, step):
            return [chunk for chunk, at in Q_AT.items() if (c, i) == (at[0], at[1] + step)]

        @block.sync
        def _(sp):
            sp.dma_start(x_sb[:, 0:TPC, :], x[0:CHUNK, :].rearrange("(t p) d -> p t d", p=P)).then_inc(s_x[0], 16)
            sp.dma_start(consts[:, :], const).then_inc(s_consts, 16)
            sp.dma_start(wq_sb[:, :, :], wq.rearrange("(k p) n -> p k n", p=P)).then_inc(s_q_weights, 16)
            sp.dma_start(bq_sb[:, :], bq).then_inc(s_q_weights, 16)
            for dst, src in ((ctx_sb[:, :, :, :].rearrange("p k b s -> p (k b) s"), ctx_t),
                             (wk_sb[:, :, :], wk.rearrange("(k p) n -> p k n", p=P)),
                             (bk_sb[:, :], bk),
                             (tau_sb[:, :], tau.rearrange("(o b) -> o b", o=1).to_broadcast([P, BATCH]))):
                sp.dma_start(dst, src).then_inc(s_k_inputs, 16)
            sp.dma_start(delta_sb[:, :], delta).then_inc(s_delta, 16)
            sp.dma_start(wv_sb[:, :, :], wv.rearrange("(k p) n -> p k n", p=P)).then_inc(s_v_inputs, 16)
            sp.dma_start(bv_sb[:, :], bv.rearrange("(o n) -> o n", o=1).to_broadcast([P, DIM])).then_inc(s_v_inputs, 16)
            for c in range(1, CHUNKS):
                sp.dma_start(x_sb[:, TPC * c:TPC * (c + 1), :],
                             x[CHUNK * c:CHUNK * (c + 1), :].rearrange("(t p) d -> p t d", p=P)).then_inc(s_x[c], 16)
            sp.dma_start(wo_sb[:, :, :], wo.rearrange("(k p) n -> p k n", p=P)).then_inc(s_out_weights, 16)
            sp.dma_start(bo_sb[:, :], bo.rearrange("(o n) -> o n", o=1).to_broadcast([P, DIM])).then_inc(s_out_weights, 16)
            sp.dma_start(rw_sb[:, :, :], rw.rearrange("(k p) n -> p k n", p=P)).then_inc(s_out_weights, 16)
            sp.dma_start(rb_sb[:, :], rb.rearrange("(o n) -> o n", o=1).to_broadcast([P, EXPERTS])).then_inc(s_out_weights, 16)
            sp.dma_start(b1_sb[:, :, :], b1.rearrange("p (e m) -> p e m", m=HIDDEN_BLOCKS)).then_inc(s_biases, 16)
            for n in range(3):
                sp.dma_start(q_stack[SPLIT:STACK, n, :, :].rearrange("p h s -> p (h s)"), ones).then_inc(ones_loaded, 16)
            sp.dma_start(k_stack[STACK:STACK_T, :, :, :].rearrange("p b h s -> p (b h s)"),
                         minus_ones).then_inc(ones_loaded, 16)
            sp.wait_ge(pool_ready, 1)
            sp.dma_start(rows[TOKENS:TOKENS + P, :], row_buf[:, 0, :]).then_inc(zeros_stored, 16)
            def store_q(c):
                sp.wait_ge(q_low, c + 1)
                sp.dma_start(q_parts[c].rearrange("(m p) w s -> p m (w s)", p=P),
                             q_split[:, :, :, :].rearrange("p m w s -> p m (w s)")).then_inc(q_stored, 16)

            def load_q(c):
                sp.wait_ge(q_stored, 16 * (c + 1))
                if c >= 3:
                    sp.wait_ge(st_ready, UNITS * (c - 2))
                for n, part in enumerate(Q_PARTS):
                    src = q_parts[c][:, part, :].rearrange("(h d) s -> d h s", d=HDIM)
                    sp.dma_start(q_stack[HDIM * n:HDIM * (n + 1), stack_slot(c), :, :], src).then_inc(q_loaded[c], 16)

            def store_k(b):
                sp.wait_ge(k_split_done, b + 1)
                sp.dma_start(k_parts[b].rearrange("(m p) w s -> p m (w s)", p=P),
                             k_split[:, b, :, :, :].rearrange("p m w s -> p m (w s)")).then_inc(k_stored[b], 16)

            def load_k(b):
                src = d_parts[b].rearrange("w (o s) -> w o s", o=1).to_broadcast([3, HEADS, CTX])
                sp.dma_start(k_stack[SPLIT:STACK, b, :, 0:CTX], src).then_inc(k_loaded[b], 16)
                sp.wait_ge(k_stored[b], 16)
                for n, part in enumerate(K_PARTS):
                    src = k_parts[b][:, part, 0:CTX].rearrange("(h d) s -> d h s", d=HDIM)
                    sp.dma_start(k_stack[HDIM * n:HDIM * (n + 1), b, :, 0:CTX], src).then_inc(k_loaded[b], 16)

            def store_rows(t):
                sp.wait_ge(ln2_done, t + 1)
                sp.dma_start(rows[P * t:P * (t + 1), :], row_buf[:, t % TPC, :]).then_inc(rows_stored[t % TPC], 16)

            def load_experts(q, first, last):
                for e in range(first, last):
                    sp.dma_start(w_sb[:, (q % 2) * EXPERTS + e, :], weights[q, :, e, :]).then_inc(s_quarter[q], 16)

            store_q(0)
            sp.wait_ge(d_split_done, 1)
            sp.dma_start(d_parts.rearrange("b w s -> b (w s)"),
                         delta_split[:, :, :].rearrange("b w s -> b (w s)")).then_inc(d_stored, 16)
            store_k(0)
            load_q(0)
            sp.wait_ge(d_stored, 16)
            sp.wait_ge(pool_ready, 3)
            load_k(0)
            store_q(1)
            load_q(1)
            store_k(1)
            load_k(1)
            for c in range(-1, CHUNKS):
                for chunk, at in Q_AT.items():
                    if at[0] == c:
                        store_q(chunk)
                        load_q(chunk)
                if c == -1:
                    load_experts(0, 0, EARLY_EXPERTS)
                if c == CHUNKS - 1:
                    sp.wait_ge(st_ready, UNITS * c)
                    sp.wait_ge(max_loaded, 16 * CHUNKS)
                    load_experts(0, EARLY_EXPERTS, EXPERTS - 1)
                if c >= 1:
                    for t in range(TPC):
                        store_rows(TPC * (c - 1) + t)
            sp.wait_ge(st_ready, UNITS * CHUNKS)
            load_experts(0, EXPERTS - 1, EXPERTS)
            for t in range(TILES - TPC, TILES):
                store_rows(t)
            sp.wait_ge(pv_done, UNITS * CHUNKS)
            sp.dma_start(b2_sb[:, :, :].rearrange("p e n -> p (e n)"),
                         b2.rearrange("(o n) -> o n", o=1).to_broadcast([P, EXPERTS * DIM])).then_inc(s_biases, 16)
            for q in range(QUARTERS):
                if q == 1:
                    for e in range(EXPERTS):
                        sp.wait_ge(xin_ready, 2 * e + 2)
                        load_experts(q, e, e + 1)
                if q >= 2:
                    sp.wait_ge(y_ready, SLOT_TILES * (q - 1))
                    load_experts(q, 0, EXPERTS)
                sp.wait_ge(s_quarter[q], 16 * EXPERTS)
                sp.sem_inc(quarter_ready, 1)
            sp.sem_inc(quarter_ready, 1)

        @block.gpsimd
        def _(pool):
            pool.memset(row_buf[:, 0, :], 0.0).then_inc(pool_ready, 1)
            pool.memset(minus_half[:, :], -0.5).then_inc(pool_ready, 1)
            pool.memset(k_stack[0:STACK, :, :, CTX:CTX_PAD], 0.0).then_inc(pool_ready, 1)
            pool.memset(v_main[:, :, :, :], 0.0).then_inc(pool_ready, 1)
            pool.memset(v_rest[:, :, :, :, :], 0.0).then_inc(pool_ready, 1)

            def power(var, rstd, mv, t0, n, signal):
                pool.tensor_scalar(var[:, t0:t0 + n], mv[:, t0:t0 + n, 1], EPS, None, ALU.add).then_inc(pool_step, 1)
                count[0] += 1
                pool.wait_ge(pool_step, count[0])
                pool.tensor_tensor(rstd[:, t0:t0 + n], var[:, t0:t0 + n], minus_half[:, 0:n],
                                   ALU.pow).then_inc(signal, 1)

            count = [0]

            def power1(c):
                pool.wait_ge(ln1_stats, c + 1)
                if c == 0:
                    pool.wait_ge(pool_ready, 2)
                power(var1, rstd1, mv1, TPC * c, TPC, rstd1_done)

            def add_bo(c):
                pool.wait_ge(ln1_done, c + 1)
                if c == 0:
                    pool.wait_ge(s_out_weights, 64)
                at = x_sb[:, TPC * c:TPC * (c + 1), :]
                pool.tensor_tensor(at, at, bo_sb[:, :].rearrange("p (o n) -> p o n", o=1).to_broadcast([P, TPC, DIM]),
                                   ALU.add).then_inc(x_biased, 1)

            def power2(t):
                pool.wait_ge(ln2_stats, t + 1)
                power(var2, rstd2, mv2, t, 1, rstd2_done)

            power1(0)
            power1(1)
            pool.wait_ge(s_v_inputs, 32)
            pool.wait_ge(s_consts, 16)
            pool.wait_ge(pool_ready, 5)
            mask = const_of("rest_rows")
            wide = mask.rearrange("p (o j q) -> p o j q", o=1, q=1).to_broadcast([P, GROUPS, 4, HDIM])
            for b in range(BATCH):
                pool.wait_ge(v_copied, 2 * b + 1)
                pool.tensor_tensor(v_main[:, b, :, 0:HDIM], v_tmp[:, b, 0, :].rearrange("p (h d) -> p h d", d=HDIM),
                                   bv_sb[:, :].rearrange("p (h d) -> p h d", d=HDIM), ALU.add).then_inc(v_done, 1)
                pool.wait_ge(v_copied, 2 * b + 2)
                pool.tensor_tensor(v_tmp[:, b, 1, :], v_tmp[:, b, 1, :], bv_sb[:, :], ALU.add).then_inc(v_biased, 1)
                pool.wait_ge(v_biased, b + 1)
                pool.tensor_tensor(v_rest[:, b, :, :, 0:HDIM],
                                   v_tmp[:, b, 1, :].rearrange("p (g j d) -> p g j d", g=GROUPS, j=4), wide,
                                   ALU.mult).then_inc(v_done, 1)
                pool.tensor_copy(v_rest[:, b, :, :, HDIM],
                                 mask.rearrange("p (o j) -> p o j", o=1).to_broadcast([P, GROUPS, 4])).then_inc(v_done, 1)
            pool.memset(v_main[:, :, :, HDIM:HDIM + 1], 1.0).then_inc(v_done, 1)
            power1(2)
            for c, i in SCHEDULE:
                for t in due(c, i, RESIDUAL):
                    power2(t)
                if c == 0 and i == 8:
                    power1(3)
                if c == -1 and i == 12:
                    add_bo(0)
                    add_bo(1)
                if c == 0 and i == 12:
                    add_bo(2)
                    add_bo(3)
            for t in range(TILES - TPC, TILES):
                power2(t)

            pool.wait_ge(routed, 2)
            pool.wait_ge(zeros_stored, 16)
            for n in range(TPC):
                pool.wait_ge(rows_stored[n], 16 * CHUNKS)

            def gather(j):
                if j >= GATHERS:
                    pool.wait_ge(xin_ready, j - GATHERS + 1)
                    pool.wait_ge(y_started, j - GATHERS + 1)
                pool.indirect_dma_start(slot_in[:, j % GATHERS, :], None, rows,
                                        bass.IndirectOffsetOnAxis(slot_row[:, 0, j:j + 1], 0)).then_inc(gathered[j % GATHERS], 16)

            for j in range(GATHERS):
                gather(j)
            pool.wait_ge(s_biases, 32)
            for j in range(SLOT_TILES):
                expert = pool.value_load(tile_expert[0:1, j:j + 1], min_val=0, max_val=EXPERTS - 1)
                pool.wait_ge(gathered[j % GATHERS], 16 * (j // GATHERS + 1))
                pool.tensor_tensor(y_acc[:, j, :], slot_in[:, j % GATHERS, DIM:2 * DIM],
                                   b2_sb[:, bass.ds(expert, 1), :].rearrange("p o n -> p (o n)"),
                                   ALU.add).then_inc(y_started, 1)
                if j + GATHERS < SLOT_TILES:
                    gather(j + GATHERS)
            for j in range(SLOT_TILES):
                pool.wait_ge(y_added, SLOT_TILES * (QUARTERS - 1) + j + 1)
                pool.indirect_dma_start(out, bass.IndirectOffsetOnAxis(slot_row[:, 1, j:j + 1], 0), y_acc[:, j, :],
                                        None).then_inc(s_out, 16)
            pool.wait_ge(s_out, 16 * SLOT_TILES)

        @block.tensor
        def _(pe):
            pe.wait_ge(warm_ready, 1)
            for _ in range(WARM_UPS):
                pe.matmul(st_ps[0][:, :], warm[:, 0:P], warm[:, :], start=True, stop=True)
            pe.wait_ge(s_consts, 16)
            def turn_x(c):
                pe.wait_ge(ln1_done, c + 1)
                if c >= 1:
                    pe.wait_ge(q_rest_done, KD * c)
                if c == 3:
                    pe.wait_ge(mt_copied, 1)
                for k in range(KD):
                    for t in range(TPC):
                        ins = pe.transpose(work_ps[k][:, P * t:P * (t + 1)], xn[:, c % 2, t, P * k:P * (k + 1)], ident)
                    ins.then_inc(xt_ready, 1)

            def project_q(c):
                pe.wait_ge(xt_copied, KD * (c + 1))
                if c == 0:
                    pe.wait_ge(s_q_weights, 32)
                for m in range(KD):
                    for k in range(KD):
                        ins = pe.matmul(work_ps[m][:, :], wq_sb[:, k, P * m:P * (m + 1)], xn_t[:, k, :],
                                        start=(k == 0), stop=(k == KD - 1))
                    ins.then_inc(q_ready, 1)

            def scores(c, i):
                n = STEPS * c + i
                if n == 0:
                    pe.wait_ge(pool_ready, 5)
                    pe.wait_ge(ones_loaded, 64)
                    pe.wait_ge(k_split_done, 1)
                if i == 0 and c in (0, 2):
                    pe.wait_ge(k_loaded[c // 2], 16 * (len(K_PARTS) + 1))
                if i == 0:
                    pe.wait_ge(q_loaded[c], 16 * len(Q_PARTS))
                if n == 2:
                    pe.wait_ge(v_copied, 2 * BATCH)
                if c == 0 and n >= 4:
                    pe.wait_ge(max_done, n - 3)
                if c > 0:
                    pe.wait_ge(max_done, n - 1)
                t, first = i // SCORE_BANKS, HEADS_PER_BANK * (i % SCORE_BANKS)
                for h in range(first, min(first + HEADS_PER_BANK, HEADS)):
                    at = CTX * (h - first)
                    ins = pe.matmul(score_bank(c, i)[:, at:at + CTX], q_stack[0:STACK, stack_slot(c), h, P * t:P * (t + 1)],
                                    k_stack[0:STACK, c // 2, h, 0:CTX], start=True, stop=True)
                ins.then_inc(score_ready, 1)

            def turn_max(c):
                pe.wait_ge(max_parts, c + 1)
                pe.wait_ge(ident_ready, 1)
                if c >= 2:
                    pe.wait_ge(x2t_copied, TPC * (c - 1))
                pe.wait_ge(q_rest_done, KD * (CHUNKS if c >= 1 else 3))
                turned = work_ps[1][0:3 * HEADS, 0:CHUNK // 2].bitcast(BF16)
                for t in range(TPC):
                    ins = pe.transpose(turned[:, P * t:P * (t + 1)],
                                       max_split[:, t, :, :].rearrange("p w h -> p (w h)"), ident_b)
                ins.then_inc(mt_ready, 1)

            def scores_t(c, u):
                n = UNITS * c + u
                if n == 0:
                    pe.wait_ge(v_done, 3 * BATCH + 1)
                if u == 0:
                    pe.wait_ge(max_loaded, 16 * (c + 1))
                if n >= 2:
                    pe.wait_ge(probs_ready, n - 1)
                g, j = u // UNITS_PER_GROUP, u % UNITS_PER_GROUP - 1
                if j < 0:
                    for j in range(4):
                        ins = pe.matmul(st_ps[n % 2][32 * j:32 * j + 32, :],
                                        k_stack[0:STACK_T, c // 2, 4 * g + j, HEAD_ROWS:CTX_PAD],
                                        q_stack[0:STACK_T, stack_slot(c), 4 * g + j, :], start=True, stop=True)
                else:
                    ins = pe.matmul(st_ps[n % 2][:, :], k_stack[0:STACK_T, c // 2, 4 * g + j, 0:HEAD_ROWS],
                                    q_stack[0:STACK_T, stack_slot(c), 4 * g + j, :], start=True, stop=True)
                ins.then_inc(st_ready, 1)

            def values_rest(c, g):
                group = GROUPS * c + g
                pe.wait_ge(probs_ready, UNITS_PER_GROUP * group + 1)
                if group >= 2:
                    pe.wait_ge(o_copied, group - 1)
                pe.matmul(o_ps[group % 2][:, :], v_rest[:, c // 2, g, :, :].rearrange("p j n -> p (j n)"),
                          probs[:, UNITS_PER_GROUP * group % PROBS, :], start=True, stop=False,
                          skip_group_check=True).then_inc(pv_done, 1)

            def values(c, g):
                group = GROUPS * c + g
                n = UNITS_PER_GROUP * group + 1
                pe.wait_ge(probs_ready, n + 4)
                for j in range(4):
                    pe.matmul(o_ps[group % 2][32 * j:32 * j + 32, :], v_main[:, c // 2, 4 * g + j, :],
                              probs[:, (n + j) % PROBS, :], start=False, stop=True,
                              skip_group_check=True).then_inc(pv_done, 1)

            def turn_o(t):
                c = t // TPC
                pe.wait_ge(o_copied, GROUPS * (c + 1))
                if t > 0 and t % TPC == 0:
                    pe.wait_ge(logits_done, t)
                elif t > 0 and c < CHUNKS - 1:
                    pe.wait_ge(x2_done, t)
                if c == CHUNKS - 1:
                    pe.wait_ge(max_done, STEPS * CHUNKS)
                    pe.wait_ge(probs_ready, UNITS * CHUNKS)
                pe.wait_ge(q_rest_done, KD * CHUNKS)
                for g in range(GROUPS):
                    ins = pe.transpose(out_ps(t)[0][:, P * g:P * (g + 1)],
                                       attn_t[:, c % 2, g, P * (t % TPC):P * (t % TPC + 1)], ident)
                ins.then_inc(o_turned, 1)

            def turn_on(t):
                pe.wait_ge(on_ready, t + 1)
                if t > 0 and t % TPC == 0:
                    pe.wait_ge(x2t_copied, t)
                elif t % TPC >= 2 and t < TILES - TPC:
                    pe.wait_ge(x2t_copied, t - 1)
                pe.wait_ge(mt_copied, min(t // TPC + 2, CHUNKS))
                for k in range(KD):
                    ins = pe.transpose(out_ps(t)[1][:, P * k:P * (k + 1)], attn[:, t % TPC, P * k:P * (k + 1)], ident)
                ins.then_inc(on_turned, 1)

            def project_out(t):
                pe.wait_ge(on_copied, t + 1)
                if t % TPC >= 2 and t < TILES - TPC:
                    pe.wait_ge(logits_done, t - 1)
                if t == 0:
                    pe.wait_ge(s_out_weights, 64)
                for k in range(KD):
                    ins = pe.matmul(out_ps(t)[0][:, 0:DIM], attn_nt[:, t % TPC, k, :], wo_sb[:, k, :],
                                    start=(k == 0), stop=(k == KD - 1))
                ins.then_inc(proj_ready, 1)

            def turn_x2(t):
                pe.wait_ge(ln2_done, t + 1)
                if t % TPC < TPC - 1 and t < TILES - TPC:
                    pe.wait_ge(on_copied, t + 2)
                for k in range(KD):
                    ins = pe.transpose(out_ps(t)[1][:, P * k:P * (k + 1)], row_buf[:, t % TPC, P * k:P * (k + 1)], ident)
                ins.then_inc(x2t_ready, 1)

            def route(t):
                pe.wait_ge(x2t_copied, t + 1)
                if t % TPC < TPC - 2 and t < TILES - TPC:
                    pe.wait_ge(on_ready, t + 3)
                elif t < TILES - TPC:
                    pe.wait_ge(x2_done, TPC * (t // TPC + 1))
                    pe.wait_ge(logits_done, t)
                else:
                    pe.wait_ge(x2_done, t + 1)
                for k in range(KD):
                    ins = pe.matmul(out_ps(t)[0][:, 0:EXPERTS], x2n_t[:, t % TPC, k, :], rw_sb[:, k, :],
                                    start=(k == 0), stop=(k == KD - 1))
                ins.then_inc(logits_ready, 1)

            turn_x(0)
            project_q(0)
            pe.wait_ge(s_k_inputs, 64)
            for b, ps in enumerate((score_ps, o_ps)):
                for m in range(KD):
                    for k in range(KD):
                        ins = pe.matmul(ps[m][:, 0:CTX_PAD], wk_sb[:, k, P * m:P * (m + 1)], ctx_sb[:, k, b, :],
                                        start=(k == 0), stop=(k == KD - 1))
                    ins.then_inc(k_ready, 1)
            turn_x(1)
            project_q(1)
            pe.wait_ge(s_v_inputs, 32)
            pe.wait_ge(k_split_done, BATCH)
            for b in range(BATCH):
                for k in range(KD):
                    ins = pe.matmul(st_ps[b][:, 0:DIM], ctx_sb[:, k, b, 0:HEAD_ROWS], wv_sb[:, k, :],
                                    start=(k == 0), stop=(k == KD - 1))
                ins.then_inc(v_ready, 1)
                for j in range(4):
                    for k in range(KD):
                        ins = pe.matmul(o_ps[b][32 * j:32 * j + 32, 0:DIM], ctx_sb[:, k, b, HEAD_ROWS:CTX_PAD],
                                        wv_sb[:, k, :], start=(k == 0), stop=(k == KD - 1))
                ins.then_inc(v_ready, 1)
            for c, i in SCHEDULE:
                for chunk in q_due(c, i, 0):
                    turn_x(chunk)
                for chunk in q_due(c, i, 1):
                    project_q(chunk)
                if c + 1 < CHUNKS:
                    scores(c + 1, i)
                for chunk, unit in unit_due(c, i, 0):
                    scores_t(chunk, unit)
                for chunk, unit in unit_due(c, i, 1):
                    if unit % UNITS_PER_GROUP == 0:
                        values_rest(chunk, unit // UNITS_PER_GROUP)
                    if unit % UNITS_PER_GROUP == UNITS_PER_GROUP - 1:
                        values(chunk, unit // UNITS_PER_GROUP)
                if 0 <= c < CHUNKS and i == MAX_AT:
                    turn_max(c)
                for at, step in ((ROUTE, route), (TURN_O, turn_o), (PROJECT, project_out), (TURN_X2, turn_x2),
                                 (TURN_ON, turn_on)):
                    for t in due(c, i, at):
                        step(t)
            for step in (turn_o, turn_on, project_out, turn_x2, route):
                for t in range(TILES - TPC, TILES):
                    step(t)

            pe.wait_ge(onehot_done, 1)
            hot = onehot_b[:, :, :].rearrange("p t e -> p (t e)")
            pe.matmul(score_ps[0][:, 0:TILES * EXPERTS], upper_b[:, :], hot, start=True, stop=True).then_inc(count_ready, 1)
            pe.matmul(score_ps[1][:, 0:TILES * EXPERTS], ones_b[:, :], hot, start=True, stop=True).then_inc(count_ready, 1)
            for t in range(TILES):
                pe.wait_ge(hots_done, 2 + t + 1)
                ins = pe.matmul(st_ps[0][:, 0:3 * SLOT_TILES], lane_hot[:, t, :],
                                tile_hot[:, t, :, :].rearrange("p w j -> p (w j)"), start=(t == 0), stop=(t == TILES - 1))
            ins.then_inc(info_ready, 1)

            experts = [None] * SLOT_TILES

            def load_expert(j):
                experts[j] = pe.value_load(tile_expert[0:1, j:j + 1], min_val=0, max_val=EXPERTS - 1)

            def turn_in(j):
                pe.wait_ge(gathered[j % GATHERS], 16 * (j // GATHERS + 1))
                if j >= 2:
                    pe.wait_ge(xin_copied, j - 1)
                for k in range(KD):
                    ins = pe.transpose(xin_ps[j % 2][:, P * k:P * (k + 1)], slot_in[:, j % GATHERS, P * k:P * (k + 1)], ident)
                ins.then_inc(xin_ready, 1)

            def up(n, j):
                slot_used(biased, pe, n, j)
                pe.wait_ge(w1_moved, n + 1)
                for m in range(HIDDEN_BLOCKS):
                    for k in range(KD):
                        ins = pe.matmul(h_ps[j % RING][:, P * m:P * (m + 1)], w1_now[:, j % RING, k, P * m:P * (m + 1)],
                                        slot_xt[:, j, k, :], start=(k == 0), stop=(k == KD - 1))
                ins.then_inc(h_ready, 1)

            def down(n, j, buffer):
                slot_used(y_added, pe, n, j)
                pe.wait_ge(u_ready, n + 1)
                for k in range(KH):
                    at = KD * 2 * HQ + k * DIM
                    ins = pe.matmul(y_ps[j % RING][:, 0:DIM], act_ut[:, j % RING, k, :],
                                    w_sb[:, bass.ds(buffer + experts[j], 1), at:at + DIM].rearrange("p o n -> p (o n)"),
                                    start=(k == 0), stop=(k == KH - 1))
                ins.then_inc(y_ready, 1)

            pe.wait_ge(routed, 2)
            load_expert(0)
            turn_in(0)
            turn_in(1)
            for j in range(SLOT_TILES):
                pe.wait_ge(xin_copied, j + 1)
                up(j, j)
                if j + 1 < SLOT_TILES:
                    load_expert(j + 1)
                if j + 2 < SLOT_TILES:
                    turn_in(j + 2)
                if j >= 2:
                    down(j - 2, j - 2, 0)
            with pe.Fori(1, QUARTERS, 1) as q:
                buffer = pe.snap((q % 2) * EXPERTS)
                other = pe.snap(((q + 1) % 2) * EXPERTS)
                for j in range(SLOT_TILES):
                    n = SLOT_TILES * q + j
                    up(n, j)
                    down(n - 2, (j - 2) % SLOT_TILES, buffer if j >= 2 else other)
            n = SLOT_TILES * QUARTERS
            for back in (2, 1):
                down(n - back, SLOT_TILES - back, ((QUARTERS - 1) % 2) * EXPERTS)

        @block.scalar
        def _(act):
            def copy_xt(c):
                for k in range(KD):
                    act.wait_ge(xt_ready, KD * c + k + 1)
                    if c >= 1 and k == 0:
                        act.wait_ge(q_ready, KD * c)
                    act.activation(xn_t[:, k, :], work_ps[k][:, :], ACT.Copy).then_inc(xt_copied, 1)

            def q_highs(c):
                if c == 0:
                    act.wait_ge(s_q_weights, 32)
                for m in range(KD):
                    act.wait_ge(q_ready, KD * c + m + 1)
                    if c >= 1 and m == 0:
                        act.wait_ge(q_stored, 16 * c)
                    act.activation(q_split[:, m, 0, :], work_ps[m][:, :], ACT.Identity,
                                   bias=bq_sb[:, m:m + 1]).then_inc(q_high, 1)

            def copy_max(c):
                act.wait_ge(mt_ready, c + 1)
                if c >= 2:
                    act.wait_ge(max_loaded, 16 * (c - 1))
                act.activation(max_t[0:3 * HEADS, c % 2, :], work_ps[1][0:3 * HEADS, 0:CHUNK // 2].bitcast(BF16),
                               ACT.Copy).then_inc(mt_copied, 1)

            def load_max(c):
                act.wait_ge(mt_copied, c + 1)
                act.dma_start(q_stack[STACK:STACK_T, stack_slot(c), :, :],
                              max_t[0:3 * HEADS, c % 2, :]).then_inc(max_loaded, 16)

            def exps(c, u):
                n = UNITS * c + u
                act.wait_ge(st_ready, n + 1)
                if n >= PROBS:
                    act.wait_ge(pv_done, n - PROBS + 1)
                act.activation(probs[:, n % PROBS, :], st_ps[n % 2][:, :], ACT.Exp, scale=SCALE).then_inc(probs_ready, 1)

            def copy_o(c, g):
                group = GROUPS * c + g
                act.wait_ge(pv_done, UNITS_PER_GROUP * (group + 1))
                if c >= 2:
                    act.wait_ge(o_turned, TPC * (c - 1))
                act.activation(attn_t[:, c % 2, g, :], o_ps[group % 2][:, :], ACT.Copy).then_inc(o_copied, 1)

            def copy_on(t):
                act.wait_ge(on_turned, t + 1)
                if t >= TPC:
                    act.wait_ge(proj_ready, t - TPC + 1)
                act.activation(attn_nt[:, t % TPC, :, :].rearrange("p k n -> p (k n)"), out_ps(t)[1][:, 0:DIM],
                               ACT.Copy).then_inc(on_copied, 1)

            def copy_x2(t):
                act.wait_ge(x2t_ready, t + 1)
                if t >= TPC:
                    act.wait_ge(logits_ready, t - TPC + 1)
                act.activation(x2n_t[:, t % TPC, :, :].rearrange("p k n -> p (k n)"), out_ps(t)[1][:, 0:DIM],
                               ACT.Copy).then_inc(x2t_copied, 1)

            copy_xt(0)
            q_highs(0)
            copy_xt(1)
            q_highs(1)
            for b in range(BATCH):
                for ps, dst in ((st_ps, v_tmp[:, b, 0, :]), (o_ps, v_tmp[:, b, 1, :])):
                    act.wait_ge(v_ready, 2 * b + (1 if ps is st_ps else 2))
                    act.activation(dst, ps[b][:, 0:DIM], ACT.Copy).then_inc(v_copied, 1)
            for c, i in SCHEDULE:
                for t in due(c, i, COPY_ON):
                    copy_on(t)
                for t in due(c, i, COPY_X2):
                    copy_x2(t)
                if 0 <= c < CHUNKS and i == MAX_AT + 1:
                    copy_max(c)
                    load_max(c)
                for chunk in q_due(c, i, 0):
                    copy_xt(chunk)
                for chunk in q_due(c, i, 1):
                    q_highs(chunk)
                for chunk, unit in unit_due(c, i, 0):
                    exps(chunk, unit)
                for chunk, unit in unit_due(c, i, 1):
                    if unit % UNITS_PER_GROUP == UNITS_PER_GROUP - 1:
                        copy_o(chunk, unit // UNITS_PER_GROUP)
            for copy in (copy_on, copy_x2):
                for t in range(TILES - TPC, TILES):
                    copy(t)

            def copy_in(j):
                act.wait_ge(xin_ready, j + 1)
                act.activation(slot_xt[:, j, :, :].rearrange("p k n -> p (k n)"), xin_ps[j % 2][:, 0:DIM],
                               ACT.Copy).then_inc(xin_copied, 1)

            def move_w1(n, j, buffer):
                slot_used(h_ready, act, n, j)
                act.activation(w1_now[:, j % RING, :, :].rearrange("p k n -> p (k n)"),
                               w_sb[:, bass.ds(buffer + experts[j], 1), 0:KD * 2 * HQ].rearrange("p o n -> p (o n)"),
                               ACT.Copy).then_inc(w1_moved, 1)

            def gates(n, j):
                slot_used(u_ready, act, n, j)
                act.wait_ge(biased, n + 1)
                act.activation(gate[:, j % RING, :, :], hidden[:, j % RING, KH:2 * KH, :], ACT.Sigmoid).then_inc(gate_ready, 1)

            def load_expert(j):
                experts[j] = act.value_load(tile_expert[0:1, j:j + 1], min_val=0, max_val=EXPERTS - 1)

            experts = [None] * SLOT_TILES
            act.wait_ge(routed, 2)
            load_expert(0)
            act.wait_ge(quarter_ready, 1)
            move_w1(0, 0, 0)
            copy_in(0)
            copy_in(1)
            for j in range(SLOT_TILES):
                if j + 1 < SLOT_TILES:
                    load_expert(j + 1)
                    move_w1(j + 1, j + 1, 0)
                else:
                    act.wait_ge(quarter_ready, 2)
                    move_w1(j + 1, 0, EXPERTS)
                if j + 2 < SLOT_TILES:
                    copy_in(j + 2)
                gates(j, j)
            with act.Fori(1, QUARTERS, 1) as q:
                buffer = act.snap((q % 2) * EXPERTS)
                other = act.snap(((q + 1) % 2) * EXPERTS)
                for j in range(SLOT_TILES):
                    n = SLOT_TILES * q + j
                    if j + 1 < SLOT_TILES:
                        move_w1(n + 1, j + 1, buffer)
                    else:
                        act.wait_ge(quarter_ready, q + 2)
                        move_w1(n + 1, 0, other)
                    gates(n, j)

        @block.vector
        def _(dve):
            count = [0]

            def step(ins):
                ins.then_inc(dve_step, 1)
                count[0] += 1

            def settle():
                dve.wait_ge(dve_step, count[0])

            def split3(full, rest, high, mid, low, signal):
                settle()
                step(dve.tensor_copy(high, full))
                settle()
                step(dve.tensor_tensor(rest, full, high, ALU.subtract))
                settle()
                step(dve.tensor_copy(mid, rest))
                settle()
                dve.tensor_tensor(low, rest, mid, ALU.subtract).then_inc(signal, 1)

            def stats1_of(c):
                dve.wait_ge(s_x[c], 16)
                for t in range(TPC * c, TPC * (c + 1)):
                    step(dve.bn_stats(stats1[:, t, :], x_sb[:, t, :]))
                settle()
                for t in range(TPC * c, TPC * (c + 1)):
                    ins = dve.bn_aggr(mv1[:, t, :], stats1[:, t, :])
                ins.then_inc(ln1_stats, 1)

            def norm1(c):
                dve.wait_ge(rstd1_done, c + 1)
                if c >= 2:
                    dve.wait_ge(xt_ready, KD * (c - 1))
                for t in range(TPC):
                    n = TPC * c + t
                    ins = dve.tensor_scalar(xn[:, c % 2, t, :], x_sb[:, n, :], mv1[:, n, 0:1], rstd1[:, n:n + 1],
                                            ALU.subtract, ALU.mult)
                ins.then_inc(ln1_done, 1)

            def rest_of_q(c):
                for m in range(KD):
                    dve.wait_ge(q_high, KD * c + m + 1)
                    dve.scalar_tensor_tensor(q_rest[:, m, :], work_ps[m][:, :], bq_sb[:, m:m + 1], q_split[:, m, 0, :],
                                             ALU.add, ALU.subtract).then_inc(q_rest_done, 1)
                dve.wait_ge(q_rest_done, KD * (c + 1))
                step(dve.tensor_copy(q_split[:, :, 1, :], q_rest[:, :, :]))
                settle()
                dve.tensor_tensor(q_split[:, :, 2, :], q_rest[:, :, :], q_split[:, :, 1, :],
                                  ALU.subtract).then_inc(q_low, 1)

            def split_k(b, ps):
                for m in range(KD):
                    dve.wait_ge(k_ready, KD * b + m + 1)
                    step(dve.tensor_scalar(k_full[:, b, m, :], ps[m][:, 0:CTX_PAD], bk_sb[:, m:m + 1], tau_sb[:, b:b + 1],
                                           ALU.add, ALU.mult))
                split3(k_full[:, b, :, :], k_rest[:, b, :, :], k_split[:, b, :, 0, :], k_split[:, b, :, 1, :],
                       k_split[:, b, :, 2, :], k_split_done)

            dve.memset(warm[:, :], 0.0).then_inc(warm_ready, 1)
            stats1_of(0)
            norm1(0)
            dve.wait_ge(s_delta, 16)
            split3(delta_sb[:, :], delta_rest[:, :], delta_split[:, 0, :], delta_split[:, 1, :], delta_split[:, 2, :],
                   d_split_done)
            stats1_of(1)
            norm1(1)
            rest_of_q(0)
            dve.wait_ge(s_k_inputs, 64)
            split_k(0, score_ps)
            split_k(1, o_ps)
            rest_of_q(1)
            stats1_of(2)
            norm1(2)
            dve.wait_ge(s_consts, 16)
            dve.tensor_copy(ident_b, ident).then_inc(ident_ready, 1)
            step(dve.tensor_copy(upper_b[:, :], const_of("upper")))
            step(dve.memset(ones_b[:, :], 1.0))
            step(dve.tensor_copy(lanes_b[:, :], const_of("slot_in_tile")))

            def maxes(c, i):
                n = STEPS * c + i
                t, first = i // SCORE_BANKS, HEADS_PER_BANK * (i % SCORE_BANKS)
                k = min(HEADS_PER_BANK, HEADS - first)
                dve.wait_ge(score_ready, n + 1)
                dve.tensor_reduce(row_max[:, c % 2, t, first:first + k],
                                  score_bank(c, i)[:, 0:k * CTX].rearrange("p (h s) -> p h s", s=CTX), AX_X,
                                  ALU.max).then_inc(max_done, 1)

            def split_max(c):
                dve.wait_ge(max_done, STEPS * (c + 1))
                if c >= 1:
                    dve.wait_ge(mt_ready, c)
                split3(row_max[:, c % 2, :, :], max_rest[:, :, :], max_split[:, :, 0, :], max_split[:, :, 1, :],
                       max_split[:, :, 2, :], max_parts)

            def normalise(t):
                dve.wait_ge(o_turned, t + 1)
                o = out_ps(t)[0][:, :].rearrange("p (h n) -> p h n", n=32)
                step(dve.reciprocal(inverse[:, t % TPC, :], o[:, :, HDIM]))
                settle()
                if t >= TPC:
                    dve.wait_ge(on_turned, t - TPC + 1)
                dve.tensor_tensor(attn[:, t % TPC, :].rearrange("p (h d) -> p h d", d=HDIM), o[:, :, 0:HDIM],
                                  inverse[:, t % TPC, :].rearrange("p (h o) -> p h o", o=1).to_broadcast([P, HEADS, HDIM]),
                                  ALU.mult).then_inc(on_ready, 1)

            def residual(t):
                dve.wait_ge(proj_ready, t + 1)
                if t == 0:
                    dve.wait_ge(zeros_stored, 16)
                dve.wait_ge(x_biased, t // TPC + 1)
                if t >= TPC:
                    dve.wait_ge(rows_stored[t % TPC], 16 * (t // TPC))
                    dve.wait_ge(x2t_ready, t - TPC + 1)
                dve.tensor_tensor(row_buf[:, t % TPC, DIM:2 * DIM], out_ps(t)[0][:, 0:DIM], x_sb[:, t, :],
                                  ALU.add).then_inc(x2_done, 1)

            def stats2_of(t):
                dve.wait_ge(x2_done, t + 1)
                step(dve.bn_stats(stats2[:, t, :], row_buf[:, t % TPC, DIM:2 * DIM]))
                settle()
                dve.bn_aggr(mv2[:, t, :], stats2[:, t, :]).then_inc(ln2_stats, 1)

            def norm2(t):
                dve.wait_ge(rstd2_done, t + 1)
                dve.tensor_scalar(row_buf[:, t % TPC, 0:DIM], row_buf[:, t % TPC, DIM:2 * DIM], mv2[:, t, 0:1],
                                  rstd2[:, t:t + 1], ALU.subtract, ALU.mult).then_inc(ln2_done, 1)

            def logits_of(t):
                dve.wait_ge(logits_ready, t + 1)
                if t == 0:
                    dve.wait_ge(s_out_weights, 64)
                dve.tensor_tensor(logits[:, t, :], out_ps(t)[0][:, 0:EXPERTS], rb_sb[:, :], ALU.add).then_inc(logits_done, 1)

            for c, i in SCHEDULE:
                for chunk in q_due(c, i, 2):
                    rest_of_q(chunk)
                for at, do in ((LOGITS, logits_of), (NORMALISE, normalise), (RESIDUAL, residual), (NORM2, norm2)):
                    for t in due(c, i, at):
                        do(t)
                if c + 1 < CHUNKS:
                    maxes(c + 1, i)
                    if i == STEPS - 1:
                        split_max(c + 1)
                for t in due(c, i, RESIDUAL):
                    stats2_of(t)
                if i == 8 and c == 0:
                    stats1_of(3)
                if i == 10 and c == 0:
                    norm1(3)
            for do in (normalise, residual, stats2_of, norm2, logits_of):
                for t in range(TILES - TPC, TILES):
                    do(t)

            def wide_e(ap):
                return ap.rearrange("p (t o) -> p t o", o=1).to_broadcast([P, TILES, EXPERTS])

            def row_e(ap):
                return ap.rearrange("p (o e) -> p o e", o=1).to_broadcast([P, TILES, EXPERTS])

            dve.wait_ge(logits_done, TILES)
            step(dve.tensor_reduce(best[:, :], logits[:, :, :], AX_X, ALU.max))
            settle()
            step(dve.tensor_tensor(key[:, :, :], logits[:, :, :], wide_e(best[:, :]), ALU.is_equal))
            settle()
            step(dve.tensor_tensor(key[:, :, :], key[:, :, :], row_e(const_of("first_expert")), ALU.mult))
            settle()
            step(dve.tensor_reduce(best[:, :], key[:, :, :], AX_X, ALU.max))
            settle()
            step(dve.tensor_tensor(onehot[:, :, :], row_e(const_of("first_expert")), wide_e(best[:, :]), ALU.is_equal))
            settle()
            dve.tensor_copy(onehot_b[:, :, :], onehot[:, :, :]).then_inc(onehot_done, 1)
            dve.wait_ge(count_ready, 2)
            step(dve.tensor_copy(counts[:, :, :], score_ps[1][:, 0:TILES * EXPERTS].rearrange("p (t e) -> p e t", e=EXPERTS)))
            settle()
            flat = lambda ap: ap.rearrange("p a b -> p (a b)")
            step(dve.tensor_tensor_scan(flat(upto[:, :, :]), const_of("carry"), flat(counts[:, :, :]), 0.0, ALU.mult, ALU.add))
            settle()
            step(dve.tensor_tensor(over[:, :, :], upto[:, :, TILES - 1:TILES].to_broadcast([P, EXPERTS, TILES]),
                                   const_of("tile_starts").rearrange("p (o t) -> p o t", o=1).to_broadcast([P, EXPERTS, TILES]),
                                   ALU.is_gt))
            settle()
            step(dve.tensor_reduce(n_tiles[:, :], over[:, :, :], AX_X, ALU.add))
            step(dve.tensor_tensor(upto[:, :, :], upto[:, :, :], counts[:, :, :], ALU.subtract))
            settle()
            step(dve.tensor_tensor_scan(last_tile[:, :], const_of("one8"), n_tiles[:, :], 0.0, ALU.mult, ALU.add))
            settle()
            step(dve.tensor_tensor(start_slot[:, :], last_tile[:, :], n_tiles[:, :], ALU.subtract))
            settle()
            step(dve.tensor_scalar(start_slot[:, :], start_slot[:, :], float(P), None, ALU.mult))
            step(dve.tensor_tensor(place[:, :, :], score_ps[0][:, 0:TILES * EXPERTS].rearrange("p (t e) -> p t e", e=EXPERTS),
                                   upto[:, :, :].rearrange("p e t -> p t e"), ALU.add))
            settle()
            step(dve.tensor_tensor(place[:, :, :], place[:, :, :], row_e(start_slot[:, :]), ALU.add))
            settle()
            step(dve.tensor_tensor(place[:, :, :], place[:, :, :], onehot[:, :, :], ALU.mult))
            settle()
            step(dve.tensor_reduce(slot[:, :], place[:, :, :], AX_X, ALU.add))
            settle()

            def wide_j(ap):
                return ap.rearrange("p (t o) -> p t o", o=1).to_broadcast([P, TILES, SLOT_TILES])

            def row_j(ap):
                return ap.rearrange("p (o j) -> p o j", o=1).to_broadcast([P, TILES, SLOT_TILES])

            step(dve.tensor_scalar(slot_lane[:, :], slot[:, :], 1.0 / P, None, ALU.mult))
            step(dve.tensor_scalar(row_f[:, 0, :], const_of("slot_tile"), 1.0, None, ALU.add))
            settle()
            step(dve.tensor_tensor(passed[:, :, :], wide_j(slot_lane[:, :]), row_j(row_f[:, 0, :]), ALU.is_ge))
            settle()
            step(dve.tensor_reduce(slot_tile_of[:, :], passed[:, :, :], AX_X, ALU.add))
            settle()
            step(dve.scalar_tensor_tensor(slot_lane[:, :], slot_tile_of[:, :], -float(P), slot[:, :], ALU.mult, ALU.add))
            step(dve.tensor_tensor(tile_hot[:, :, 2, :], wide_j(slot_tile_of[:, :]), row_j(const_of("slot_tile")), ALU.is_equal))
            settle()
            dve.tensor_tensor(tile_hot[:, :, 0, :], tile_hot[:, :, 2, :], wide_j(const_of("tile_of_token")),
                              ALU.mult).then_inc(hots_done, 1)
            dve.tensor_scalar(tile_hot[:, :, 1, :], tile_hot[:, :, 2, :], const_of("row"), None, ALU.mult).then_inc(hots_done, 1)
            for t in range(TILES):
                dve.tensor_scalar(lane_hot[:, t, :], lanes_b[:, :], slot_lane[:, t:t + 1], None,
                                  ALU.is_equal).then_inc(hots_done, 1)
            step(dve.tensor_tensor(ended[:, :, :],
                                   const_of("slot_tile").rearrange("p (j o) -> p j o", o=1).to_broadcast([P, SLOT_TILES, EXPERTS]),
                                   last_tile[:, :].rearrange("p (o e) -> p o e", o=1).to_broadcast([P, SLOT_TILES, EXPERTS]),
                                   ALU.is_ge))
            settle()
            step(dve.tensor_reduce(expert_f[:, :], ended[:, :, :], AX_X, ALU.add))
            settle()
            dve.tensor_scalar(tile_expert[:, :], expert_f[0:1, :], float(EXPERTS - 1), None, ALU.min).then_inc(routed, 1)
            dve.wait_ge(info_ready, 1)
            step(dve.tensor_copy(flat(slot_info[:, :, :]), st_ps[0][:, 0:3 * SLOT_TILES]))
            settle()
            step(dve.scalar_tensor_tensor(row_f[:, 0, :], slot_info[:, 0, :], float(P), slot_info[:, 1, :], ALU.mult, ALU.add))
            step(dve.tensor_scalar(unused[:, :], slot_info[:, 2, :], -1.0, 1.0, ALU.mult, ALU.add))
            settle()

            def both(ap):
                return ap.rearrange("p (o j) -> p o j", o=1).to_broadcast([P, 2, SLOT_TILES])

            step(dve.tensor_tensor(spare[:, :, :], both(unused[:, :]),
                                   const_of("spare_row").rearrange("p (w j) -> p w j", w=2), ALU.mult))
            settle()
            dve.tensor_tensor(slot_row[:, :, :], spare[:, :, :], both(row_f[:, 0, :]), ALU.add).then_inc(routed, 1)

            experts = [None] * SLOT_TILES

            def bias(n, j, first):
                slot_used(u_ready, dve, n, j)
                dve.wait_ge(h_ready, n + 1)
                b1_now = b1_sb[:, bass.ds(first + experts[j], 1), :].rearrange("p o (m n) -> p (o m) n", n=1)
                dve.tensor_tensor(hidden[:, j % RING, :, :], h_ps[j % RING][:, :].rearrange("p (m n) -> p m n", n=P),
                                  b1_now.to_broadcast([P, HIDDEN_BLOCKS, P]), ALU.add).then_inc(biased, 1)

            def gated(n, j):
                slot_used(y_ready, dve, n, j)
                dve.wait_ge(gate_ready, n + 1)
                dve.tensor_tensor(act_ut[:, j % RING, :, :], hidden[:, j % RING, 0:KH, :], gate[:, j % RING, :, :],
                                  ALU.mult).then_inc(u_ready, 1)

            def add_y(n, j):
                dve.wait_ge(y_ready, n + 1)
                if isinstance(n, int) and n < SLOT_TILES:
                    dve.wait_ge(y_started, j + 1)
                dve.tensor_tensor(y_acc[:, j, :], y_ps[j % RING][:, 0:DIM], y_acc[:, j, :], ALU.add).then_inc(y_added, 1)

            dve.wait_ge(s_biases, 32)
            dve.wait_ge(routed, 2)
            experts[0] = dve.value_load(tile_expert[0:1, 0:1], min_val=0, max_val=EXPERTS - 1)
            for j in range(SLOT_TILES):
                bias(j, j, 0)
                if j + 1 < SLOT_TILES:
                    experts[j + 1] = dve.value_load(tile_expert[0:1, j + 1:j + 2], min_val=0, max_val=EXPERTS - 1)
                gated(j, j)
                if j >= 2:
                    add_y(j - 2, j - 2)
            dve.wait_ge(y_started, SLOT_TILES)
            with dve.Fori(1, QUARTERS, 1) as q:
                first = dve.snap(q * EXPERTS)
                for j in range(SLOT_TILES):
                    n = SLOT_TILES * q + j
                    bias(n, j, first)
                    gated(n, j)
                    if j >= 2:
                        add_y(n - 2, j - 2)
                    else:
                        add_y(n - 2, SLOT_TILES + j - 2)
            n = SLOT_TILES * QUARTERS
            for back in (2, 1):
                add_y(n - back, SLOT_TILES - back)


def kernel(**inputs):
    import concourse.bacc as _bacc
    from concourse.bass_utils import run_bass_kernel_spmd as _run

    a = {name: np.ascontiguousarray(value) for name, value in inputs.items()}
    ctx_t = np.zeros((BATCH, DIM, CTX_PAD), np.float32)
    ctx_t[:, :, :CTX] = a["ctx_1024"].transpose(0, 2, 1)
    w1 = a["L0_ffn_w1"].reshape(EXPERTS, KD, P, 2, QUARTERS, HQ).transpose(4, 2, 0, 1, 3, 5)
    w2 = a["L0_ffn_w2"].reshape(EXPERTS, QUARTERS, KH, P, DIM).transpose(1, 3, 0, 2, 4)
    arrays = {
        "x": a["x"].reshape(TOKENS, DIM),
        "ctx_t": ctx_t.reshape(BATCH, KD, P, CTX_PAD).transpose(2, 1, 0, 3).reshape(P, KD * BATCH, CTX_PAD),
        "tau": a["condB_tau"],
        "delta": a["fside_BxS2_0"],
        "wq": a["L0_xcond_Wq"].T, "bq": a["L0_xcond_bq"].reshape(KD, P).T,
        "wk": a["L0_xcond_Wk"].T, "bk": a["L0_xcond_bk"].reshape(KD, P).T,
        "wv": a["L0_xcond_Wv"].T, "bv": a["L0_xcond_bv"],
        "wo": a["L0_xcond_Wo"].T, "bo": a["L0_xcond_bo"],
        "rw": a["L0_ffn_router_w"], "rb": a["L0_ffn_router_b"],
        "weights": np.concatenate([w1.reshape(QUARTERS, P, EXPERTS, -1), w2.reshape(QUARTERS, P, EXPERTS, -1)], axis=3),
        "b1": a["L0_ffn_b1"].reshape(EXPERTS, 2, QUARTERS, KH, P).transpose(4, 2, 0, 1, 3).reshape(P, -1),
        "b2": a["L0_ffn_b2"].reshape(-1),
        "const": CONSTANTS,
        "ones": np.ones((STACK - SPLIT, HEADS * CHUNK), mybir.dt.np(BF16)),
        "minus_ones": np.tile(np.where(np.arange(CTX_PAD) < CTX, -1.0, 0.0).astype(mybir.dt.np(BF16)),
                              (STACK_T - STACK, BATCH * HEADS)),
    }
    nc = _bacc.Bacc("TRN2", target_bir_lowering=False, num_devices=1)
    feeds, args = {}, []
    for name, value in arrays.items():
        value = np.ascontiguousarray(value)
        feeds[f"in_{name}_dram"] = value
        args.append(nc.dram_tensor(f"in_{name}_dram", value.shape, mybir.dt.from_np(value.dtype), kind="ExternalInput").ap())
    args.append(nc.dram_tensor("out_dram", (TOKENS + P * SLOT_TILES, DIM), F32, kind="ExternalOutput").ap())
    args.append(nc.dram_tensor("q_parts", (CHUNKS, DIM, 3, CHUNK), BF16).ap())
    args.append(nc.dram_tensor("k_parts", (BATCH, DIM, 3, CTX_PAD), BF16).ap())
    args.append(nc.dram_tensor("d_parts", (BATCH, 3, CTX), BF16).ap())
    args.append(nc.dram_tensor("rows", (TOKENS + P, 2 * DIM), F32).ap())
    build(nc, *args)
    r = _run(nc, [feeds], core_ids=[0])
    return r.results[0]["out_dram"][:TOKENS].reshape(BATCH, SEQ, DIM)
```
